# Optimizing a Trainium2 kernel written in Bass

```python
import numpy as np
import jax
import jax.numpy as jnp

def _softmax(x, axis=-1):
    return jax.nn.softmax(x, axis=axis)

def _gelu(x):
    return jax.nn.gelu(x, approximate=True)

def _silu(x):
    return jax.nn.silu(x)

def _sigmoid(x):
    return jax.nn.sigmoid(x)

def _layernorm(x, axis=-1, eps=1e-05):
    m = jnp.mean(x, axis=axis, keepdims=True)
    v = jnp.var(x, axis=axis, keepdims=True)
    return (x - m) / jnp.sqrt(v + eps)

def _scatter_add(tgt, idx, src, axis=0):
    return tgt.at[idx].add(src)

def _segment_sum(src, seg, n):
    return jax.ops.segment_sum(src, seg, n)
kernel_name = 'mk_pixart_resid_d4_seqx_r4_f01797'

def setup_inputs(seed: int=0):
    np.random.seed(seed)
    _w = jnp.asarray

    def _rec_inputs():
        import jax
        import jax.numpy as jnp
        _rk = jax.random.key(seed)
        x = -0.0002928 + 1 * jax.random.normal(jax.random.fold_in(_rk, 1), (4, 512, 256), jnp.float32)
        _lenS = 512 - jax.random.randint(jax.random.fold_in(_rk, 7), (4,), 0, max(1, 512 // 4) + 1, jnp.int32)
        _lenS2 = 512 - jax.random.randint(jax.random.fold_in(_rk, 8), (4,), 0, max(1, 512 // 4) + 1, jnp.int32)
        _ctx_1024P = jax.random.normal(jax.random.fold_in(_rk, 11), (4, 16, 256), jnp.float32)
        _ctx_1024c = jax.random.dirichlet(jax.random.fold_in(_rk, 511), 0.3 * jnp.ones((16,), jnp.float32), (4, 512))
        _ctx_1024t = jnp.einsum('bsk,bkd->bsd', _ctx_1024c, _ctx_1024P)
        _ctx_1024t = _ctx_1024t * jax.lax.rsqrt(jnp.mean(jnp.square(_ctx_1024t)) + 1e-12) * 0.953939
        ctx_1024 = -1.39393e-06 + 0.999914 * (_ctx_1024t + 0.3 * jax.random.normal(jax.random.fold_in(_rk, 611), (4, 512, 256), jnp.float32))
        condB_tau = jax.random.uniform(jax.random.fold_in(_rk, 12), (4,), jnp.float32, 0.0, 1.23395)
        fside_BxS2_0 = -0.00205293 + 0.99739 * jax.random.normal(jax.random.fold_in(_rk, 13), (4, 512), jnp.float32)
        condB_pt = jax.random.uniform(jax.random.fold_in(_rk, 15), (4,), jnp.float32, 0.0, 226.919)
        return (x, ctx_1024, condB_tau, fside_BxS2_0, condB_pt, _lenS2)
    x, ctx_1024, condB_tau, fside_BxS2_0, condB_pt, _lenS2 = _rec_inputs()

    def _L0_xcond_setup():
        import jax, jax.numpy as jnp
        import numpy as np
        B, S, D, H = (2, 512, 256, 16)
        DK = D // H

        def _split_heads(x):
            b, s, _ = x.shape
            return x.reshape(b, s, H, DK).transpose(0, 2, 1, 3)
        key = jax.random.key(seed)
        ks = jax.random.split(key, 14)
        inp = {'query': jax.random.normal(ks[0], (B, S, D), jnp.float32), 'key': jax.random.normal(ks[1], (B, S, D), jnp.float32), 'value': jax.random.normal(ks[2], (B, S, D), jnp.float32), 'tau': jax.random.uniform(ks[3], (B, 1), jnp.float32, 0.5, 1.5), 'delta': jax.random.normal(ks[4], (B, S), jnp.float32)}
        sc = 1.0 / np.sqrt(D)
        for i, name in enumerate(['q', 'k', 'v', 'o']):
            inp[f'W{name}'] = jax.random.normal(ks[5 + 2 * i], (D, D), jnp.float32) * sc
            inp[f'b{name}'] = jax.random.normal(ks[6 + 2 * i], (D,), jnp.float32) * 0.01
        return inp
    _L0_xcond_all = _L0_xcond_setup()
    _L0_xcond_in = {k: v for k, v in _L0_xcond_all.items() if k in ('Wq', 'bq', 'Wk', 'bk', 'Wv', 'bv', 'Wo', 'bo')}
    del _L0_xcond_all

    def _L0_ffn_setup():
        import jax, jax.numpy as jnp
        import numpy as np
        S, B, D, H, DH = (1024, 8, 256, 16, 64)

        def _forward(x, Wg, Wq, bq, Wkv, bkv, Wo, bo, ln_g, ln_b):
            s_len, bsz, d_model = x.shape
            n_head, _, d_head = Wq.shape
            cap = s_len // n_head
            scale = 1.0 / d_head ** 0.5
            h = jnp.transpose(x, (1, 0, 2))
            t = h
            probs = jax.nn.softmax(h @ Wg, axis=-1)
            scores = jnp.transpose(probs, (0, 2, 1))
            _, idx = jax.lax.top_k(scores, cap)
            idx = jnp.sort(idx, axis=-1)
            hg = jnp.take_along_axis(h[:, None, :, :], idx[..., None], axis=2)
            hg = jnp.transpose(hg, (1, 0, 2, 3))
            q = jnp.einsum('hbcd,hde->hbce', hg, Wq) + bq[:, None, None, :]
            kv = jnp.einsum('hbcd,hde->hbce', hg, Wkv) + bkv[:, None, None, :]
            k, v = jnp.split(kv, 2, axis=-1)
            att = jnp.einsum('hbid,hbjd->hbij', q, k) * scale
            p = jax.nn.softmax(att, axis=1)
            av = jnp.einsum('hbij,hbjd->hbid', p, v)
            ao = jnp.einsum('hbid,hde->hbie', av, Wo) + bo
            tok = jnp.transpose(idx, (1, 0, 2))
            b_ids = jnp.arange(bsz)[None, :, None]
            outs = jnp.zeros_like(t).at[b_ids, tok].add(ao)
            y = t + outs
            mu = jnp.mean(y, axis=-1, keepdims=True)
            var = jnp.var(y, axis=-1, keepdims=True)
            yn = (y - mu) * jax.lax.rsqrt(var + 1e-05) * ln_g + ln_b
            return jnp.transpose(yn, (1, 0, 2))
        key = jax.random.key(seed)
        ks = jax.random.split(key, 6)
        s = 0.02
        return {'x': jax.random.normal(ks[0], (S, B, D), jnp.float32), 'attn_mask': jnp.zeros((S, S), jnp.bool_), 'Wg': jax.random.normal(ks[1], (D, H), jnp.float32) * s, 'Wq': jax.random.normal(ks[2], (H, D, DH), jnp.float32) * s, 'bq': jnp.zeros((H, DH), jnp.float32), 'Wkv': jax.random.normal(ks[3], (H, D, 2 * DH), jnp.float32) * s, 'bkv': jnp.zeros((H, 2 * DH), jnp.float32), 'Wo': jax.random.normal(ks[4], (H, DH, D), jnp.float32) * s, 'bo': jnp.zeros((D,), jnp.float32), 'ln_g': jnp.ones((D,), jnp.float32), 'ln_b': jnp.zeros((D,), jnp.float32)}
    _L0_ffn_all = _L0_ffn_setup()
    _L0_ffn_in = {k: v for k, v in _L0_ffn_all.items() if k in ('attn_mask', 'Wg', 'Wq', 'bq', 'Wkv', 'bkv', 'Wo', 'bo', 'ln_g', 'ln_b')}
    del _L0_ffn_all

    def _L1_xcond_setup():
        import jax, jax.numpy as jnp
        import numpy as np
        D_MODEL = 256
        N_HEADS = 16
        key = jax.random.key(seed)
        ks = jax.random.split(key, 16)
        B, L, S, D = (4, 512, 512, D_MODEL)
        inp = {'q': jax.random.normal(ks[0], (B, L, D), jnp.float32), 'k': jax.random.normal(ks[1], (B, S, D), jnp.float32), 'v': jax.random.normal(ks[2], (B, S, D), jnp.float32), 'tau': jax.random.uniform(ks[3], (B, 1), jnp.float32, 0.5, 1.5), 'delta': jax.random.normal(ks[4], (B, S), jnp.float32)}
        s = 1.0 / np.sqrt(D)
        inp['Wq'] = jax.random.normal(ks[5], (D, D), jnp.float32) * s
        inp['bq'] = jnp.zeros((D,), jnp.float32)
        inp['Wk'] = jax.random.normal(ks[6], (D, D), jnp.float32) * s
        inp['bk'] = jnp.zeros((D,), jnp.float32)
        inp['Wv'] = jax.random.normal(ks[7], (D, D), jnp.float32) * s
        inp['bv'] = jnp.zeros((D,), jnp.float32)
        inp['Wo'] = jax.random.normal(ks[8], (D, D), jnp.float32) * s
        inp['bo'] = jnp.zeros((D,), jnp.float32)
        return inp
    _L1_xcond_all = _L1_xcond_setup()
    _L1_xcond_in = {k: v for k, v in _L1_xcond_all.items() if k in ('Wq', 'bq', 'Wk', 'bk', 'Wv', 'bv', 'Wo', 'bo')}
    del _L1_xcond_all

    def _L1_ffn_setup():
        import jax, jax.numpy as jnp
        import numpy as np
        B, S, H, I, E, TOPK, KS = (4, 1024, 256, 128, 16, 2, 3)
        key = jax.random.key(seed)
        ks = jax.random.split(key, 9)
        sc = 0.02
        return {'hidden_states': jax.random.normal(ks[0], (B, S, H), dtype=jnp.float32), 'router_w': jax.random.normal(ks[1], (H, E), dtype=jnp.float32) * sc, 'router_bias': jnp.zeros((E,), dtype=jnp.float32), 'expert_gate_w': jax.random.normal(ks[2], (E - 1, H, I), dtype=jnp.float32) * sc, 'expert_up_w': jax.random.normal(ks[3], (E - 1, H, I), dtype=jnp.float32) * sc, 'expert_down_w': jax.random.normal(ks[4], (E - 1, I, H), dtype=jnp.float32) * sc, 'conv_w': jax.random.normal(ks[5], (I, H, KS), dtype=jnp.float32) * sc, 'shared_up_w': jax.random.normal(ks[6], (H, I), dtype=jnp.float32) * sc, 'shared_down_w': jax.random.normal(ks[7], (I, H), dtype=jnp.float32) * sc}
    _L1_ffn_all = _L1_ffn_setup()
    _L1_ffn_in = {k: v for k, v in _L1_ffn_all.items() if k in ('router_w', 'router_bias', 'expert_gate_w', 'expert_up_w', 'expert_down_w', 'conv_w', 'shared_up_w', 'shared_down_w')}
    del _L1_ffn_all

    def _L2_xcond_setup():
        import jax, jax.numpy as jnp
        import numpy as np
        N, L, H, Q = (64, 258, 256, 64)
        WINDOW = 16.0
        DEV_POW = 128.0
        key = jax.random.key(seed)
        k1, k2, k3, k4, k5, k6 = jax.random.split(key, 6)
        encoder_outputs = jax.random.normal(k1, (N, L, H), dtype=jnp.float32)
        decoder_h_t = jax.random.normal(k2, (N, Q, H), dtype=jnp.float32)
        src_len = jax.random.randint(k3, (N,), 32, L + 1).astype(jnp.int32)
        p_t = jax.random.uniform(k4, (N,), dtype=jnp.float32) * (src_len.astype(jnp.float32) - 1.0)
        W_a = jax.random.normal(k5, (H, H), dtype=jnp.float32) * (1.0 / np.sqrt(H))
        W_c = jax.random.normal(k6, (H, 2 * H), dtype=jnp.float32) * (1.0 / np.sqrt(2 * H))
        return {'encoder_outputs': encoder_outputs, 'decoder_h_t': decoder_h_t, 'src_len': src_len, 'p_t': p_t, 'W_a': W_a, 'W_c': W_c}
    _L2_xcond_all = _L2_xcond_setup()
    _L2_xcond_in = {k: v for k, v in _L2_xcond_all.items() if k in ('W_a', 'W_c')}
    del _L2_xcond_all

    def _L2_ffn_setup():
        import jax, jax.numpy as jnp
        import numpy as np
        B, T, D, H, E, K = (2, 256, 256, 16, 8, 2)
        HS = D // H
        FF = 4 * D

        def layernorm(x, g, b, eps=1e-05):
            m = jnp.mean(x, axis=-1, keepdims=True)
            v = jnp.mean((x - m) ** 2, axis=-1, keepdims=True)
            return (x - m) * jax.lax.rsqrt(v + eps) * g + b
        key = jax.random.key(seed)
        ks = jax.random.split(key, 10)
        s = 0.02
        return {'x': jax.random.normal(ks[0], (B, T, D), jnp.float32), 'Wq': jax.random.normal(ks[1], (H, D, HS), jnp.float32) * s, 'Wk': jax.random.normal(ks[2], (H, D, HS), jnp.float32) * s, 'Wv': jax.random.normal(ks[3], (H, D, HS), jnp.float32) * s, 'gate_W': jax.random.normal(ks[4], (D, E), jnp.float32) * s, 'W1': jax.random.normal(ks[5], (E, D, FF), jnp.float32) * s, 'b1': jnp.zeros((E, FF), jnp.float32), 'W2': jax.random.normal(ks[6], (E, FF, D), jnp.float32) * s, 'b2': jnp.zeros((E, D), jnp.float32), 'ln1_g': jnp.ones((D,), jnp.float32), 'ln1_b': jnp.zeros((D,), jnp.float32), 'ln2_g': jnp.ones((D,), jnp.float32), 'ln2_b': jnp.zeros((D,), jnp.float32)}
    _L2_ffn_all = _L2_ffn_setup()
    _L2_ffn_in = {k: v for k, v in _L2_ffn_all.items() if k in ('Wq', 'Wk', 'Wv', 'gate_W', 'W1', 'b1', 'W2', 'b2', 'ln1_g', 'ln1_b', 'ln2_g', 'ln2_b')}
    del _L2_ffn_all

    def _L3_xcond_setup():
        import jax, jax.numpy as jnp
        import numpy as np
        N, L, H, Q = (64, 258, 256, 64)
        WINDOW = 16.0
        DEV_POW = 128.0
        key = jax.random.key(seed)
        k1, k2, k3, k4, k5, k6 = jax.random.split(key, 6)
        encoder_outputs = jax.random.normal(k1, (N, L, H), dtype=jnp.float32)
        decoder_h_t = jax.random.normal(k2, (N, Q, H), dtype=jnp.float32)
        src_len = jax.random.randint(k3, (N,), 32, L + 1).astype(jnp.int32)
        p_t = jax.random.uniform(k4, (N,), dtype=jnp.float32) * (src_len.astype(jnp.float32) - 1.0)
        W_a = jax.random.normal(k5, (H, H), dtype=jnp.float32) * (1.0 / np.sqrt(H))
        W_c = jax.random.normal(k6, (H, 2 * H), dtype=jnp.float32) * (1.0 / np.sqrt(2 * H))
        return {'encoder_outputs': encoder_outputs, 'decoder_h_t': decoder_h_t, 'src_len': src_len, 'p_t': p_t, 'W_a': W_a, 'W_c': W_c}
    _L3_xcond_all = _L3_xcond_setup()
    _L3_xcond_in = {k: v for k, v in _L3_xcond_all.items() if k in ('W_a', 'W_c')}
    del _L3_xcond_all

    def _L3_ffn_setup():
        import jax, jax.numpy as jnp
        import numpy as np
        B, S, D = (4, 512, 256)
        E = 8
        DFF = 1024
        CAP_FACTOR = 1.25
        key = jax.random.key(seed)
        ks = jax.random.split(key, 4)
        std_gate = float(np.sqrt(0.1 / D))
        inputs = jax.random.normal(ks[0], (B, S, D), dtype=jnp.float32)
        gate_w = jax.random.normal(ks[1], (E, D), dtype=jnp.float32) * std_gate
        w1 = jax.random.normal(ks[2], (E, D, DFF), dtype=jnp.float32) * (1.0 / np.sqrt(D))
        b1 = jnp.zeros((E, DFF), dtype=jnp.float32)
        w2 = jax.random.normal(ks[3], (E, DFF, D), dtype=jnp.float32) * (1.0 / np.sqrt(DFF))
        b2 = jnp.zeros((E, D), dtype=jnp.float32)
        return {'inputs': inputs, 'gate_w': gate_w, 'w1': w1, 'b1': b1, 'w2': w2, 'b2': b2}
    _L3_ffn_all = _L3_ffn_setup()
    _L3_ffn_in = {k: v for k, v in _L3_ffn_all.items() if k in ('gate_w', 'w1', 'b1', 'w2', 'b2')}
    del _L3_ffn_all
    return {'x': x, 'ctx_1024': ctx_1024, 'condB_tau': condB_tau, 'fside_BxS2_0': fside_BxS2_0, 'condB_pt': condB_pt, '_lenS2': _lenS2, 'L0_xcond_Wq': _L0_xcond_in['Wq'], 'L0_xcond_bq': _L0_xcond_in['bq'], 'L0_xcond_Wk': _L0_xcond_in['Wk'], 'L0_xcond_bk': _L0_xcond_in['bk'], 'L0_xcond_Wv': _L0_xcond_in['Wv'], 'L0_xcond_bv': _L0_xcond_in['bv'], 'L0_xcond_Wo': _L0_xcond_in['Wo'], 'L0_xcond_bo': _L0_xcond_in['bo'], 'L0_ffn_attn_mask': _L0_ffn_in['attn_mask'], 'L0_ffn_Wg': _L0_ffn_in['Wg'], 'L0_ffn_Wq': _L0_ffn_in['Wq'], 'L0_ffn_bq': _L0_ffn_in['bq'], 'L0_ffn_Wkv': _L0_ffn_in['Wkv'], 'L0_ffn_bkv': _L0_ffn_in['bkv'], 'L0_ffn_Wo': _L0_ffn_in['Wo'], 'L0_ffn_bo': _L0_ffn_in['bo'], 'L0_ffn_ln_g': _L0_ffn_in['ln_g'], 'L0_ffn_ln_b': _L0_ffn_in['ln_b'], 'L1_xcond_Wq': _L1_xcond_in['Wq'], 'L1_xcond_bq': _L1_xcond_in['bq'], 'L1_xcond_Wk': _L1_xcond_in['Wk'], 'L1_xcond_bk': _L1_xcond_in['bk'], 'L1_xcond_Wv': _L1_xcond_in['Wv'], 'L1_xcond_bv': _L1_xcond_in['bv'], 'L1_xcond_Wo': _L1_xcond_in['Wo'], 'L1_xcond_bo': _L1_xcond_in['bo'], 'L1_ffn_router_w': _L1_ffn_in['router_w'], 'L1_ffn_router_bias': _L1_ffn_in['router_bias'], 'L1_ffn_expert_gate_w': _L1_ffn_in['expert_gate_w'], 'L1_ffn_expert_up_w': _L1_ffn_in['expert_up_w'], 'L1_ffn_expert_down_w': _L1_ffn_in['expert_down_w'], 'L1_ffn_conv_w': _L1_ffn_in['conv_w'], 'L1_ffn_shared_up_w': _L1_ffn_in['shared_up_w'], 'L1_ffn_shared_down_w': _L1_ffn_in['shared_down_w'], 'L2_xcond_W_a': _L2_xcond_in['W_a'], 'L2_xcond_W_c': _L2_xcond_in['W_c'], 'L2_ffn_Wq': _L2_ffn_in['Wq'], 'L2_ffn_Wk': _L2_ffn_in['Wk'], 'L2_ffn_Wv': _L2_ffn_in['Wv'], 'L2_ffn_gate_W': _L2_ffn_in['gate_W'], 'L2_ffn_W1': _L2_ffn_in['W1'], 'L2_ffn_b1': _L2_ffn_in['b1'], 'L2_ffn_W2': _L2_ffn_in['W2'], 'L2_ffn_b2': _L2_ffn_in['b2'], 'L2_ffn_ln1_g': _L2_ffn_in['ln1_g'], 'L2_ffn_ln1_b': _L2_ffn_in['ln1_b'], 'L2_ffn_ln2_g': _L2_ffn_in['ln2_g'], 'L2_ffn_ln2_b': _L2_ffn_in['ln2_b'], 'L3_xcond_W_a': _L3_xcond_in['W_a'], 'L3_xcond_W_c': _L3_xcond_in['W_c'], 'L3_ffn_gate_w': _L3_ffn_in['gate_w'], 'L3_ffn_w1': _L3_ffn_in['w1'], 'L3_ffn_b1': _L3_ffn_in['b1'], 'L3_ffn_w2': _L3_ffn_in['w2'], 'L3_ffn_b2': _L3_ffn_in['b2']}

def reference(x, ctx_1024, condB_tau, fside_BxS2_0, condB_pt, _lenS2, L0_xcond_Wq, L0_xcond_bq, L0_xcond_Wk, L0_xcond_bk, L0_xcond_Wv, L0_xcond_bv, L0_xcond_Wo, L0_xcond_bo, L0_ffn_attn_mask, L0_ffn_Wg, L0_ffn_Wq, L0_ffn_bq, L0_ffn_Wkv, L0_ffn_bkv, L0_ffn_Wo, L0_ffn_bo, L0_ffn_ln_g, L0_ffn_ln_b, L1_xcond_Wq, L1_xcond_bq, L1_xcond_Wk, L1_xcond_bk, L1_xcond_Wv, L1_xcond_bv, L1_xcond_Wo, L1_xcond_bo, L1_ffn_router_w, L1_ffn_router_bias, L1_ffn_expert_gate_w, L1_ffn_expert_up_w, L1_ffn_expert_down_w, L1_ffn_conv_w, L1_ffn_shared_up_w, L1_ffn_shared_down_w, L2_xcond_W_a, L2_xcond_W_c, L2_ffn_Wq, L2_ffn_Wk, L2_ffn_Wv, L2_ffn_gate_W, L2_ffn_W1, L2_ffn_b1, L2_ffn_W2, L2_ffn_b2, L2_ffn_ln1_g, L2_ffn_ln1_b, L2_ffn_ln2_g, L2_ffn_ln2_b, L3_xcond_W_a, L3_xcond_W_c, L3_ffn_gate_w, L3_ffn_w1, L3_ffn_b1, L3_ffn_w2, L3_ffn_b2):
    import jax
    import jax.numpy as jnp

    def _L0_xcond_ref(query, key, value, tau, delta, Wq, bq, Wk, bk, Wv, bv, Wo, bo):
        import jax, jax.numpy as jnp
        import numpy as np
        B, S, D, H = (2, 512, 256, 16)
        DK = D // H

        def _split_heads(x):
            b, s, _ = x.shape
            return x.reshape(b, s, H, DK).transpose(0, 2, 1, 3)
        q = _split_heads(query @ Wq.T + bq)
        k = _split_heads(key @ Wk.T + bk)
        v = _split_heads(value @ Wv.T + bv)
        scores = jnp.einsum('bhqd,bhkd->bhqk', q, k)
        scores = scores * tau[:, :, None, None] + delta[:, None, None, :]
        scores = scores / jnp.sqrt(jnp.asarray(DK, scores.dtype))
        p_attn = jax.nn.softmax(scores, axis=-1)
        x = jnp.einsum('bhqk,bhkd->bhqd', p_attn, v)
        x = x.transpose(0, 2, 1, 3).reshape(query.shape[0], -1, H * DK)
        return x @ Wo.T + bo

    def _L0_ffn_ref(x, attn_mask, Wg, Wq, bq, Wkv, bkv, Wo, bo, ln_g, ln_b):
        import jax, jax.numpy as jnp
        import numpy as np
        S, B, D, H, DH = (1024, 8, 256, 16, 64)

        def _forward(x, Wg, Wq, bq, Wkv, bkv, Wo, bo, ln_g, ln_b):
            s_len, bsz, d_model = x.shape
            n_head, _, d_head = Wq.shape
            cap = s_len // n_head
            scale = 1.0 / d_head ** 0.5
            h = jnp.transpose(x, (1, 0, 2))
            t = h
            probs = jax.nn.softmax(h @ Wg, axis=-1)
            scores = jnp.transpose(probs, (0, 2, 1))
            _, idx = jax.lax.top_k(scores, cap)
            idx = jnp.sort(idx, axis=-1)
            hg = jnp.take_along_axis(h[:, None, :, :], idx[..., None], axis=2)
            hg = jnp.transpose(hg, (1, 0, 2, 3))
            q = jnp.einsum('hbcd,hde->hbce', hg, Wq) + bq[:, None, None, :]
            kv = jnp.einsum('hbcd,hde->hbce', hg, Wkv) + bkv[:, None, None, :]
            k, v = jnp.split(kv, 2, axis=-1)
            att = jnp.einsum('hbid,hbjd->hbij', q, k) * scale
            p = jax.nn.softmax(att, axis=1)
            av = jnp.einsum('hbij,hbjd->hbid', p, v)
            ao = jnp.einsum('hbid,hde->hbie', av, Wo) + bo
            tok = jnp.transpose(idx, (1, 0, 2))
            b_ids = jnp.arange(bsz)[None, :, None]
            outs = jnp.zeros_like(t).at[b_ids, tok].add(ao)
            y = t + outs
            mu = jnp.mean(y, axis=-1, keepdims=True)
            var = jnp.var(y, axis=-1, keepdims=True)
            yn = (y - mu) * jax.lax.rsqrt(var + 1e-05) * ln_g + ln_b
            return jnp.transpose(yn, (1, 0, 2))
        return _forward(x, Wg, Wq, bq, Wkv, bkv, Wo, bo, ln_g, ln_b)

    def _L1_xcond_ref(q, k, v, tau, delta, Wq, bq, Wk, bk, Wv, bv, Wo, bo):
        import jax, jax.numpy as jnp
        import numpy as np
        D_MODEL = 256
        N_HEADS = 16
        B, L, D = q.shape
        S = k.shape[1]
        H = N_HEADS
        E = D // H
        qh = (q @ Wq.T + bq).reshape(B, L, H, E)
        kh = (k @ Wk.T + bk).reshape(B, S, H, E)
        vh = (v @ Wv.T + bv).reshape(B, S, H, E)
        scale = 1.0 / np.sqrt(E).astype(np.float32)
        scores = jnp.einsum('blhe,bshe->bhls', qh, kh)
        scores = scores * tau[:, None, None, :] + delta[:, None, None, :]
        a = jax.nn.softmax(scale * scores, axis=-1)
        out = jnp.einsum('bhls,bshd->blhd', a, vh).reshape(B, L, D)
        return out @ Wo.T + bo

    def _L1_ffn_ref(hidden_states, router_w, router_bias, expert_gate_w, expert_up_w, expert_down_w, conv_w, shared_up_w, shared_down_w):
        import jax, jax.numpy as jnp
        import numpy as np
        B, S, H, I, E, TOPK, KS = (4, 1024, 256, 128, 16, 2, 3)
        b, s, h = hidden_states.shape
        flat = hidden_states.reshape(b * s, h)
        logits = (flat @ router_w).astype(jnp.float32) + router_bias
        probs = jax.nn.softmax(logits, axis=-1)
        top_w, top_i = jax.lax.top_k(probs, TOPK)
        norm_w = top_w / (jnp.sum(top_w, axis=-1, keepdims=True) + 1e-06)
        norm_w = norm_w.astype(hidden_states.dtype)
        combine = jnp.sum(jax.nn.one_hot(top_i, E, dtype=norm_w.dtype) * norm_w[..., None], axis=1)
        routed = combine[:, E - 1:E] * flat
        for e in range(E - 1):
            y = jax.nn.silu(flat @ expert_gate_w[e]) * (flat @ expert_up_w[e]) @ expert_down_w[e]
            routed = routed + combine[:, e:e + 1] * y
        routed = routed.reshape(b, s, h)
        x_ncw = jnp.transpose(hidden_states, (0, 2, 1))
        gate = jax.lax.conv_general_dilated(x_ncw, conv_w, window_strides=(1,), padding=[(KS - 1, 0)], dimension_numbers=('NCW', 'OIW', 'NCW'))
        gate = jnp.transpose(gate, (0, 2, 1))
        shared = jax.nn.silu(gate) * (hidden_states @ shared_up_w) @ shared_down_w
        return shared + routed

    def _L2_xcond_ref(encoder_outputs, decoder_h_t, src_len, p_t, W_a, W_c):
        import jax, jax.numpy as jnp
        import numpy as np
        N, L, H, Q = (64, 258, 256, 64)
        WINDOW = 16.0
        DEV_POW = 128.0
        n, l, h = encoder_outputs.shape
        idx = jnp.arange(l, dtype=jnp.float32)
        src_end = src_len.astype(jnp.float32)
        attn_start = jnp.maximum(p_t - WINDOW, 0.0)
        attn_end = jnp.minimum(p_t + WINDOW, src_end)
        mask = (idx[None, :] < attn_start[:, None]) | (idx[None, :] > attn_end[:, None])
        score = jnp.einsum('nqh,hk,nlk->nql', decoder_h_t, W_a, encoder_outputs)
        score = jnp.where(mask[:, None, :], -1000000000.0, score)
        align = jax.nn.softmax(score, axis=2)
        gauss = jnp.exp(-(idx[None, :] - p_t[:, None]) ** 2 / DEV_POW)
        align = align * gauss[:, None, :]
        context = jnp.einsum('nql,nlh->nqh', align, encoder_outputs)
        cat = jnp.concatenate([context, decoder_h_t], axis=2)
        return jnp.tanh(cat @ W_c.T)

    def _L2_ffn_ref(x, Wq, Wk, Wv, gate_W, W1, b1, W2, b2, ln1_g, ln1_b, ln2_g, ln2_b):
        import jax, jax.numpy as jnp
        import numpy as np
        B, T, D, H, E, K = (2, 256, 256, 16, 8, 2)
        HS = D // H
        FF = 4 * D

        def layernorm(x, g, b, eps=1e-05):
            m = jnp.mean(x, axis=-1, keepdims=True)
            v = jnp.mean((x - m) ** 2, axis=-1, keepdims=True)
            return (x - m) * jax.lax.rsqrt(v + eps) * g + b
        b, t, d = x.shape
        q = jnp.einsum('btd,hdf->bhtf', x, Wq)
        k = jnp.einsum('btd,hdf->bhtf', x, Wk)
        v = jnp.einsum('btd,hdf->bhtf', x, Wv)
        wei = jnp.einsum('bhtf,bhsf->bhts', q, k) * d ** (-0.5)
        mask = jnp.tril(jnp.ones((t, t), bool))
        wei = jnp.where(mask, wei, -jnp.inf)
        wei = jax.nn.softmax(wei, axis=-1)
        attn = jnp.einsum('bhts,bhsf->bhtf', wei, v)
        attn = attn.transpose(0, 2, 1, 3).reshape(b, t, d)
        y = x + layernorm(attn, ln1_g, ln1_b)
        flat = y.reshape(-1, d)
        logits = flat @ gate_W
        topv, topi = jax.lax.top_k(logits, K)
        w = jax.nn.softmax(topv, axis=-1)
        combine = jnp.sum(jax.nn.one_hot(topi, E, dtype=flat.dtype) * w[..., None], axis=1)
        h = jax.nn.relu(jnp.einsum('nd,edf->enf', flat, W1) + b1[:, None, :])
        eo = jnp.einsum('enf,efd->end', h, W2) + b2[:, None, :]
        moe = jnp.einsum('ne,end->nd', combine, eo)
        out = y + layernorm(moe.reshape(b, t, d), ln2_g, ln2_b)
        return out

    def _L3_xcond_ref(encoder_outputs, decoder_h_t, src_len, p_t, W_a, W_c):
        import jax, jax.numpy as jnp
        import numpy as np
        N, L, H, Q = (64, 258, 256, 64)
        WINDOW = 16.0
        DEV_POW = 128.0
        n, l, h = encoder_outputs.shape
        idx = jnp.arange(l, dtype=jnp.float32)
        src_end = src_len.astype(jnp.float32)
        attn_start = jnp.maximum(p_t - WINDOW, 0.0)
        attn_end = jnp.minimum(p_t + WINDOW, src_end)
        mask = (idx[None, :] < attn_start[:, None]) | (idx[None, :] > attn_end[:, None])
        score = jnp.einsum('nqh,hk,nlk->nql', decoder_h_t, W_a, encoder_outputs)
        score = jnp.where(mask[:, None, :], -1000000000.0, score)
        align = jax.nn.softmax(score, axis=2)
        gauss = jnp.exp(-(idx[None, :] - p_t[:, None]) ** 2 / DEV_POW)
        align = align * gauss[:, None, :]
        context = jnp.einsum('nql,nlh->nqh', align, encoder_outputs)
        cat = jnp.concatenate([context, decoder_h_t], axis=2)
        return jnp.tanh(cat @ W_c.T)

    def _L3_ffn_ref(inputs, gate_w, w1, b1, w2, b2):
        import jax, jax.numpy as jnp
        import numpy as np
        B, S, D = (4, 512, 256)
        E = 8
        DFF = 1024
        CAP_FACTOR = 1.25
        d_model = inputs.shape[-1]
        tokens = inputs.reshape(-1, d_model)
        T = tokens.shape[0]
        num_experts = gate_w.shape[0]
        capacity = int(np.ceil(CAP_FACTOR * T / num_experts))
        logits = jnp.einsum('td,ed->te', tokens.astype(jnp.float32), gate_w)
        probs = jax.nn.softmax(logits, axis=-1)
        expert_idx = jnp.argmax(probs, axis=-1)
        mask = jax.nn.one_hot(expert_idx, num_experts, dtype=jnp.float32)
        ranks = jnp.cumsum(mask, axis=0) - 1.0
        keep = (ranks < capacity) * mask
        pos = ranks.astype(jnp.int32)
        sec_mask = jax.nn.one_hot(pos, capacity, dtype=jnp.float32) * keep[:, :, None]
        combine_weights = probs[:, :, None] * sec_mask
        dispatch = jnp.einsum('tec,td->ecd', sec_mask, tokens)
        h = jax.nn.relu(jnp.einsum('ecd,edh->ech', dispatch, w1) + b1[:, None, :])
        expert_out = jnp.einsum('ech,ehd->ecd', h, w2) + b2[:, None, :]
        ans = jnp.einsum('tec,ecd->td', combine_weights, expert_out)
        return ans.reshape(inputs.shape)
    x = x + _L0_xcond_ref(_layernorm(x, axis=-1), ctx_1024, ctx_1024, condB_tau[:, None], fside_BxS2_0, L0_xcond_Wq, L0_xcond_bq, L0_xcond_Wk, L0_xcond_bk, L0_xcond_Wv, L0_xcond_bv, L0_xcond_Wo, L0_xcond_bo)
    x = x + _L0_ffn_ref(_layernorm(x, axis=-1), L0_ffn_attn_mask, L0_ffn_Wg, L0_ffn_Wq, L0_ffn_bq, L0_ffn_Wkv, L0_ffn_bkv, L0_ffn_Wo, L0_ffn_bo, L0_ffn_ln_g, L0_ffn_ln_b)
    x = x + _L1_xcond_ref(_layernorm(x, axis=-1), ctx_1024, ctx_1024, condB_tau[:, None], fside_BxS2_0, L1_xcond_Wq, L1_xcond_bq, L1_xcond_Wk, L1_xcond_bk, L1_xcond_Wv, L1_xcond_bv, L1_xcond_Wo, L1_xcond_bo)
    x = x + _L1_ffn_ref(_layernorm(x, axis=-1), L1_ffn_router_w, L1_ffn_router_bias, L1_ffn_expert_gate_w, L1_ffn_expert_up_w, L1_ffn_expert_down_w, L1_ffn_conv_w, L1_ffn_shared_up_w, L1_ffn_shared_down_w)
    x = x + _L2_xcond_ref(ctx_1024, _layernorm(x, axis=-1), _lenS2, condB_pt, L2_xcond_W_a, L2_xcond_W_c)
    x = x + _L2_ffn_ref(_layernorm(x, axis=-1), L2_ffn_Wq, L2_ffn_Wk, L2_ffn_Wv, L2_ffn_gate_W, L2_ffn_W1, L2_ffn_b1, L2_ffn_W2, L2_ffn_b2, L2_ffn_ln1_g, L2_ffn_ln1_b, L2_ffn_ln2_g, L2_ffn_ln2_b)
    x = x + _L3_xcond_ref(ctx_1024, _layernorm(x, axis=-1), _lenS2, condB_pt, L3_xcond_W_a, L3_xcond_W_c)
    x = x + _L3_ffn_ref(_layernorm(x, axis=-1), L3_ffn_gate_w, L3_ffn_w1, L3_ffn_b1, L3_ffn_w2, L3_ffn_b2)
    return x

_drawn_inputs = setup_inputs


def setup_inputs(seed=0):
    import zlib

    import numpy as np

    out = dict(_drawn_inputs(seed))
    spreads = {'L0_ffn_bq': (0.0, 0.1),
     'L0_ffn_bkv': (0.0, 0.1),
     'L0_ffn_bo': (0.0, 0.1),
     'L0_ffn_ln_g': (1.0, 0.2),
     'L0_ffn_ln_b': (0.0, 0.1),
     'L1_xcond_bq': (0.0, 0.1),
     'L1_xcond_bk': (0.0, 2.0),
     'L1_xcond_bv': (0.0, 0.1),
     'L1_xcond_bo': (0.0, 0.1),
     'L1_ffn_router_bias': (0.0, 0.1),
     'L2_ffn_b1': (0.0, 0.1),
     'L2_ffn_b2': (0.0, 0.1),
     'L2_ffn_ln1_g': (1.0, 0.2),
     'L2_ffn_ln1_b': (0.0, 0.1),
     'L2_ffn_ln2_g': (1.0, 0.2),
     'L2_ffn_ln2_b': (0.0, 0.287),
     'L3_ffn_b1': (0.0, 2.0),
     'L3_ffn_b2': (0.0, 0.8)}
    factors = {'L0_xcond_bq': 4.637,
     'L0_xcond_bk': 64.0,
     'L1_ffn_expert_gate_w': 4.267,
     'L1_ffn_expert_up_w': 3.584,
     'L1_ffn_expert_down_w': 3.727,
     'L2_ffn_Wq': 3.643,
     'L2_ffn_Wk': 4.218}
    for name, (base, spread) in spreads.items():
        noise = np.random.default_rng([zlib.crc32(name.encode()), seed]).standard_normal(out[name].shape)
        drawn = base * np.exp(spread * noise) if base else spread * noise
        out[name] = jnp.asarray(drawn.astype(out[name].dtype))
    for name, factor in factors.items():
        out[name] = (out[name] * factor).astype(out[name].dtype)
    return out
```

```python
from contextlib import ExitStack, contextmanager

import concourse.bass as bass
from concourse import mybir

F32 = mybir.dt.float32
BF16 = mybir.dt.bfloat16
I32 = mybir.dt.int32
U32 = mybir.dt.uint32
ALU = mybir.AluOpType
ACT = mybir.ActivationFunctionType
AX_X = mybir.AxisListType.X

P = 128
B, S, D = 4, 512, 256
NT = S // P
DC = D // P
H, DK = 16, 16
HG = 4
NG = H // HG
HP = 32
PAIRS = ((0, 0), (0, 1), (0, 2), (1, 0), (1, 1), (2, 0))
ROW_DELTA = DK * len(PAIRS)
ROW_MAX = ROW_DELTA + 3
ROWS = ROW_MAX + 2
PAD = 2
EPS = 1e-5
LOWEST = -3.0e38
E1, I1, KS1 = 16, 128, 3
E2, FF = 8, 1024
FC = FF // P
CAPACITY = 320
WINDOW, DEV_POW, MASKED = 16.0, 128.0, -1000000000.0


@contextmanager
def Stage(nc, tag, sems, buffers=()):
    with ExitStack() as ctx:
        signals = {s: ctx.enter_context(nc.semaphore(f"{tag}_{s}")) for s in sems.split()}
        tiles = {name: ctx.enter_context(nc.sbuf_tensor(f"{tag}_{name}", shape, dt)) for name, shape, dt in buffers}
        with nc.Block() as block:
            yield block, {**signals, **tiles}
        numbers = [s.num for s in signals.values()]
        nc.all_engine_barrier(sems_to_clear=range(min(numbers), max(numbers) + 1))


def linker(engine, sem):
    count = [0]

    def link(ins):
        count[0] += 1
        ins.then_inc(sem, 1)
        engine.wait_ge(sem, count[0])
    return link


def inverse_root(nc, link, out, var, half, scratch, guess):
    v = nc.vector
    link(v.tensor_scalar(half, var, EPS, None, ALU.add))
    link(v.tensor_scalar(guess, half.bitcast(I32), 1, None, ALU.arith_shift_right))
    link(v.tensor_scalar(out.bitcast(I32), guess, -1.0, float(0x5F3759DF), ALU.mult, ALU.add))
    link(v.tensor_scalar(half, half, -0.5, None, ALU.mult))
    for _ in range(4):
        link(v.tensor_tensor(scratch, out, out, ALU.mult))
        link(v.tensor_tensor(scratch, scratch, half, ALU.mult))
        link(v.scalar_tensor_tensor(out, scratch, 1.5, out, ALU.add, ALU.mult))


def moments(nc, link, src, st, mv):
    for t in range(NT):
        ins = nc.vector.bn_stats(st[:, t, :], src[:, t, :])
    link(ins)
    for t in range(NT):
        ins = nc.vector.bn_aggr(mv[:, t, :], st[:, t, :])
    link(ins)


STAT_BUFFERS = (("st", [P, NT, 6], F32), ("mv", [P, NT, 2], F32), ("rs", [P, NT], F32), ("half", [P, NT], F32),
                ("scr", [P, NT], F32), ("guess", [P, NT], I32))


def norm_stage(nc, m, tag):
    with Stage(nc, tag, "step normed turned", STAT_BUFFERS) as (block, k):
        @block.vector
        def _(dve):
            link = linker(dve, k["step"])
            moments(nc, link, m.x, k["st"], k["mv"])
            inverse_root(nc, link, k["rs"][:], k["mv"][:, :, 1], k["half"][:], k["scr"][:], k["guess"][:])
            for t in range(NT):
                nc.vector.tensor_scalar(m.n[:, t, :], m.x[:, t, :], k["mv"][:, t, 0:1], k["rs"][:, t:t + 1],
                                        ALU.subtract, ALU.mult).then_inc(k["normed"], 1)

        @block.tensor
        def _(pe):
            for t in range(NT):
                pe.wait_ge(k["normed"], t + 1)
                for c in range(DC):
                    ins = nc.tensor.transpose(m.ps[:, c, t * P:(t + 1) * P], m.n[:, t, c * P:(c + 1) * P], m.ident[:])
            ins.then_inc(k["turned"], 1)

        @block.scalar
        def _(act):
            act.wait_ge(k["turned"], 1)
            nc.scalar.activation(m.nt[:, :, PAD:PAD + S], m.ps[:, 0:DC, :], ACT.Copy)


def affine_norm(nc, link, src, dst, gain, shift, k):
    moments(nc, link, src, k["st"], k["mv"])
    inverse_root(nc, link, k["rs"][:], k["mv"][:, :, 1], k["half"][:], k["scr"][:], k["guess"][:])
    for t in range(NT):
        ins = nc.vector.tensor_scalar(dst[:, t, :], src[:, t, :], k["mv"][:, t, 0:1], k["rs"][:, t:t + 1],
                                      ALU.subtract, ALU.mult)
    link(ins)
    for t in range(NT):
        ins = nc.vector.tensor_tensor(dst[:, t, :], dst[:, t, :], gain, ALU.mult)
    link(ins)
    for t in range(NT):
        ins = nc.vector.tensor_tensor(dst[:, t, :], dst[:, t, :], shift, ALU.add)
    link(ins)


def double_norm_stage(nc, m, tag, gain, shift):
    with Stage(nc, tag, "step", STAT_BUFFERS) as (block, k):
        @block.vector
        def _(dve):
            link = linker(dve, k["step"])
            moments(nc, link, m.x, k["st"], k["mv"])
            inverse_root(nc, link, k["rs"][:], k["mv"][:, :, 1], k["half"][:], k["scr"][:], k["guess"][:])
            for t in range(NT):
                ins = nc.vector.tensor_scalar(m.n[:, t, :], m.x[:, t, :], k["mv"][:, t, 0:1], k["rs"][:, t:t + 1],
                                              ALU.subtract, ALU.mult)
            link(ins)
            affine_norm(nc, link, m.n, m.y, gain, shift, k)
            for t in range(NT):
                nc.vector.tensor_tensor(m.x[:, t, :], m.x[:, t, :], m.y[:, t, :], ALU.add)


ATTENTION_BUFFERS = (
    ("qs", [P, H, S], BF16), ("ks", [P, H, S], BF16), ("v", [P, NT, H, HP], F32),
    ("ot", [P, NG, S], F32), ("on", [P, NG, S], F32),
    ("qp", [P, 3, DC, S], BF16), ("kp", [P, 3, DC, S], BF16),
    ("probs", [P, 3, 2, S], F32), ("recip", [P, S], F32),
    ("mx", [P, NG, NT, HG], F32), ("mxd", [P, NG, NT, HG], F32), ("m1", [P, NT, HG], BF16),
    ("mp", [P, NT, 2, HG], F32), ("mt", [2 * HG, 2, S], BF16), ("diag", [P, 2, P], F32),
    ("tq", [P, 1], F32), ("bqs", [P, DC], F32),
)


def attention_stage(nc, m, tag, w, source, causal):
    first = [(g, t, j) for g in range(NG) for t in range(NT) for j in range(HG)]
    second = [(g, t, j) for g in range(NG) for t in range(NT) for j in (0, 2)]
    per_group = NT * HG // 2
    LAG = HG * NT + 6
    BANK_M, BANK_O, BANK_P = 2, 3, 4

    def order():
        out, s = [], 0
        for u in range(len(first) + LAG + 2):
            if u < len(first):
                out.append(("max", u))
                if u % (HG * NT) == HG * NT - 1:
                    out.append(("turn", u // (HG * NT)))
            while s < len(second) and (2 * s + LAG <= u or u >= len(first)):
                out.append(("score", s))
                if s >= 1:
                    out.append(("value", s - 1))
                    if (s - 1) % per_group == per_group - 1:
                        out.append(("spread", (s - 1) // per_group))
                s += 1
        out.append(("value", len(second) - 1))
        out.append(("spread", NG - 1))
        turns = [o for o in out if o[0] == "turn"]
        for t in turns:
            at = out.index(t)
            out.remove(t)
            out.insert(min(at + 3, len(out)), t)
        for t in [o for o in out if o[0] == "spread"]:
            at = out.index(t)
            out.remove(t)
            out.insert(min(at + 2, len(out)), t)
        return out

    ORDER = order()
    misc = [o for o in ORDER if o[0] in ("turn", "spread")]
    sems = ("projq projk projv qk_out v_out scaled qsplit ksplit rep maxed maxdone turned turn_out mrow scored "
            "exped masked valued o_out spread recips normed proj step gstep ready")
    with Stage(nc, tag, sems, ATTENTION_BUFFERS) as (block, k):
        qf, kf = k["ot"][:, 0:DC, :], k["ot"][:, DC:2 * DC, :]
        qrest, krest = k["on"][:, 0:DC, :], k["on"][:, DC:2 * DC, :]
        kc = source
        koff = PAD if causal else 0

        @block.sync
        def _(sp):
            for dst, src in ((k["qs"][ROW_DELTA:ROW_MAX], m.quarter_rows), (k["ks"][ROW_MAX:ROWS], m.one_rows),
                             (k["ks"][ROW_DELTA:ROW_MAX], m.zero_rows if causal else m.delta_rows)):
                sp.dma_start(dst, src[:].unsqueeze(1).to_broadcast([dst.shape[0], H, S])).then_inc(k["rep"], 16)
            for part, ready, dst, side in ((k["kp"], k["ksplit"], k["ks"], 1), (k["qp"], k["qsplit"], k["qs"], 0)):
                for p in range(3):
                    sp.wait_ge(ready, p + 1)
                    for n, pair in enumerate(PAIRS):
                        if pair[side] == p:
                            sp.dma_start(dst[n * DK:(n + 1) * DK].rearrange("i h s -> i (h s)"),
                                         part[:, p].rearrange("p c s -> p (c s)")).then_inc(k["rep"], 16)
            for g in range(NG):
                sp.wait_ge(k["turn_out"], g + 1)
                sp.dma_start(k["qs"][ROW_MAX:ROWS, g * HG:(g + 1) * HG, :], k["mt"][:, g % 2, :]).then_inc(k["mrow"], 16)
            sp.wait_ge(k["mrow"], 16 * NG)

        @block.tensor
        def _(pe):
            for proj, bank, weight, src, off in ((k["projk"], 2, w.k, kc, koff), (k["projq"], 0, w.q, m.nt, PAD)):
                for c in range(DC):
                    for i in range(DC):
                        ins = nc.tensor.matmul(m.ps[:, bank + c, :], weight[:, i, c * P:(c + 1) * P],
                                               src[:, i, off:off + S], start=(i == 0), stop=(i == DC - 1))
                    ins.then_inc(proj, 1)
            for t in range(NT):
                for i in range(DC):
                    ins = nc.tensor.matmul(m.ps[:, 4 + t, 0:D], kc[:, i, koff + t * P:koff + (t + 1) * P],
                                           w.v[:, i, :], start=(i == 0), stop=(i == DC - 1))
                ins.then_inc(k["projv"], 1)
            pe.wait_ge(k["qk_out"], 2 * DC)
            pe.wait_ge(k["v_out"], NT)
            pe.wait_ge(k["rep"], 16 * (3 + 2 * len(PAIRS)))
            pe.wait_ge(k["ready"], 1)
            misc_used = 0
            for what, u in ORDER:
                if what == "max":
                    g, t, j = first[u]
                    h = g * HG + j
                    if u >= 2:
                        pe.wait_ge(k["maxed"], u - 1)
                    n = (t + 1) * P if causal else S
                    nc.tensor.matmul(m.ps[:, u % 2, 0:n], k["qs"][0:ROW_MAX, h, t * P:(t + 1) * P],
                                     k["ks"][0:ROW_MAX, h, 0:n], start=True, stop=True).then_inc(k["scored"], 1)
                elif what == "turn":
                    pe.wait_ge(k["maxdone"], u + 1)
                    if misc_used:
                        last, n = misc[misc_used - 1]
                        pe.wait_ge(k["turn_out"] if last == "turn" else k["recips"], n + 1)
                    misc_used += 1
                    for t in range(NT):
                        ins = nc.tensor.transpose(m.ps[0:2 * HG, BANK_M, t * P:(t + 1) * P],
                                                  k["mp"][:, t].rearrange("p a j -> p (a j)"), m.ident[:])
                    ins.then_inc(k["turned"], 1)
                elif what == "score":
                    g, t, j = second[u]
                    if u % per_group == 0:
                        pe.wait_ge(k["mrow"], 16 * (g + 1))
                    if u >= 2:
                        pe.wait_ge(k["exped"], u - 1)
                    q0 = t * P if causal else 0
                    for i in range(2):
                        h = g * HG + j + i
                        ins = nc.tensor.matmul(m.ps[:, BANK_P + 2 * (u % 2) + i, q0:S],
                                               k["ks"][0:ROWS, h, t * P:(t + 1) * P], k["qs"][0:ROWS, h, q0:S],
                                               start=True, stop=True)
                    ins.then_inc(k["proj"], 1)
                elif what == "value":
                    g, t, j = second[u]
                    if causal:
                        pe.wait_ge(k["masked"], u + 1)
                    else:
                        pe.wait_ge(k["exped"], u + 1)
                    if t == 0 and g >= 1:
                        pe.wait_ge(k["o_out"], g)
                    q0 = t * P if causal else 0
                    for i in range(2):
                        ins = nc.tensor.matmul(m.ps[HP * (j + i):HP * (j + i + 1), BANK_O, q0:S],
                                               k["v"][:, t, g * HG + j + i, :], k["probs"][:, u % 3, i, q0:S],
                                               start=(t == 0), stop=(t == NT - 1))
                    ins.then_inc(k["valued"], 1)
                else:
                    pe.wait_ge(k["o_out"], u + 1)
                    if misc_used:
                        last, n = misc[misc_used - 1]
                        pe.wait_ge(k["turn_out"] if last == "turn" else k["recips"], n + 1)
                    misc_used += 1
                    nc.tensor.matmul(m.ps[:, BANK_M, :], m.spread[:], k["ot"][:, u, :], start=True,
                                     stop=True).then_inc(k["spread"], 1)
            pe.wait_ge(k["exped"], len(second))
            pe.wait_ge(k["normed"], NG)
            for t in range(NT):
                for g in range(NG):
                    ins = nc.tensor.matmul(m.ps[:, 4 + t, 0:D], k["on"][:, g, t * P:(t + 1) * P], w.o[:, g, :],
                                           start=(g == 0), stop=(g == NG - 1))
                ins.then_inc(k["proj"], 1)

        @block.scalar
        def _(act):
            for c in range(DC):
                act.wait_ge(k["projk"], c + 1)
                nc.scalar.activation(kf[:, c, :], m.ps[:, 2 + c, :], ACT.Identity,
                                     bias=w.bk[:, c:c + 1]).then_inc(k["qk_out"], 1)
            act.wait_ge(k["scaled"], 1)
            for c in range(DC):
                act.wait_ge(k["projq"], c + 1)
                nc.scalar.activation(qf[:, c, :], m.ps[:, c, :], ACT.Identity, bias=k["bqs"][:, c:c + 1],
                                     scale=k["tq"][:, 0:1]).then_inc(k["qk_out"], 1)
            for what, u in ORDER:
                if what == "turn":
                    act.wait_ge(k["turned"], u + 1)
                    if u >= 2:
                        act.wait_ge(k["mrow"], 16 * (u - 1))
                    nc.scalar.activation(k["mt"][:, u % 2, :], m.ps[0:2 * HG, BANK_M, :], ACT.Copy)\
                        .then_inc(k["turn_out"], 1)
                elif what == "score":
                    g, t, j = second[u]
                    act.wait_ge(k["proj"], u + 1)
                    if u >= 3:
                        act.wait_ge(k["valued"], u - 2)
                    q0 = t * P if causal else 0
                    b = BANK_P + 2 * (u % 2)
                    nc.scalar.activation(k["probs"][:, u % 3, :, q0:S], m.ps[:, b:b + 2, q0:S], ACT.Exp)\
                        .then_inc(k["exped"], 1)
                elif what == "value" and u % per_group == per_group - 1:
                    g = u // per_group
                    act.wait_ge(k["valued"], u + 1)
                    nc.scalar.activation(k["ot"][:, g, :], m.ps[:, BANK_O, :], ACT.Copy).then_inc(k["o_out"], 1)

        @block.vector
        def _(dve):
            link = linker(dve, k["step"])
            if causal:
                nc.vector.memset(k["tq"][:], 1.0 / 16.0)
                link(nc.vector.memset(k["mx"][:], LOWEST))
            else:
                link(nc.vector.tensor_scalar(k["tq"][:], m.tau[:], 0.25, None, ALU.mult))
            nc.vector.tensor_scalar(k["bqs"][:], w.bq[:], k["tq"][:, 0:1], None, ALU.mult).then_inc(k["scaled"], 1)
            dve.wait_ge(k["qk_out"], 2 * DC)
            nc.vector.tensor_copy(k["qp"][:, 0], qf).then_inc(k["qsplit"], 1)
            dve.wait_ge(k["qsplit"], 1)
            link(nc.vector.tensor_tensor(qrest, qf, k["qp"][:, 0], ALU.subtract))
            nc.vector.tensor_copy(k["qp"][:, 1], qrest).then_inc(k["qsplit"], 1)
            dve.wait_ge(k["qsplit"], 2)
            nc.vector.tensor_tensor(k["qp"][:, 2], qrest, k["qp"][:, 1], ALU.subtract).then_inc(k["qsplit"], 1)
            dve.wait_ge(k["ready"], 1)
            for t in range(NT):
                dve.wait_ge(k["projv"], t + 1)
                nc.vector.tensor_tensor(k["v"][:, t, :, 0:DK], m.ps[:, 4 + t, 0:D].rearrange("p (h i) -> p h i", h=H),
                                        w.bv[:].rearrange("p (h i) -> p h i", h=H), ALU.add).then_inc(k["v_out"], 1)

            def split_maxima(g):
                if causal:
                    link(nc.vector.tensor_tensor(k["mx"][:, g], k["mx"][:, g], k["mxd"][:, g], ALU.max))
                link(nc.vector.tensor_scalar(k["m1"][:], k["mx"][:, g], -1.0, None, ALU.mult))
                if g >= 1:
                    dve.wait_ge(k["turned"], g)
                nc.vector.tensor_copy(k["mp"][:, :, 0, :], k["m1"][:])
                nc.vector.scalar_tensor_tensor(k["mp"][:, :, 1, :], k["mx"][:, g], -1.0, k["m1"][:], ALU.mult, ALU.subtract)\
                    .then_inc(k["maxdone"], 1)

            for what, u in ORDER:
                if what == "max":
                    g, t, j = first[u]
                    dve.wait_ge(k["scored"], u + 1)
                    if causal:
                        if t:
                            nc.vector.tensor_reduce(k["mx"][:, g, t, j:j + 1], m.ps[:, u % 2, 0:t * P], AX_X, ALU.max)
                        if u >= 2:
                            dve.wait_ge(k["maxed"], u - 1)
                        ins = nc.vector.tensor_tensor_reduce(
                            out=k["diag"][:, u % 2, :], in0=m.ps[:, u % 2, t * P:(t + 1) * P], in1=m.later[:], scale=1.0,
                            scalar=LOWEST, op0=ALU.add, op1=ALU.max, accum_out=k["mxd"][:, g, t, j:j + 1])
                    else:
                        ins = nc.vector.tensor_reduce(k["mx"][:, g, t, j:j + 1], m.ps[:, u % 2, :], AX_X, ALU.max)
                    ins.then_inc(k["maxed"], 1)
                    if u % (HG * NT) == HG * NT - 1:
                        dve.wait_ge(k["maxed"], u + 1)
                        split_maxima(g)
                elif what == "spread":
                    dve.wait_ge(k["spread"], u + 1)
                    if u >= 1:
                        dve.wait_ge(k["normed"], u)
                    nc.vector.reciprocal(k["recip"][:], m.ps[:, BANK_M, :]).then_inc(k["recips"], 1)
            for t in range(NT):
                dve.wait_ge(k["proj"], len(second) + t + 1)
                if causal:
                    nc.vector.tensor_copy(m.y[:, t, :], m.ps[:, 4 + t, 0:D])
                else:
                    nc.vector.tensor_tensor(m.x[:, t, :], m.x[:, t, :], m.ps[:, 4 + t, 0:D], ALU.add)

        @block.gpsimd
        def _(pool):
            link = linker(pool, k["gstep"])
            link(nc.gpsimd.memset(k["v"][:, :, :, DK:HP], 0.0))
            nc.gpsimd.memset(k["v"][:, :, :, DK:DK + 1], 1.0).then_inc(k["ready"], 1)
            pool.wait_ge(k["qk_out"], DC)
            nc.gpsimd.tensor_copy(k["kp"][:, 0], kf).then_inc(k["ksplit"], 1)
            pool.wait_ge(k["ksplit"], 1)
            link(nc.gpsimd.tensor_tensor(krest, kf, k["kp"][:, 0], ALU.subtract))
            nc.gpsimd.tensor_copy(k["kp"][:, 1], krest).then_inc(k["ksplit"], 1)
            pool.wait_ge(k["ksplit"], 2)
            nc.gpsimd.tensor_tensor(k["kp"][:, 2], krest, k["kp"][:, 1], ALU.subtract).then_inc(k["ksplit"], 1)
            for what, u in ORDER:
                if what == "score" and causal:
                    g, t, j = second[u]
                    pool.wait_ge(k["exped"], u + 1)
                    blk = k["probs"][:, u % 3, :, t * P:(t + 1) * P]
                    nc.gpsimd.affine_select(out=blk, in_=blk, compare_op=ALU.is_ge, fill=0.0, base=0,
                                            pattern=[[0, 2], [1, P]], channel_multiplier=-1).then_inc(k["masked"], 1)
                elif what == "spread":
                    pool.wait_ge(k["recips"], u + 1)
                    nc.gpsimd.tensor_tensor(k["on"][:, u, :], k["ot"][:, u, :], k["recip"][:], ALU.mult)\
                        .then_inc(k["normed"], 1)


def batch_stage(nc, m, b, x_in, ctx_in, tau, delta, lens, pt):
    bufs = (("drow", [1, S], F32), ("drest", [1, S], F32), ("dparts", [1, 3, S], BF16), ("len_i", [P, 1], I32))
    with Stage(nc, "load", "xin cin small turned step sent", bufs) as (block, k):
        @block.sync
        def _(sp):
            sp.dma_start(k["drow"][:], delta[bass.ds(b, 1), :]).then_inc(k["small"], 16)
            for dst, src in ((m.tau, tau), (m.pt, pt), (k["len_i"], lens)):
                sp.dma_start(dst[:], src.rearrange("(n a) -> n a", a=1)[bass.ds(b, 1), :].partition_broadcast(P))\
                    .then_inc(k["small"], 16)
            sp.wait_ge(k["step"], 4)
            sp.dma_start(m.delta_rows[:, :], k["dparts"][:].rearrange("a r s -> a (r s)")).then_inc(k["sent"], 16)
            sp.wait_ge(k["sent"], 16)

        @block.scalar
        def _(act):
            act.dma_start(m.x[:], x_in[bass.ds(b, 1)].rearrange("o (t p) d -> p (o t) d", p=P)).then_inc(k["xin"], 16)
            act.dma_start(m.c[:], ctx_in[bass.ds(b, 1)].rearrange("o (t p) d -> p (o t) d", p=P)).then_inc(k["cin"], 16)
            act.wait_ge(k["xin"], 16)
            act.wait_ge(k["turned"], 1)
            nc.scalar.activation(m.ct[:], m.ps[:, 0:DC, :], ACT.Copy)

        @block.tensor
        def _(pe):
            pe.wait_ge(k["cin"], 16)
            for t in range(NT):
                for c in range(DC):
                    ins = nc.tensor.transpose(m.ps[:, c, t * P:(t + 1) * P], m.c[:, t, c * P:(c + 1) * P], m.ident[:])
            ins.then_inc(k["turned"], 1)

        @block.vector
        def _(dve):
            link = linker(dve, k["step"])
            dve.wait_ge(k["small"], 64)
            link(nc.vector.tensor_copy(k["dparts"][:, 0], k["drow"][:]))
            link(nc.vector.tensor_tensor(k["drest"][:], k["drow"][:], k["dparts"][:, 0], ALU.subtract))
            link(nc.vector.tensor_copy(k["dparts"][:, 1], k["drest"][:]))
            link(nc.vector.tensor_tensor(k["dparts"][:, 2], k["drest"][:], k["dparts"][:, 1], ALU.subtract))
            nc.vector.tensor_copy(m.len_f[:], k["len_i"][:])


def window_stage(nc, m):
    bufs = (("end", [P, 2], F32), ("start", [P, 1], F32), ("dist", [P, S], F32), ("off", [P, S], F32))
    with Stage(nc, "win", "step sq", bufs) as (block, k):
        @block.vector
        def _(dve):
            link = linker(dve, k["step"])
            link(nc.vector.tensor_scalar(k["start"][:], m.pt[:], WINDOW, 0.0, ALU.subtract, ALU.max))
            link(nc.vector.tensor_scalar(k["end"][:, 0:1], m.pt[:], WINDOW, None, ALU.add))
            link(nc.vector.tensor_tensor(k["end"][:, 1:2], k["end"][:, 0:1], m.len_f[:], ALU.min))
            link(nc.vector.tensor_scalar(k["off"][:], m.index[:], k["start"][:, 0:1], None, ALU.is_lt))
            link(nc.vector.tensor_scalar(k["dist"][:], m.index[:], k["end"][:, 1:2], None, ALU.is_gt))
            link(nc.vector.tensor_tensor(k["off"][:], k["off"][:], k["dist"][:], ALU.max))
            nc.vector.tensor_scalar(m.keep[:], k["off"][:], -1.0, 1.0, ALU.mult, ALU.add)
            nc.vector.tensor_scalar(m.big[:], k["off"][:], MASKED, None, ALU.mult)
            link(nc.vector.tensor_scalar(k["dist"][:], m.index[:], m.pt[:, 0:1], None, ALU.subtract))
            nc.vector.tensor_tensor(k["off"][:], k["dist"][:], k["dist"][:], ALU.mult).then_inc(k["sq"], 1)

        @block.scalar
        def _(act):
            act.wait_ge(k["sq"], 1)
            nc.scalar.activation(m.gauss[:], k["off"][:], ACT.Exp, scale=-1.0 / DEV_POW)


def location_stage(nc, m, tag, w):
    bufs = (("qa", [P, DC, S], F32), ("sc", [P, NT, S], F32), ("mx", [P, NT], F32), ("nmx", [P, NT], F32),
            ("sums", [P, NT], F32), ("rsum", [P, NT], F32), ("al", [P, NT, S], F32), ("alt", [P, NT, S], F32),
            ("cx", [P, DC, S], F32), ("th", [P, NT, D], F32))
    with Stage(nc, tag, "proj proj_out scored masked maxed exped weighed turned turned_out ctx ctx_out outp tanhed step",
               bufs) as (block, k):
        @block.tensor
        def _(pe):
            for c in range(DC):
                for i in range(DC):
                    ins = nc.tensor.matmul(m.ps[:, c, :], w.a[:, i, c * P:(c + 1) * P], m.nt[:, i, PAD:PAD + S],
                                           start=(i == 0), stop=(i == DC - 1))
                ins.then_inc(k["proj"], 1)
            pe.wait_ge(k["proj_out"], DC)
            for t in range(NT):
                for c in range(DC):
                    ins = nc.tensor.matmul(m.ps[:, 4 + t, :], k["qa"][:, c, t * P:(t + 1) * P], m.ct[:, c, :],
                                           start=(c == 0), stop=(c == DC - 1))
                ins.then_inc(k["scored"], 1)
            for t in range(NT):
                pe.wait_ge(k["weighed"], t + 1)
                for n in range(NT):
                    ins = nc.tensor.transpose(m.ps[:, t, n * P:(n + 1) * P], k["al"][:, t, n * P:(n + 1) * P], m.ident[:])
                ins.then_inc(k["turned"], 1)
            pe.wait_ge(k["turned_out"], NT)
            for c in range(DC):
                for n in range(NT):
                    ins = nc.tensor.matmul(m.ps[:, 4 + c, :], m.c[:, n, c * P:(c + 1) * P], k["alt"][:, n, :],
                                           start=(n == 0), stop=(n == NT - 1))
                ins.then_inc(k["ctx"], 1)
            pe.wait_ge(k["ctx_out"], DC)
            for t in range(NT):
                for n in range(2 * DC):
                    lhs = k["cx"][:, n, t * P:(t + 1) * P] if n < DC else \
                        m.nt[:, n - DC, PAD + t * P:PAD + (t + 1) * P]
                    ins = nc.tensor.matmul(m.ps[:, t, 0:D], lhs, w.c[:, n, :], start=(n == 0), stop=(n == 2 * DC - 1))
                ins.then_inc(k["outp"], 1)

        @block.scalar
        def _(act):
            for c in range(DC):
                act.wait_ge(k["proj"], c + 1)
                nc.scalar.activation(k["qa"][:, c, :], m.ps[:, c, :], ACT.Copy).then_inc(k["proj_out"], 1)
            for t in range(NT):
                act.wait_ge(k["maxed"], t + 1)
                nc.scalar.activation(k["al"][:, t, :], k["sc"][:, t, :], ACT.Exp, bias=k["nmx"][:, t:t + 1],
                                     accum_out=k["sums"][:, t:t + 1]).then_inc(k["exped"], 1)
            for t in range(NT):
                act.wait_ge(k["turned"], t + 1)
                nc.scalar.activation(k["alt"][:, :, t * P:(t + 1) * P],
                                     m.ps[:, t, :].rearrange("p (n q) -> p n q", n=NT), ACT.Copy)\
                    .then_inc(k["turned_out"], 1)
            for c in range(DC):
                act.wait_ge(k["ctx"], c + 1)
                nc.scalar.activation(k["cx"][:, c, :], m.ps[:, 4 + c, :], ACT.Copy).then_inc(k["ctx_out"], 1)
            for t in range(NT):
                act.wait_ge(k["outp"], t + 1)
                nc.scalar.activation(k["th"][:, t, :], m.ps[:, t, 0:D], ACT.Tanh).then_inc(k["tanhed"], 1)

        @block.vector
        def _(dve):
            link = linker(dve, k["step"])
            for t in range(NT):
                dve.wait_ge(k["scored"], t + 1)
                link(nc.vector.tensor_tensor(k["sc"][:, t, :], m.ps[:, 4 + t, :], m.keep[:], ALU.mult))
                link(nc.vector.tensor_tensor(k["sc"][:, t, :], k["sc"][:, t, :], m.big[:], ALU.add))
                nc.vector.tensor_reduce(k["nmx"][:, t:t + 1], k["sc"][:, t, :], AX_X, ALU.max, negate=True)\
                    .then_inc(k["maxed"], 1)
            for t in range(NT):
                dve.wait_ge(k["exped"], t + 1)
                link(nc.vector.reciprocal(k["rsum"][:, t:t + 1], k["sums"][:, t:t + 1]))
                nc.vector.scalar_tensor_tensor(k["al"][:, t, :], k["al"][:, t, :], k["rsum"][:, t:t + 1], m.gauss[:],
                                               ALU.mult, ALU.mult).then_inc(k["weighed"], 1)
            for t in range(NT):
                dve.wait_ge(k["tanhed"], t + 1)
                nc.vector.tensor_tensor(m.x[:, t, :], m.x[:, t, :], k["th"][:, t, :], ALU.add)


ROUTE_BUFFERS = (("lg", [P, NT, E1], F32), ("pr", [P, NT, E1], F32), ("rmx", [P, NT], F32), ("rsm", [P, NT], F32),
                 ("top", [P, NT, 8], F32), ("idx", [P, NT, 8], U32), ("idf", [P, NT, 8], F32), ("wt", [P, NT, 2], F32),
                 ("oh", [P, NT, E1], F32))


def spread_over(ap, n):
    return ap.unsqueeze(2).to_broadcast([P, NT, n])


def softmax_steps(nc, dve, link, k, n):
    lg, pr = k["lg"][:, :, 0:n], k["pr"][:, :, 0:n]
    link(nc.vector.tensor_reduce(k["rmx"][:], lg, AX_X, ALU.max))
    nc.vector.tensor_tensor(lg, lg, spread_over(k["rmx"][:], n), ALU.subtract).then_inc(k["logits"], 1)
    dve.wait_ge(k["rexp"], 1)
    link(nc.vector.tensor_reduce(k["rsm"][:], pr, AX_X, ALU.add))
    link(nc.vector.reciprocal(k["rsm"][:], k["rsm"][:]))
    link(nc.vector.tensor_tensor(pr, pr, spread_over(k["rsm"][:], n), ALU.mult))


def top_steps(nc, link, k, values, n):
    for t in range(NT):
        ins = nc.vector.max(k["top"][:, t, :], values[:, t, 0:n])
    link(ins)
    for t in range(NT):
        ins = nc.vector.max_index(k["idx"][:, t, :], k["top"][:, t, :], values[:, t, 0:n])
    link(ins)
    link(nc.vector.tensor_copy(k["idf"][:], k["idx"][:]))


def one_hot(nc, m, link, k, out, choice, n):
    link(nc.vector.tensor_tensor(out, m.columns[:, :, 0:n], k["idf"][:, :, choice:choice + 1].to_broadcast([P, NT, n]),
                                 ALU.is_equal))


def combine_steps(nc, m, link, k, n):
    comb, oh = m.comb[:, :, 0:n], k["oh"][:, :, 0:n]
    one_hot(nc, m, link, k, comb, 0, n)
    one_hot(nc, m, link, k, oh, 1, n)
    link(nc.vector.tensor_tensor(comb, comb, k["wt"][:, :, 0:1].to_broadcast([P, NT, n]), ALU.mult))
    link(nc.vector.tensor_tensor(oh, oh, k["wt"][:, :, 1:2].to_broadcast([P, NT, n]), ALU.mult))
    link(nc.vector.tensor_tensor(comb, comb, oh, ALU.add))


def logits_on_pe(nc, m, k, src, off, weight, n):
    for t in range(NT):
        for i in range(DC):
            ins = nc.tensor.matmul(m.ps[:, 0, t * E1:t * E1 + n], src[:, i, off + t * P:off + (t + 1) * P],
                                   weight[:, i, :], start=(i == 0), stop=(i == DC - 1))
    ins.then_inc(k["routed"], 1)


def psum_logits(m, n):
    return m.ps[:, 0, 0:NT * E1].rearrange("p (t e) -> p t e", t=NT)[:, :, 0:n]


def conv_mixture_stage(nc, m, w, gate_w, up_w, down_w):
    RING = 3
    bufs = ROUTE_BUFFERS + (("wg", [P, RING, DC, I1], F32), ("wu", [P, RING, DC, I1], F32), ("wd", [P, RING, D], F32),
                            ("th", [P, 2, S], F32), ("ga", [P, 2, S], F32), ("hid", [P, 2, S], F32),
                            ("ssum", [P, NT], F32))
    EXPERTS = E1 - 1
    units = EXPERTS + 1
    sems = "routed logits rexp step wload0 wload1 wload2 gated tanhed hidden down added"
    with Stage(nc, "cmix", sems, bufs) as (block, k):
        wload = (k["wload0"], k["wload1"], k["wload2"])
        @block.sync
        def _(sp):
            for e in range(EXPERTS):
                if e >= RING:
                    sp.wait_ge(k["down"], e - RING + 2)
                r = e % RING
                sp.dma_start(k["wg"][:, r], gate_w[e].rearrange("(c p) i -> p c i", p=P)).then_inc(wload[r], 16)
                sp.dma_start(k["wu"][:, r], up_w[e].rearrange("(c p) i -> p c i", p=P)).then_inc(wload[r], 16)
                sp.dma_start(k["wd"][:, r], down_w[e]).then_inc(wload[r], 16)

        @block.tensor
        def _(pe):
            logits_on_pe(nc, m, k, m.nt, PAD, w.router, E1)

            def down(u):
                pe.wait_ge(k["hidden"], u + 1)
                if u >= 1:
                    pe.wait_ge(k["added"], u)
                for t in range(NT):
                    ins = nc.tensor.matmul(m.ps[:, 5 + t // 2, (t % 2) * D:(t % 2 + 1) * D],
                                           k["hid"][:, u % 2, t * P:(t + 1) * P],
                                           w.sdown[:] if u == 0 else k["wd"][:, (u - 1) % RING, :], start=True, stop=True)
                ins.then_inc(k["down"], 1)

            for u in range(units):
                gate, up = m.ps[:, 1 + 2 * (u % 2), :], m.ps[:, 2 + 2 * (u % 2), :]
                if u >= 2:
                    pe.wait_ge(k["hidden"], u - 1)
                if u == 0:
                    n = 0
                    for tap in range(KS1):
                        for i in range(DC):
                            nc.tensor.matmul(gate, w.conv[:, tap, i, :], m.nt[:, i, tap:tap + S], start=(n == 0),
                                             stop=(n == KS1 * DC - 1))
                            n += 1
                    for i in range(DC):
                        ins = nc.tensor.matmul(up, w.sup[:, i, :], m.nt[:, i, PAD:PAD + S], start=(i == 0),
                                               stop=(i == DC - 1))
                else:
                    r = (u - 1) % RING
                    pe.wait_ge(wload[r], 48 * ((u - 1) // RING + 1))
                    for bank, wt in ((gate, k["wg"]), (up, k["wu"])):
                        for i in range(DC):
                            ins = nc.tensor.matmul(bank, wt[:, r, i, :], m.nt[:, i, PAD:PAD + S], start=(i == 0),
                                                   stop=(i == DC - 1))
                ins.then_inc(k["gated"], 1)
                if u >= 1:
                    down(u - 1)
            down(units - 1)

        @block.scalar
        def _(act):
            act.wait_ge(k["logits"], 1)
            nc.scalar.activation(k["pr"][:], k["lg"][:], ACT.Exp).then_inc(k["rexp"], 1)
            for u in range(units):
                act.wait_ge(k["gated"], u + 1)
                if u >= 2:
                    act.wait_ge(k["hidden"], u - 1)
                nc.scalar.activation(k["th"][:, u % 2, :], m.ps[:, 1 + 2 * (u % 2), :], ACT.Tanh, scale=0.5)\
                    .then_inc(k["tanhed"], 1)

        @block.vector
        def _(dve):
            link = linker(dve, k["step"])
            dve.wait_ge(k["routed"], 1)
            link(nc.vector.tensor_tensor(k["lg"][:], psum_logits(m, E1),
                                         w.rbias[:].unsqueeze(1).to_broadcast([P, NT, E1]), ALU.add))
            softmax_steps(nc, dve, link, k, E1)
            top_steps(nc, link, k, k["pr"], E1)
            link(nc.vector.tensor_tensor(k["ssum"][:], k["top"][:, :, 0], k["top"][:, :, 1], ALU.add))
            link(nc.vector.tensor_scalar(k["ssum"][:], k["ssum"][:], 1e-6, None, ALU.add))
            link(nc.vector.reciprocal(k["ssum"][:], k["ssum"][:]))
            link(nc.vector.tensor_tensor(k["wt"][:], k["top"][:, :, 0:2], spread_over(k["ssum"][:], 2), ALU.mult))
            combine_steps(nc, m, link, k, E1)
            for t in range(NT):
                ins = nc.vector.scalar_tensor_tensor(m.x[:, t, :], m.n[:, t, :], m.comb[:, t, EXPERTS:E1],
                                                     m.x[:, t, :], ALU.mult, ALU.add)
            link(ins)

            def add(u):
                dve.wait_ge(k["down"], u + 1)
                for t in range(NT):
                    y = m.ps[:, 5 + t // 2, (t % 2) * D:(t % 2 + 1) * D]
                    if u == 0:
                        ins = nc.vector.tensor_tensor(m.x[:, t, :], m.x[:, t, :], y, ALU.add)
                    else:
                        ins = nc.vector.scalar_tensor_tensor(m.x[:, t, :], y, m.comb[:, t, u - 1:u], m.x[:, t, :],
                                                             ALU.mult, ALU.add)
                ins.then_inc(k["added"], 1)

            for u in range(units):
                dve.wait_ge(k["tanhed"], u + 1)
                gate, up = m.ps[:, 1 + 2 * (u % 2), :], m.ps[:, 2 + 2 * (u % 2), :]
                link(nc.vector.scalar_tensor_tensor(k["ga"][:, u % 2, :], k["th"][:, u % 2, :], 1.0, gate, ALU.add, ALU.mult))
                if u >= 2:
                    dve.wait_ge(k["down"], u - 1)
                nc.vector.scalar_tensor_tensor(k["hid"][:, u % 2, :], k["ga"][:, u % 2, :], 0.5, up, ALU.mult, ALU.mult)\
                    .then_inc(k["hidden"], 1)
                if u >= 1:
                    add(u - 1)
                    if u >= 1:
                        dve.wait_ge(k["added"], u)
            add(units - 1)


def pair_route_stage(nc, m, w):
    bufs = ROUTE_BUFFERS + STAT_BUFFERS + (("an", [P, NT, D], F32), ("dl", [P, NT], F32), ("de", [P, NT], F32))
    with Stage(nc, "proute", "step normed turned turned_out routed logits rexp", bufs) as (block, k):
        @block.vector
        def _(dve):
            link = linker(dve, k["step"])
            affine_norm(nc, link, m.y, k["an"], m.ln1_g[:], m.ln1_b[:], k)
            for t in range(NT):
                ins = nc.vector.tensor_tensor(m.y[:, t, :], k["an"][:, t, :], m.n[:, t, :], ALU.add)
            ins.then_inc(k["normed"], 1)
            dve.wait_ge(k["routed"], 1)
            link(nc.vector.tensor_copy(k["lg"][:, :, 0:E2], psum_logits(m, E2)))
            top_steps(nc, link, k, k["lg"], E2)
            nc.vector.tensor_tensor(k["dl"][:], k["top"][:, :, 1], k["top"][:, :, 0], ALU.subtract).then_inc(k["logits"], 1)
            dve.wait_ge(k["rexp"], 1)
            link(nc.vector.tensor_scalar(k["dl"][:], k["de"][:], 1.0, None, ALU.add))
            link(nc.vector.reciprocal(k["wt"][:, :, 0], k["dl"][:]))
            link(nc.vector.tensor_tensor(k["wt"][:, :, 1], k["de"][:], k["wt"][:, :, 0], ALU.mult))
            combine_steps(nc, m, link, k, E2)

        @block.tensor
        def _(pe):
            pe.wait_ge(k["normed"], 1)
            for t in range(NT):
                for c in range(DC):
                    ins = nc.tensor.transpose(m.ps[:, 2 + c, t * P:(t + 1) * P], m.y[:, t, c * P:(c + 1) * P],
                                              m.ident[:])
            ins.then_inc(k["turned"], 1)
            pe.wait_ge(k["turned_out"], 1)
            logits_on_pe(nc, m, k, m.nt, PAD, w.gate2, E2)

        @block.scalar
        def _(act):
            act.wait_ge(k["turned"], 1)
            nc.scalar.activation(m.nt[:, :, PAD:PAD + S], m.ps[:, 2:2 + DC, :], ACT.Copy).then_inc(k["turned_out"], 1)
            act.wait_ge(k["logits"], 1)
            nc.scalar.activation(k["de"][:], k["dl"][:], ACT.Exp).then_inc(k["rexp"], 1)


def single_route_stage(nc, m, w):
    bufs = ROUTE_BUFFERS + (("ranks", [P, NT, E2], F32), ("kept", [P, NT, E2], F32))
    with Stage(nc, "sroute", "step routed logits rexp hot ranked", bufs) as (block, k):
        @block.tensor
        def _(pe):
            logits_on_pe(nc, m, k, m.nt, PAD, w.gate3, E2)
            pe.wait_ge(k["hot"], 1)
            for t in range(NT):
                for n in range(t + 1):
                    nc.tensor.matmul(m.ps[:, 1, t * E2:(t + 1) * E2], m.earlier[:] if n == t else m.ones[:],
                                     k["oh"][:, n, 0:E2], start=(n == 0), stop=(n == t))
            for n in range(NT):
                ins = nc.tensor.matmul(m.ps[:, 1, NT * E2:(NT + 1) * E2], m.ones[:], k["oh"][:, n, 0:E2],
                                       start=(n == 0), stop=(n == NT - 1))
            ins.then_inc(k["ranked"], 1)

        @block.scalar
        def _(act):
            act.wait_ge(k["logits"], 1)
            nc.scalar.activation(k["pr"][:, :, 0:E2], k["lg"][:, :, 0:E2], ACT.Exp).then_inc(k["rexp"], 1)

        @block.vector
        def _(dve):
            link = linker(dve, k["step"])
            dve.wait_ge(k["routed"], 1)
            link(nc.vector.tensor_copy(k["lg"][:, :, 0:E2], psum_logits(m, E2)))
            softmax_steps(nc, dve, link, k, E2)
            top_steps(nc, link, k, k["pr"], E2)
            one_hot(nc, m, link, k, k["oh"][:, :, 0:E2], 0, E2)
            nc.vector.tensor_tensor(m.comb[:, :, 0:E2], k["oh"][:, :, 0:E2], k["pr"][:, :, 0:E2], ALU.mult)\
                .then_inc(k["hot"], 1)
            dve.wait_ge(k["ranked"], 1)
            ranks = m.ps[:, 1, 0:NT * E2].rearrange("p (t e) -> p t e", t=NT)
            link(nc.vector.tensor_tensor(k["ranks"][:], ranks, m.used[:].unsqueeze(1).to_broadcast([P, NT, E2]),
                                         ALU.add))
            link(nc.vector.tensor_scalar(k["kept"][:], k["ranks"][:], float(CAPACITY), None, ALU.is_le))
            link(nc.vector.tensor_tensor(m.comb[:, :, 0:E2], m.comb[:, :, 0:E2], k["kept"][:], ALU.mult))
            nc.vector.tensor_tensor(m.used[:], m.used[:], m.ps[:, 1, NT * E2:(NT + 1) * E2], ALU.add)


def mixture_stage(nc, m, tag, b1, b2, w1, w2):
    bufs = (("w1", [P, 2, DC, FF], F32), ("w2", [P, 2, FC, D], F32), ("hidden", [P, 2, FC, S], F32),
            ("ct8", [E2, S], F32))
    sems = "wl1a wl1b wl2a wl2b turned turned_out bias chunk relu out done"
    with Stage(nc, tag, sems, bufs) as (block, k):
        wl1, wl2 = (k["wl1a"], k["wl1b"]), (k["wl2a"], k["wl2b"])

        @block.sync
        def _(sp):
            for e in range(E2):
                if e >= 2:
                    sp.wait_ge(k["chunk"], FC * (e - 1))
                sp.dma_start(k["w1"][:, e % 2], w1[e].rearrange("(c p) f -> p c f", p=P)).then_inc(wl1[e % 2], 16)
                if e >= 2:
                    sp.wait_ge(k["out"], e - 1)
                sp.dma_start(k["w2"][:, e % 2], w2[e].rearrange("(c p) d -> p c d", p=P)).then_inc(wl2[e % 2], 16)

        @block.tensor
        def _(pe):
            for t in range(NT):
                ins = nc.tensor.transpose(m.ps[0:E2, 4, t * P:(t + 1) * P], m.comb[:, t, 0:E2], m.ident[:])
            ins.then_inc(k["turned"], 1)
            pe.wait_ge(k["turned_out"], 1)
            for t in range(NT):
                ins = nc.tensor.matmul(m.ps[:, 6 + t // 2, (t % 2) * D:(t % 2 + 1) * D], k["ct8"][:, t * P:(t + 1) * P],
                                       b2[:], start=True, stop=True)
            ins.then_inc(k["bias"], 1)

            def out(e):
                pe.wait_ge(wl2[e % 2], 16 * (e // 2 + 1))
                pe.wait_ge(k["relu"], FC * (e + 1))
                pe.wait_ge(k["done"], e + 1)
                for t in range(NT):
                    for f in range(FC):
                        ins = nc.tensor.matmul(m.ps[:, 6 + t // 2, (t % 2) * D:(t % 2 + 1) * D],
                                               k["hidden"][:, e % 2, f, t * P:(t + 1) * P], k["w2"][:, e % 2, f, :],
                                               start=(f == 0), stop=(f == FC - 1))
                ins.then_inc(k["out"], 1)

            for e in range(E2):
                pe.wait_ge(wl1[e % 2], 16 * (e // 2 + 1))
                for f in range(FC):
                    n = e * FC + f
                    if n >= 4:
                        pe.wait_ge(k["relu"], n - 3)
                    for i in range(DC):
                        ins = nc.tensor.matmul(m.ps[:, n % 4, :], k["w1"][:, e % 2, i, f * P:(f + 1) * P],
                                               m.nt[:, i, PAD:PAD + S], start=(i == 0), stop=(i == DC - 1))
                    ins.then_inc(k["chunk"], 1)
                if e >= 1:
                    out(e - 1)
            out(E2 - 1)

        @block.scalar
        def _(act):
            act.wait_ge(k["turned"], 1)
            nc.scalar.activation(k["ct8"][:], m.ps[0:E2, 4, :], ACT.Copy).then_inc(k["turned_out"], 1)
            for e in range(E2):
                if e >= 2:
                    act.wait_ge(k["out"], e - 1)
                for f in range(FC):
                    n = e * FC + f
                    act.wait_ge(k["chunk"], n + 1)
                    nc.scalar.activation(k["hidden"][:, e % 2, f, :], m.ps[:, n % 4, :], ACT.Relu, bias=b1[:, e, f:f + 1]).then_inc(k["relu"], 1)

        @block.vector
        def _(dve):
            dve.wait_ge(k["bias"], 1)
            for t in range(NT):
                ins = nc.vector.tensor_copy(m.y2[:, t, :], m.ps[:, 6 + t // 2, (t % 2) * D:(t % 2 + 1) * D])
            ins.then_inc(k["done"], 1)
            for e in range(E2):
                dve.wait_ge(k["out"], e + 1)
                dve.wait_ge(k["done"], e + 1)
                for t in range(NT):
                    ins = nc.vector.scalar_tensor_tensor(
                        m.y2[:, t, :], m.ps[:, 6 + t // 2, (t % 2) * D:(t % 2 + 1) * D], m.comb[:, t, e:e + 1],
                        m.y2[:, t, :], ALU.mult, ALU.add)
                ins.then_inc(k["done"], 1)


def close_pair_stage(nc, m):
    with Stage(nc, "close2", "step", STAT_BUFFERS) as (block, k):
        @block.vector
        def _(dve):
            link = linker(dve, k["step"])
            affine_norm(nc, link, m.y2, m.y2, m.ln2_g[:], m.ln2_b[:], k)
            for t in range(NT):
                ins = nc.vector.tensor_tensor(m.y2[:, t, :], m.y2[:, t, :], m.y[:, t, :], ALU.add)
            link(ins)
            for t in range(NT):
                nc.vector.tensor_tensor(m.x[:, t, :], m.x[:, t, :], m.y2[:, t, :], ALU.add)


def store_stage(nc, m, b, out, mix):
    with Stage(nc, "store", "summed stored") as (block, k):
        @block.vector
        def _(dve):
            for t in range(NT):
                if not mix:
                    ins = nc.vector.tensor_copy(m.x[:, t, :], m.x[:, t, :])
                    continue
                ins = nc.vector.tensor_tensor(m.x[:, t, :], m.x[:, t, :], m.y2[:, t, :], ALU.add)
            ins.then_inc(k["summed"], 1)

        @block.sync
        def _(sp):
            sp.wait_ge(k["summed"], 1)
            sp.dma_start(out[bass.ds(b, 1)].rearrange("o (t p) d -> p (o t) d", p=P), m.x[:]).then_inc(k["stored"], 16)
            sp.wait_ge(k["stored"], 16)


def constant_stage(nc, m, loads):
    with Stage(nc, "const", "loaded zeroed made") as (block, k):
        @block.sync
        def _(sp):
            for dst, src in loads:
                sp.dma_start(dst, src).then_inc(k["loaded"], 16)
            sp.wait_ge(k["loaded"], 16 * len(loads))

        @block.vector
        def _(dve):
            nc.vector.memset(m.ones[:], 1.0)
            nc.vector.memset(m.nt[:, :, 0:PAD], 0.0)
            nc.vector.memset(m.used[:], 0.0)
            nc.vector.memset(m.quarter_rows[:], 0.25)
            nc.vector.memset(m.one_rows[:], 1.0)
            nc.vector.memset(m.zero_rows[:], 0.0)

        @block.gpsimd
        def _(pool):
            g = nc.gpsimd
            for tile, value in ((m.ident, 0.0), (m.later, 0.0), (m.earlier, 1.0), (m.spread, 0.0)):
                ins = g.memset(tile[:], value)
            ins.then_inc(k["zeroed"], 1)
            pool.wait_ge(k["zeroed"], 1)
            g.affine_select(out=m.ident[:], in_=m.ident[:], compare_op=ALU.not_equal, fill=1.0, base=0,
                            pattern=[[-1, P]], channel_multiplier=1)
            g.affine_select(out=m.later[:], in_=m.later[:], compare_op=ALU.is_ge, fill=LOWEST, base=0,
                            pattern=[[-1, P]], channel_multiplier=1)
            g.affine_select(out=m.earlier[:], in_=m.earlier[:], compare_op=ALU.is_ge, fill=0.0, base=0,
                            pattern=[[1, P]], channel_multiplier=-1)
            view = m.spread[:].rearrange("p (j i) -> p j i", j=HG)
            g.affine_select(out=view, in_=view, compare_op=ALU.not_equal, fill=1.0, base=-DK,
                            pattern=[[-HP, HG], [0, HP]], channel_multiplier=1)
            g.iota(m.index[:], pattern=[[1, S]], base=0, channel_multiplier=0, allow_small_or_imprecise_dtypes=True)
            g.iota(m.columns[:], pattern=[[0, NT], [1, E1]], base=0, channel_multiplier=0,
                   allow_small_or_imprecise_dtypes=True)


class Memory:

    def __init__(self, buffer):
        self.x = buffer("x", [P, NT, D], F32)
        self.n = buffer("n", [P, NT, D], F32)
        self.c = buffer("c", [P, NT, D], F32)
        self.y = buffer("y", [P, NT, D], F32)
        self.y2 = buffer("y2", [P, NT, D], F32)
        self.nt = buffer("nt", [P, DC, PAD + S], F32)
        self.ct = buffer("ct", [P, DC, S], F32)
        self.comb = buffer("comb", [P, NT, E1], F32)
        self.keep = buffer("keep", [P, S], F32)
        self.big = buffer("big", [P, S], F32)
        self.gauss = buffer("gauss", [P, S], F32)
        self.index = buffer("index", [P, S], F32)
        self.columns = buffer("columns", [P, NT, E1], F32)
        self.ident = buffer("ident", [P, P], F32)
        self.later = buffer("later", [P, P], F32)
        self.earlier = buffer("earlier", [P, P], F32)
        self.spread = buffer("spread", [P, P], F32)
        self.ones = buffer("ones", [P, P], F32)
        self.used = buffer("used", [P, E2], F32)
        self.quarter_rows = buffer("quarter_rows", [3, S], BF16)
        self.one_rows = buffer("one_rows", [2, S], BF16)
        self.zero_rows = buffer("zero_rows", [3, S], BF16)
        self.delta_rows = buffer("delta_rows", [3, S], BF16)
        self.tau = buffer("tau", [P, 1], F32)
        self.pt = buffer("pt", [P, 1], F32)
        self.len_f = buffer("len_f", [P, 1], F32)
        self.ln0_g = buffer("ln0_g", [P, D], F32)
        self.ln0_b = buffer("ln0_b", [P, D], F32)
        self.ln1_g = buffer("ln1_g", [P, D], F32)
        self.ln1_b = buffer("ln1_b", [P, D], F32)
        self.ln2_g = buffer("ln2_g", [P, D], F32)
        self.ln2_b = buffer("ln2_b", [P, D], F32)


class Weights:
    pass


class AttentionWeights:

    def __init__(self, buffer, tag):
        self.q, self.k, self.v = (buffer(f"{tag}_w{n}", [P, DC, D], F32) for n in "qkv")
        self.o = buffer(f"{tag}_wo", [P, NG, D], F32)
        self.bq, self.bk = (buffer(f"{tag}_b{n}", [P, DC], F32) for n in "qk")
        self.bv = buffer(f"{tag}_bv", [P, D], F32)

    def loads(self, a, tag):
        chunks = "(c p) n -> p c n"
        return [(self.q[:], a[f"{tag}_wq"].rearrange(chunks, p=P)), (self.k[:], a[f"{tag}_wk"].rearrange(chunks, p=P)),
                (self.v[:], a[f"{tag}_wv"].rearrange(chunks, p=P)), (self.o[:], a[f"{tag}_wo"].rearrange(chunks, p=P)),
                (self.bq[:], a[f"{tag}_bq"]), (self.bk[:], a[f"{tag}_bk"]), (self.bv[:], row(a[f"{tag}_bv"]))]


def row(vector):
    return vector.rearrange("(a n) -> a n", a=1).partition_broadcast(P)


def residual_stack(nc, a, stop=99):
    with ExitStack() as ctx:
        def buffer(name, shape, dt):
            return ctx.enter_context(nc.sbuf_tensor(name, shape, dt))

        m = Memory(buffer)
        m.ps = ctx.enter_context(nc.psum_tensor("banks", [P, 8, S], F32))
        w = Weights()
        attn = {tag: AttentionWeights(buffer, tag) for tag in ("a0", "a1", "a2")}
        loc = {}
        for tag in ("l2", "l3"):
            loc[tag] = Weights()
            loc[tag].a = buffer(f"{tag}_wa", [P, DC, D], F32)
            loc[tag].c = buffer(f"{tag}_wc", [P, 2 * DC, D], F32)
        w.router, w.rbias = buffer("w_router", [P, DC, E1], F32), buffer("w_rbias", [P, E1], F32)
        w.conv = buffer("w_conv", [P, KS1, DC, I1], F32)
        w.sup, w.sdown = buffer("w_sup", [P, DC, I1], F32), buffer("w_sdown", [P, D], F32)
        w.gate2, w.gate3 = buffer("w_gate2", [P, DC, E2], F32), buffer("w_gate3", [P, DC, E2], F32)
        b1 = {tag: buffer(f"{tag}_b1", [P, E2, FC], F32) for tag in ("m2", "m3")}
        b2 = {tag: buffer(f"{tag}_b2", [E2, D], F32) for tag in ("m2", "m3")}

        chunks = "(c p) n -> p c n"
        loads = []
        for tag in attn:
            loads += attn[tag].loads(a, tag)
        for tag in loc:
            loads += [(loc[tag].a[:], a[f"{tag}_wa"].rearrange(chunks, p=P)),
                      (loc[tag].c[:], a[f"{tag}_wc"].rearrange(chunks, p=P))]
        loads += [(w.router[:], a["router_w"].rearrange(chunks, p=P)), (w.rbias[:], row(a["router_bias"])),
                  (w.conv[:], a["conv_w"]),
                  (w.sup[:], a["shared_up"].rearrange(chunks, p=P)), (w.sdown[:], a["shared_down"]),
                  (w.gate2[:], a["gate2"].rearrange(chunks, p=P)), (w.gate3[:], a["gate3"].rearrange(chunks, p=P))]
        for tag in b1:
            loads += [(b1[tag][:], a[f"{tag}_b1"]), (b2[tag][:], a[f"{tag}_b2"])]
        loads += [(m.ln0_g[:], row(a["ln0_g"])), (m.ln0_b[:], row(a["ln0_b"])), (m.ln1_g[:], row(a["ln1_g"])),
                  (m.ln1_b[:], row(a["ln1_b"])), (m.ln2_g[:], row(a["ln2_g"])), (m.ln2_b[:], row(a["ln2_b"]))]
        constant_stage(nc, m, loads)

        with nc.Fori(0, B) as b:
            batch_stage(nc, m, b, a["x"], a["ctx"], a["tau"], a["delta"], a["lens"], a["pt"])
            window_stage(nc, m)
            norm_stage(nc, m, "n0")
            attention_stage(nc, m, "at0", attn["a0"], m.ct, False)
            if stop > 1:
                double_norm_stage(nc, m, "dn", m.ln0_g[:], m.ln0_b[:])
            if stop > 2:
                norm_stage(nc, m, "n1")
                attention_stage(nc, m, "at1", attn["a1"], m.ct, False)
            if stop > 3:
                norm_stage(nc, m, "n2")
                conv_mixture_stage(nc, m, w, a["gate_w"], a["up_w"], a["down_w"])
            if stop > 4:
                norm_stage(nc, m, "n3")
                location_stage(nc, m, "loc2", loc["l2"])
            if stop > 5:
                norm_stage(nc, m, "n4")
                attention_stage(nc, m, "at2", attn["a2"], m.nt, True)
                pair_route_stage(nc, m, w)
                mixture_stage(nc, m, "mx2", b1["m2"], b2["m2"], a["m2_w1"], a["m2_w2"])
                close_pair_stage(nc, m)
            if stop > 6:
                norm_stage(nc, m, "n5")
                location_stage(nc, m, "loc3", loc["l3"])
            if stop > 7:
                norm_stage(nc, m, "n6")
                single_route_stage(nc, m, w)
                mixture_stage(nc, m, "mx3", b1["m3"], b2["m3"], a["m3_w1"], a["m3_w2"])
            store_stage(nc, m, b, a["out"], stop > 7)


def lay_out(inputs):
    import numpy as np
    i = {n: np.asarray(v) for n, v in inputs.items()}
    c, dim, pair = np.meshgrid(np.arange(DC), np.arange(DK), np.arange(H // 2), indexing="ij")
    cols = ((pair * 2 + c) * DK + dim).reshape(-1)
    f32 = np.float32

    def columns(b):
        return b[cols].reshape(DC, P).T

    def out_rows(wo_t, bo):
        o = np.zeros((NG, HG, HP, D), f32)
        o[:, :, :DK] = wo_t.reshape(NG, HG, DK, D)
        o[0, 0, DK] = bo
        return o.reshape(NG * P, D)

    a = {"x": i["x"], "ctx": i["ctx_1024"], "tau": i["condB_tau"], "delta": i["fside_BxS2_0"], "pt": i["condB_pt"],
         "lens": i["_lenS2"]}
    for tag, pre in (("a0", "L0_xcond_"), ("a1", "L1_xcond_")):
        a[f"{tag}_wq"], a[f"{tag}_wk"] = i[pre + "Wq"].T[:, cols], i[pre + "Wk"].T[:, cols]
        a[f"{tag}_wv"], a[f"{tag}_bv"] = i[pre + "Wv"].T, i[pre + "bv"]
        a[f"{tag}_bq"], a[f"{tag}_bk"] = columns(i[pre + "bq"]), columns(i[pre + "bk"])
        a[f"{tag}_wo"] = out_rows(i[pre + "Wo"].T, i[pre + "bo"])
    heads = {n: i[f"L2_ffn_W{n}"].transpose(1, 0, 2).reshape(D, D) for n in "qkv"}
    a["a2_wq"], a["a2_wk"], a["a2_wv"] = heads["q"][:, cols], heads["k"][:, cols], heads["v"]
    a["a2_bq"] = a["a2_bk"] = np.zeros((P, DC), f32)
    a["a2_bv"] = np.zeros(D, f32)
    a["a2_wo"] = out_rows(np.eye(D, dtype=f32), np.zeros(D, f32))
    for tag, pre in (("l2", "L2_xcond_"), ("l3", "L3_xcond_")):
        a[f"{tag}_wa"], a[f"{tag}_wc"] = i[pre + "W_a"], i[pre + "W_c"].T
    a["router_w"], a["router_bias"] = i["L1_ffn_router_w"], i["L1_ffn_router_bias"]
    a["conv_w"] = i["L1_ffn_conv_w"].transpose(2, 1, 0).reshape(KS1, DC, P, I1).transpose(2, 0, 1, 3)
    a["shared_up"], a["shared_down"] = i["L1_ffn_shared_up_w"], i["L1_ffn_shared_down_w"]
    a["gate_w"], a["up_w"], a["down_w"] = (i[f"L1_ffn_expert_{n}_w"] for n in ("gate", "up", "down"))
    a["gate2"], a["gate3"] = i["L2_ffn_gate_W"], i["L3_ffn_gate_w"].T
    for tag, pre, names in (("m2", "L2_ffn_", ("W1", "b1", "W2", "b2")), ("m3", "L3_ffn_", ("w1", "b1", "w2", "b2"))):
        w1, b1, w2, b2 = (i[pre + n] for n in names)
        a[f"{tag}_w1"], a[f"{tag}_w2"], a[f"{tag}_b2"] = w1, w2, b2
        a[f"{tag}_b1"] = b1.reshape(E2, FC, P).transpose(2, 0, 1)
    a["ln0_g"], a["ln0_b"] = i["L0_ffn_ln_g"], i["L0_ffn_ln_b"]
    for n in ("ln1_g", "ln1_b", "ln2_g", "ln2_b"):
        a[n] = i["L2_ffn_" + n]
    return {n: np.ascontiguousarray(v) for n, v in a.items()}


def kernel(**inputs):
    import numpy as np
    import concourse.bacc as bacc
    from concourse.bass_utils import run_bass_kernel_spmd

    nc = bacc.Bacc("TRN2", target_bir_lowering=False, num_devices=1)
    arrays = {f"in_{n}": v for n, v in lay_out(inputs).items()}
    aps = {n[3:]: nc.dram_tensor(n, v.shape, mybir.dt.from_np(v.dtype), kind="ExternalInput").ap()
           for n, v in arrays.items()}
    aps["out"] = nc.dram_tensor("out_0", (B, S, D), F32, kind="ExternalOutput").ap()
    residual_stack(nc, aps)
    r = run_bass_kernel_spmd(nc, [arrays], core_ids=[0])
    return np.asarray(r.results[0]["out_0"])
```

```python
from contextlib import ExitStack, contextmanager

import concourse.bass as bass
from concourse import mybir

F32 = mybir.dt.float32
BF16 = mybir.dt.bfloat16
I32 = mybir.dt.int32
U32 = mybir.dt.uint32
ALU = mybir.AluOpType
ACT = mybir.ActivationFunctionType
AX_X = mybir.AxisListType.X

P = 128
B, S, D = 4, 512, 256
NT = S // P
DC = D // P
H, DK = 16, 16
HG = 4
NG = H // HG
HP = 32
PAIRS = ((0, 0), (0, 1), (0, 2), (1, 0), (1, 1), (2, 0))
ROW_DELTA = DK * len(PAIRS)
ROW_MAX = ROW_DELTA + 3
ROWS = ROW_MAX + 2
PAD = 2
EPS = 1e-5
LOWEST = -3.0e38
E1, I1, KS1 = 16, 128, 3
E2, FF = 8, 1024
FC = FF // P
CAPACITY = -(-5 * B * S // (4 * E2))
TOKENS = B * S
BLOCK = 2 * P
BLOCKS = (2 * TOKENS + E2 * (BLOCK - 1)) // BLOCK
SPARE = E2 * TOKENS
SLOTS2 = SPARE + BLOCKS * BLOCK
DROPPED = E2 * CAPACITY
WINDOW, DEV_POW, MASKED = 16.0, 128.0, -1000000000.0


@contextmanager
def Stage(nc, tag, sems, buffers=(), pool_dma=False):
    with ExitStack() as ctx:
        signals = {s: ctx.enter_context(nc.semaphore(f"{tag}_{s}")) for s in sems.split()}
        tiles = {name: ctx.enter_context(nc.sbuf_tensor(f"{tag}_{name}", shape, dt)) for name, shape, dt in buffers}
        with nc.Block() as block:
            yield block, {**signals, **tiles}
        numbers = [s.num for s in signals.values()]
        if pool_dma:
            nc.gpsimd.dma_reset(range(min(numbers), max(numbers) + 1))
        nc.all_engine_barrier(sems_to_clear=range(min(numbers), max(numbers) + 1))


def linker(engine, sem):
    count = [0]

    def link(ins):
        count[0] += 1
        ins.then_inc(sem, 1)
        engine.wait_ge(sem, count[0])
    return link


def inverse_root(nc, link, out, var, half, scratch, guess):
    v = nc.vector
    link(v.tensor_scalar(half, var, EPS, None, ALU.add))
    link(v.tensor_scalar(guess, half.bitcast(I32), 1, None, ALU.arith_shift_right))
    link(v.tensor_scalar(out.bitcast(I32), guess, -1.0, float(0x5F3759DF), ALU.mult, ALU.add))
    link(v.tensor_scalar(half, half, -0.5, None, ALU.mult))
    for _ in range(3):
        link(v.tensor_tensor(scratch, out, out, ALU.mult))
        link(v.tensor_tensor(scratch, scratch, half, ALU.mult))
        link(v.scalar_tensor_tensor(out, scratch, 1.5, out, ALU.add, ALU.mult))


def moments(nc, link, src, st, mv):
    for t in range(NT):
        ins = nc.vector.bn_stats(st[:, t, :], src[:, t, :])
    link(ins)
    for t in range(NT):
        ins = nc.vector.bn_aggr(mv[:, t, :], st[:, t, :])
    link(ins)


STAT_BUFFERS = (("st", [P, NT, 6], F32), ("mv", [P, NT, 2], F32), ("rs", [P, NT], F32), ("half", [P, NT], F32),
                ("scr", [P, NT], F32), ("guess", [P, NT], I32))


NORM_SEMS = "step normed nturned nt_out "


def norm_on_vector(nc, m, link, k):
    moments(nc, link, m.x, k["st"], k["mv"])
    inverse_root(nc, link, k["rs"][:], k["mv"][:, :, 1], k["half"][:], k["scr"][:], k["guess"][:])
    for t in range(NT):
        nc.vector.tensor_scalar(m.n[:, t, :], m.x[:, t, :], k["mv"][:, t, 0:1], k["rs"][:, t:t + 1],
                                ALU.subtract, ALU.mult).then_inc(k["normed"], 1)


def norm_on_tensor(nc, m, pe, k):
    for t in range(NT):
        pe.wait_ge(k["normed"], t + 1)
        for c in range(DC):
            ins = nc.tensor.transpose(m.ps[:, c, t * P:(t + 1) * P], m.n[:, t, c * P:(c + 1) * P], m.ident[:])
    ins.then_inc(k["nturned"], 1)


def norm_on_scalar(nc, m, act, k):
    act.wait_ge(k["nturned"], 1)
    for c in range(DC):
        nc.scalar.activation(m.nt[:, c, PAD:PAD + S], m.ps[:, c, :], ACT.Copy).then_inc(k["nt_out"], 1)


def affine_norm(nc, link, src, dst, gain, shift, k):
    moments(nc, link, src, k["st"], k["mv"])
    inverse_root(nc, link, k["rs"][:], k["mv"][:, :, 1], k["half"][:], k["scr"][:], k["guess"][:])
    for t in range(NT):
        ins = nc.vector.tensor_scalar(dst[:, t, :], src[:, t, :], k["mv"][:, t, 0:1], k["rs"][:, t:t + 1],
                                      ALU.subtract, ALU.mult)
    link(ins)
    for t in range(NT):
        ins = nc.vector.tensor_tensor(dst[:, t, :], dst[:, t, :], gain, ALU.mult)
    link(ins)
    for t in range(NT):
        ins = nc.vector.tensor_tensor(dst[:, t, :], dst[:, t, :], shift, ALU.add)
    link(ins)


def double_norm(nc, m, dve, link, k, gain):
    moments(nc, link, m.x, k["st"], k["mv"])
    inverse_root(nc, link, k["rs"][:], k["mv"][:, :, 1], k["half"][:], k["scr"][:], k["guess"][:])
    link(nc.vector.tensor_tensor(k["var2"][:], k["rs"][:], k["rs"][:], ALU.mult))
    link(nc.vector.tensor_tensor(k["var2"][:], k["var2"][:], k["mv"][:, :, 1], ALU.mult))
    inverse_root(nc, link, k["rs2"][:], k["var2"][:], k["half"][:], k["scr"][:], k["guess"][:])
    link(nc.vector.tensor_tensor(k["rs2"][:], k["rs2"][:], k["rs"][:], ALU.mult))
    for t in range(NT):
        ins = nc.vector.tensor_scalar(m.n[:, t, :], m.x[:, t, :], k["mv"][:, t, 0:1], k["rs2"][:, t:t + 1],
                                      ALU.subtract, ALU.mult)
    link(ins)
    link(nc.vector.tensor_tensor(m.n[:], m.n[:], gain.unsqueeze(1).to_broadcast([P, NT, D]), ALU.mult))
    dve.wait_ge(k["shifted"], 1)
    link(nc.vector.tensor_tensor(m.x[:], m.y[:], m.n[:], ALU.add))


ATTENTION_BUFFERS = (
    ("qs", [P, H, S], BF16), ("ks", [P, H, S], BF16), ("v", [P, NT, H, HP], F32),
    ("ot", [P, NG, S], F32), ("on", [P, NG, S], F32),
    ("qp", [P, 3, DC, S], BF16), ("kp", [P, 3, DC, S], BF16),
    ("probs", [P, 3, 2, S], F32), ("recip", [P, S], F32),
    ("mx", [P, NG, NT, HG], F32), ("mxd", [P, NG, NT, HG], F32), ("m1", [P, NT, HG], BF16),
    ("mp", [P, NT, 2, HG], F32), ("mt", [2 * HG, 2, S], BF16), ("diag", [P, 2, P], F32),
    ("tq", [P, 1], F32), ("bqs", [P, DC], F32), ("rs2", [P, NT], F32), ("var2", [P, NT], F32),
) + STAT_BUFFERS


def attention_stage(nc, m, tag, w, source, causal, doubled=None):
    first = [(g, t, j) for g in range(NG) for t in range(NT) for j in range(HG)]
    second = [(g, t, j) for g in range(NG) for t in range(NT) for j in (0, 2)]
    per_group = NT * HG // 2
    LAG = HG * NT + 6
    BANK_M, BANK_O, BANK_P = 2, 3, 4

    def order():
        out, s = [], 0
        for u in range(len(first) + LAG + 2):
            if u < len(first):
                out.append(("max", u))
                if u % (HG * NT) == HG * NT - 1:
                    out.append(("turn", u // (HG * NT)))
            while s < len(second) and (2 * s + LAG <= u or u >= len(first)):
                out.append(("score", s))
                if s >= 1:
                    out.append(("value", s - 1))
                    if (s - 1) % per_group == per_group - 1:
                        out.append(("spread", (s - 1) // per_group))
                s += 1
        out.append(("value", len(second) - 1))
        out.append(("spread", NG - 1))
        turns = [o for o in out if o[0] == "turn"]
        for t in turns:
            at = out.index(t)
            out.remove(t)
            out.insert(min(at + 3, len(out)), t)
        for t in [o for o in out if o[0] == "spread"]:
            at = out.index(t)
            out.remove(t)
            out.insert(min(at + 2, len(out)), t)
        return out

    ORDER = order()
    misc = [o for o in ORDER if o[0] in ("turn", "spread")]
    sems = NORM_SEMS + (
        "projq projk projv qfull kfull qrest krest v_out scaled qsplit ksplit fixed repk0 repk1 repq0 repq1 maxed "
        "maxdone turned turn_out mrow scored exped masked valued o_out spread recips divided proj gstep ready shifted")
    with Stage(nc, tag, sems, ATTENTION_BUFFERS) as (block, k):
        qf, kf = k["ot"][:, 0:DC, :], k["ot"][:, DC:2 * DC, :]
        qrest, krest = k["on"][:, 0:DC, :], k["on"][:, DC:2 * DC, :]
        kc = source
        koff = PAD if causal else 0

        @block.sync
        def _(sp):
            for dst, src in ((k["qs"][ROW_DELTA:ROW_MAX], m.quarter_rows), (k["ks"][ROW_MAX:ROWS], m.one_rows),
                             (k["ks"][ROW_DELTA:ROW_MAX], m.zero_rows if causal else m.delta_rows)):
                sp.dma_start(dst, src[:].unsqueeze(1).to_broadcast([dst.shape[0], H, S])).then_inc(k["fixed"], 16)
            kside = (k["kp"], k["kfull"], k["ksplit"], k["ks"], (k["repk0"], k["repk1"]), 1)
            qside = (k["qp"], k["qfull"], k["qsplit"], k["qs"], (k["repq0"], k["repq1"]), 0)
            for (part, full, split, dst, rep, side), c in (
                    ((kside, 0), (qside, 0), (kside, 1), (qside, 1)) if causal else
                    ((kside, 0), (kside, 1), (qside, 0), (qside, 1))):
                for p in range(3):
                    if p == 0:
                        sp.wait_ge(full, 2 * c + 2)
                    else:
                        sp.wait_ge(split, 2 * c + p)
                    for n, pair in enumerate(PAIRS):
                        if pair[side] == p:
                            heads = slice(c * H // DC, (c + 1) * H // DC)
                            sp.dma_start(dst[n * DK:(n + 1) * DK, heads].rearrange("i h s -> i (h s)"),
                                         part[:, p, c]).then_inc(rep[c], 16)
            for g in range(NG):
                sp.wait_ge(k["turn_out"], g + 1)
                sp.dma_start(k["qs"][ROW_MAX:ROWS, g * HG:(g + 1) * HG, :], k["mt"][:, g % 2, :]).then_inc(k["mrow"], 16)
            sp.wait_ge(k["mrow"], 16 * NG)

        @block.tensor
        def _(pe):
            def project(signal, bank, weight, src, off, c):
                for i in range(DC):
                    if src is m.nt:
                        pe.wait_ge(k["nt_out"], i + 1)
                    ins = nc.tensor.matmul(m.ps[:, bank + c, :], weight[:, i, c * P:(c + 1) * P],
                                           src[:, i, off:off + S], start=(i == 0), stop=(i == DC - 1))
                ins.then_inc(signal, 1)

            def project_v():
                for t in range(NT):
                    for i in range(DC):
                        ins = nc.tensor.matmul(m.ps[:, 4 + t, 0:D], kc[:, i, koff + t * P:koff + (t + 1) * P],
                                               w.v[:, i, :], start=(i == 0), stop=(i == DC - 1))
                    ins.then_inc(k["projv"], 1)

            if causal:
                norm_on_tensor(nc, m, pe, k)
                for c in range(DC):
                    project(k["projk"], 2, w.k, kc, koff, c)
                    project(k["projq"], 0, w.q, m.nt, PAD, c)
                project_v()
            else:
                for c in range(DC):
                    project(k["projk"], 2, w.k, kc, koff, c)
                project_v()
                norm_on_tensor(nc, m, pe, k)
                for c in range(DC):
                    project(k["projq"], 0, w.q, m.nt, PAD, c)
            pe.wait_ge(k["kfull"], 2 * DC)
            pe.wait_ge(k["qfull"], 2 * DC)
            pe.wait_ge(k["fixed"], 48)
            misc_used = 0
            for what, u in ORDER:
                if what == "max":
                    g, t, j = first[u]
                    h = g * HG + j
                    if (t, j) == (0, 0) and g % 2 == 0:
                        pe.wait_ge((k["repk0"], k["repk1"])[g // 2], 16 * len(PAIRS))
                        pe.wait_ge((k["repq0"], k["repq1"])[g // 2], 16 * len(PAIRS))
                    if u >= 2:
                        pe.wait_ge(k["maxed"], u - 1)
                    n = (t + 1) * P if causal else S
                    nc.tensor.matmul(m.ps[:, u % 2, 0:n], k["qs"][0:ROW_MAX, h, t * P:(t + 1) * P],
                                     k["ks"][0:ROW_MAX, h, 0:n], start=True, stop=True).then_inc(k["scored"], 1)
                elif what == "turn":
                    pe.wait_ge(k["maxdone"], u + 1)
                    if misc_used:
                        last, n = misc[misc_used - 1]
                        pe.wait_ge(k["turn_out"] if last == "turn" else k["recips"], n + 1)
                    misc_used += 1
                    for t in range(NT):
                        ins = nc.tensor.transpose(m.ps[0:2 * HG, BANK_M, t * P:(t + 1) * P],
                                                  k["mp"][:, t].rearrange("p a j -> p (a j)"), m.ident[:])
                    ins.then_inc(k["turned"], 1)
                elif what == "score":
                    g, t, j = second[u]
                    if u == 0:
                        pe.wait_ge(k["v_out"], NT)
                        pe.wait_ge(k["ready"], 1)
                    if u % per_group == 0:
                        pe.wait_ge(k["mrow"], 16 * (g + 1))
                    if u >= 2:
                        pe.wait_ge(k["exped"], u - 1)
                    q0 = t * P if causal else 0
                    for i in range(2):
                        h = g * HG + j + i
                        ins = nc.tensor.matmul(m.ps[:, BANK_P + 2 * (u % 2) + i, q0:S],
                                               k["ks"][0:ROWS, h, t * P:(t + 1) * P], k["qs"][0:ROWS, h, q0:S],
                                               start=True, stop=True)
                    ins.then_inc(k["proj"], 1)
                elif what == "value":
                    g, t, j = second[u]
                    if causal:
                        pe.wait_ge(k["masked"], u + 1)
                    else:
                        pe.wait_ge(k["exped"], u + 1)
                    if t == 0 and g >= 1:
                        pe.wait_ge(k["o_out"], g)
                    q0 = t * P if causal else 0
                    for i in range(2):
                        ins = nc.tensor.matmul(m.ps[HP * (j + i):HP * (j + i + 1), BANK_O, q0:S],
                                               k["v"][:, t, g * HG + j + i, :], k["probs"][:, u % 3, i, q0:S],
                                               start=(t == 0), stop=(t == NT - 1))
                    ins.then_inc(k["valued"], 1)
                else:
                    pe.wait_ge(k["o_out"], u + 1)
                    if misc_used:
                        last, n = misc[misc_used - 1]
                        pe.wait_ge(k["turn_out"] if last == "turn" else k["recips"], n + 1)
                    misc_used += 1
                    nc.tensor.matmul(m.ps[:, BANK_M, :], m.spread[:], k["ot"][:, u, :], start=True,
                                     stop=True).then_inc(k["spread"], 1)
            pe.wait_ge(k["exped"], len(second))
            for g in range(NG):
                pe.wait_ge(k["divided"], g + 1)
                for t in range(NT):
                    ins = nc.tensor.matmul(m.ps[:, 4 + t, 0:D], k["on"][:, g, t * P:(t + 1) * P], w.o[:, g, :],
                                           start=(g == 0), stop=(g == NG - 1))
                    if g == NG - 1:
                        ins.then_inc(k["proj"], 1)

        @block.scalar
        def _(act):
            def take_k(c):
                act.wait_ge(k["projk"], c + 1)
                nc.scalar.activation(kf[:, c, :], m.ps[:, 2 + c, :], ACT.Identity,
                                     bias=w.bk[:, c:c + 1]).then_inc(k["kfull"], 1)
                nc.scalar.activation(k["kp"][:, 0, c], m.ps[:, 2 + c, :], ACT.Identity,
                                     bias=w.bk[:, c:c + 1]).then_inc(k["kfull"], 1)

            def take_q(c):
                act.wait_ge(k["projq"], c + 1)
                for dst in (qf[:, c, :], k["qp"][:, 0, c]):
                    nc.scalar.activation(dst, m.ps[:, c, :], ACT.Identity, bias=k["bqs"][:, c:c + 1],
                                         scale=k["tq"][:, 0:1]).then_inc(k["qfull"], 1)

            act.wait_ge(k["scaled"], 1)
            if causal:
                norm_on_scalar(nc, m, act, k)
                for c in range(DC):
                    take_k(c)
                    take_q(c)
            else:
                for c in range(DC):
                    take_k(c)
                norm_on_scalar(nc, m, act, k)
                for c in range(DC):
                    take_q(c)
            for what, u in ORDER:
                if what == "turn":
                    act.wait_ge(k["turned"], u + 1)
                    if u >= 2:
                        act.wait_ge(k["mrow"], 16 * (u - 1))
                    nc.scalar.activation(k["mt"][:, u % 2, :], m.ps[0:2 * HG, BANK_M, :], ACT.Copy)\
                        .then_inc(k["turn_out"], 1)
                elif what == "score":
                    g, t, j = second[u]
                    act.wait_ge(k["proj"], u + 1)
                    if u >= 3:
                        act.wait_ge(k["valued"], u - 2)
                    q0 = t * P if causal else 0
                    b = BANK_P + 2 * (u % 2)
                    nc.scalar.activation(k["probs"][:, u % 3, :, q0:S], m.ps[:, b:b + 2, q0:S], ACT.Exp)\
                        .then_inc(k["exped"], 1)
                elif what == "value" and u % per_group == per_group - 1:
                    g = u // per_group
                    act.wait_ge(k["valued"], u + 1)
                    nc.scalar.activation(k["ot"][:, g, :], m.ps[:, BANK_O, :], ACT.Copy).then_inc(k["o_out"], 1)

        @block.vector
        def _(dve):
            link = linker(dve, k["step"])
            if causal:
                nc.vector.memset(k["tq"][:], 1.0 / 16.0)
                link(nc.vector.memset(k["mx"][:], LOWEST))
            else:
                link(nc.vector.tensor_scalar(k["tq"][:], m.tau[:], 0.25, None, ALU.mult))
            nc.vector.tensor_scalar(k["bqs"][:], w.bq[:], k["tq"][:, 0:1], None, ALU.mult).then_inc(k["scaled"], 1)
            if doubled is not None:
                double_norm(nc, m, dve, link, k, doubled[0])
            norm_on_vector(nc, m, link, k)

            def take_v():
                dve.wait_ge(k["ready"], 1)
                for t in range(NT):
                    dve.wait_ge(k["projv"], t + 1)
                    nc.vector.tensor_tensor(
                        k["v"][:, t, :, 0:DK], m.ps[:, 4 + t, 0:D].rearrange("p (h i) -> p h i", h=H),
                        w.bv[:].rearrange("p (h i) -> p h i", h=H), ALU.add).then_inc(k["v_out"], 1)

            if not causal:
                take_v()
            for c in range(DC):
                dve.wait_ge(k["qfull"], 2 * c + 2)
                nc.vector.tensor_tensor(qrest[:, c], qf[:, c], k["qp"][:, 0, c], ALU.subtract).then_inc(k["qrest"], 1)
                dve.wait_ge(k["qrest"], c + 1)
                nc.vector.tensor_copy(k["qp"][:, 1, c], qrest[:, c]).then_inc(k["qsplit"], 1)
                dve.wait_ge(k["qsplit"], 2 * c + 1)
                nc.vector.tensor_tensor(k["qp"][:, 2, c], qrest[:, c], k["qp"][:, 1, c], ALU.subtract)\
                    .then_inc(k["qsplit"], 1)
            if causal:
                take_v()

            def split_maxima(g):
                if causal:
                    link(nc.vector.tensor_tensor(k["mx"][:, g], k["mx"][:, g], k["mxd"][:, g], ALU.max))
                link(nc.vector.tensor_scalar(k["m1"][:], k["mx"][:, g], -1.0, None, ALU.mult))
                if g >= 1:
                    dve.wait_ge(k["turned"], g)
                nc.vector.tensor_copy(k["mp"][:, :, 0, :], k["m1"][:])
                nc.vector.scalar_tensor_tensor(k["mp"][:, :, 1, :], k["mx"][:, g], -1.0, k["m1"][:], ALU.mult, ALU.subtract)\
                    .then_inc(k["maxdone"], 1)

            for what, u in ORDER:
                if what == "max":
                    g, t, j = first[u]
                    dve.wait_ge(k["scored"], u + 1)
                    if causal:
                        if t:
                            nc.vector.tensor_reduce(k["mx"][:, g, t, j:j + 1], m.ps[:, u % 2, 0:t * P], AX_X, ALU.max)
                        if u >= 2:
                            dve.wait_ge(k["maxed"], u - 1)
                        ins = nc.vector.tensor_tensor_reduce(
                            out=k["diag"][:, u % 2, :], in0=m.ps[:, u % 2, t * P:(t + 1) * P], in1=m.later[:], scale=1.0,
                            scalar=LOWEST, op0=ALU.add, op1=ALU.max, accum_out=k["mxd"][:, g, t, j:j + 1])
                    else:
                        ins = nc.vector.tensor_reduce(k["mx"][:, g, t, j:j + 1], m.ps[:, u % 2, :], AX_X, ALU.max)
                    ins.then_inc(k["maxed"], 1)
                    if u % (HG * NT) == HG * NT - 1:
                        dve.wait_ge(k["maxed"], u + 1)
                        split_maxima(g)
                elif what == "spread":
                    dve.wait_ge(k["spread"], u + 1)
                    if u >= 1:
                        dve.wait_ge(k["divided"], u)
                    nc.vector.reciprocal(k["recip"][:], m.ps[:, BANK_M, :]).then_inc(k["recips"], 1)
            for t in range(NT):
                dve.wait_ge(k["proj"], len(second) + t + 1)
                if causal:
                    nc.vector.tensor_copy(m.y[:, t, :], m.ps[:, 4 + t, 0:D])
                else:
                    nc.vector.tensor_tensor(m.x[:, t, :], m.x[:, t, :], m.ps[:, 4 + t, 0:D], ALU.add)

        @block.gpsimd
        def _(pool):
            link = linker(pool, k["gstep"])
            link(nc.gpsimd.memset(k["v"][:, :, :, DK:HP], 0.0))
            nc.gpsimd.memset(k["v"][:, :, :, DK:DK + 1], 1.0).then_inc(k["ready"], 1)
            if doubled is not None:
                for t in range(NT):
                    ins = nc.gpsimd.tensor_tensor(m.y[:, t, :], m.x[:, t, :], doubled[1], ALU.add)
                ins.then_inc(k["shifted"], 1)
            for c in range(DC):
                pool.wait_ge(k["kfull"], 2 * c + 2)
                nc.gpsimd.tensor_tensor(krest[:, c], kf[:, c], k["kp"][:, 0, c], ALU.subtract).then_inc(k["krest"], 1)
                pool.wait_ge(k["krest"], c + 1)
                nc.gpsimd.tensor_copy(k["kp"][:, 1, c], krest[:, c]).then_inc(k["ksplit"], 1)
                pool.wait_ge(k["ksplit"], 2 * c + 1)
                nc.gpsimd.tensor_tensor(k["kp"][:, 2, c], krest[:, c], k["kp"][:, 1, c], ALU.subtract)\
                    .then_inc(k["ksplit"], 1)
            for what, u in ORDER:
                if what == "score" and causal:
                    g, t, j = second[u]
                    pool.wait_ge(k["exped"], u + 1)
                    blk = k["probs"][:, u % 3, :, t * P:(t + 1) * P]
                    nc.gpsimd.affine_select(out=blk, in_=blk, compare_op=ALU.is_ge, fill=0.0, base=0,
                                            pattern=[[0, 2], [1, P]], channel_multiplier=-1).then_inc(k["masked"], 1)
                elif what == "spread":
                    pool.wait_ge(k["recips"], u + 1)
                    nc.gpsimd.tensor_tensor(k["on"][:, u, :], k["ot"][:, u, :], k["recip"][:], ALU.mult)\
                        .then_inc(k["divided"], 1)


def batch_stage(nc, m, tag, b, x_in, ctx_in, tau, delta, lens, pt):
    bufs = (("drow", [1, S], F32), ("drest", [1, S], F32), ("dparts", [1, 3, S], BF16), ("len_i", [P, 1], I32),
            ("end", [P, 2], F32), ("start", [P, 1], F32), ("dist", [P, S], F32), ("off", [P, S], F32))
    with Stage(nc, tag + "load", "xin cin small turned step sent squared", bufs) as (block, k):
        @block.sync
        def _(sp):
            sp.dma_start(k["drow"][:], delta[bass.ds(b, 1), :]).then_inc(k["small"], 16)
            for dst, src in ((m.tau, tau), (m.pt, pt), (k["len_i"], lens)):
                sp.dma_start(dst[:], src.rearrange("(n a) -> n a", a=1)[bass.ds(b, 1), :].partition_broadcast(P))\
                    .then_inc(k["small"], 16)
            sp.wait_ge(k["step"], 4)
            sp.dma_start(m.delta_rows[:, :], k["dparts"][:].rearrange("a r s -> a (r s)")).then_inc(k["sent"], 16)
            sp.wait_ge(k["sent"], 16)

        @block.scalar
        def _(act):
            act.dma_start(m.x[:], batch_rows(x_in, b)).then_inc(k["xin"], 16)
            act.dma_start(m.c[:], ctx_in[bass.ds(b, 1)].rearrange("o (t p) d -> p (o t) d", p=P)).then_inc(k["cin"], 16)
            act.wait_ge(k["turned"], 1)
            nc.scalar.activation(m.ct[:], m.ps[:, 0:DC, :], ACT.Copy)
            act.wait_ge(k["squared"], 1)
            nc.scalar.activation(m.gauss[:], k["off"][:], ACT.Exp, scale=-1.0 / DEV_POW)
            act.wait_ge(k["xin"], 16)

        @block.tensor
        def _(pe):
            pe.wait_ge(k["cin"], 16)
            for t in range(NT):
                for c in range(DC):
                    ins = nc.tensor.transpose(m.ps[:, c, t * P:(t + 1) * P], m.c[:, t, c * P:(c + 1) * P], m.ident[:])
            ins.then_inc(k["turned"], 1)

        @block.vector
        def _(dve):
            link = linker(dve, k["step"])
            dve.wait_ge(k["small"], 64)
            link(nc.vector.tensor_copy(k["dparts"][:, 0], k["drow"][:]))
            link(nc.vector.tensor_tensor(k["drest"][:], k["drow"][:], k["dparts"][:, 0], ALU.subtract))
            link(nc.vector.tensor_copy(k["dparts"][:, 1], k["drest"][:]))
            link(nc.vector.tensor_tensor(k["dparts"][:, 2], k["drest"][:], k["dparts"][:, 1], ALU.subtract))
            link(nc.vector.tensor_copy(m.len_f[:], k["len_i"][:]))
            link(nc.vector.tensor_scalar(k["start"][:], m.pt[:], WINDOW, 0.0, ALU.subtract, ALU.max))
            link(nc.vector.tensor_scalar(k["end"][:, 0:1], m.pt[:], WINDOW, None, ALU.add))
            link(nc.vector.tensor_tensor(k["end"][:, 1:2], k["end"][:, 0:1], m.len_f[:], ALU.min))
            link(nc.vector.tensor_scalar(k["off"][:], m.index[:], k["start"][:, 0:1], None, ALU.is_lt))
            link(nc.vector.tensor_scalar(k["dist"][:], m.index[:], k["end"][:, 1:2], None, ALU.is_gt))
            link(nc.vector.tensor_tensor(k["off"][:], k["off"][:], k["dist"][:], ALU.max))
            nc.vector.tensor_scalar(m.keep[:], k["off"][:], -1.0, 1.0, ALU.mult, ALU.add)
            nc.vector.tensor_scalar(m.big[:], k["off"][:], MASKED, None, ALU.mult)
            link(nc.vector.tensor_scalar(k["dist"][:], m.index[:], m.pt[:, 0:1], None, ALU.subtract))
            nc.vector.tensor_tensor(k["off"][:], k["dist"][:], k["dist"][:], ALU.mult).then_inc(k["squared"], 1)


def location_stage(nc, m, tag, w):
    bufs = STAT_BUFFERS + (("qa", [P, DC, S], F32), ("sc", [P, NT, S], F32), ("mx", [P, NT], F32), ("nmx", [P, NT], F32),
            ("sums", [P, NT], F32), ("rsum", [P, NT], F32), ("al", [P, NT, S], F32), ("alt", [P, NT, S], F32),
            ("cx", [P, DC, S], F32), ("th", [P, NT, D], F32))
    sems = NORM_SEMS + "proj proj_out scored maxed exped weighed turned turned_out ctx ctx_out outp tanhed"
    with Stage(nc, tag, sems, bufs) as (block, k):
        @block.tensor
        def _(pe):
            norm_on_tensor(nc, m, pe, k)
            for c in range(DC):
                for i in range(DC):
                    pe.wait_ge(k["nt_out"], i + 1)
                    ins = nc.tensor.matmul(m.ps[:, 2 + c, :], w.a[:, i, c * P:(c + 1) * P], m.nt[:, i, PAD:PAD + S],
                                           start=(i == 0), stop=(i == DC - 1))
                ins.then_inc(k["proj"], 1)
            pe.wait_ge(k["proj_out"], DC)
            for t in range(NT):
                for c in range(DC):
                    ins = nc.tensor.matmul(m.ps[:, 4 + t, :], k["qa"][:, c, t * P:(t + 1) * P], m.ct[:, c, :],
                                           start=(c == 0), stop=(c == DC - 1))
                ins.then_inc(k["scored"], 1)
            for t in range(NT):
                pe.wait_ge(k["weighed"], t + 1)
                for n in range(NT):
                    ins = nc.tensor.transpose(m.ps[:, t, n * P:(n + 1) * P], k["al"][:, t, n * P:(n + 1) * P], m.ident[:])
                ins.then_inc(k["turned"], 1)
            pe.wait_ge(k["turned_out"], NT)
            for c in range(DC):
                for n in range(NT):
                    ins = nc.tensor.matmul(m.ps[:, 4 + c, :], m.c[:, n, c * P:(c + 1) * P], k["alt"][:, n, :],
                                           start=(n == 0), stop=(n == NT - 1))
                ins.then_inc(k["ctx"], 1)
            pe.wait_ge(k["ctx_out"], DC)
            for t in range(NT):
                for n in range(2 * DC):
                    lhs = k["cx"][:, n, t * P:(t + 1) * P] if n < DC else \
                        m.nt[:, n - DC, PAD + t * P:PAD + (t + 1) * P]
                    ins = nc.tensor.matmul(m.ps[:, t, 0:D], lhs, w.c[:, n, :], start=(n == 0), stop=(n == 2 * DC - 1))
                ins.then_inc(k["outp"], 1)

        @block.scalar
        def _(act):
            norm_on_scalar(nc, m, act, k)
            for c in range(DC):
                act.wait_ge(k["proj"], c + 1)
                nc.scalar.activation(k["qa"][:, c, :], m.ps[:, 2 + c, :], ACT.Copy).then_inc(k["proj_out"], 1)
            for t in range(NT):
                act.wait_ge(k["maxed"], t + 1)
                nc.scalar.activation(k["al"][:, t, :], k["sc"][:, t, :], ACT.Exp, bias=k["nmx"][:, t:t + 1],
                                     accum_out=k["sums"][:, t:t + 1]).then_inc(k["exped"], 1)
            for t in range(NT):
                act.wait_ge(k["turned"], t + 1)
                nc.scalar.activation(k["alt"][:, :, t * P:(t + 1) * P],
                                     m.ps[:, t, :].rearrange("p (n q) -> p n q", n=NT), ACT.Copy)\
                    .then_inc(k["turned_out"], 1)
            for c in range(DC):
                act.wait_ge(k["ctx"], c + 1)
                nc.scalar.activation(k["cx"][:, c, :], m.ps[:, 4 + c, :], ACT.Copy).then_inc(k["ctx_out"], 1)
            for t in range(NT):
                act.wait_ge(k["outp"], t + 1)
                nc.scalar.activation(k["th"][:, t, :], m.ps[:, t, 0:D], ACT.Tanh).then_inc(k["tanhed"], 1)

        @block.vector
        def _(dve):
            link = linker(dve, k["step"])
            norm_on_vector(nc, m, link, k)
            for t in range(NT):
                dve.wait_ge(k["scored"], t + 1)
                link(nc.vector.tensor_tensor(k["sc"][:, t, :], m.ps[:, 4 + t, :], m.keep[:], ALU.mult))
                link(nc.vector.tensor_tensor(k["sc"][:, t, :], k["sc"][:, t, :], m.big[:], ALU.add))
                nc.vector.tensor_reduce(k["nmx"][:, t:t + 1], k["sc"][:, t, :], AX_X, ALU.max, negate=True)\
                    .then_inc(k["maxed"], 1)
            for t in range(NT):
                dve.wait_ge(k["exped"], t + 1)
                link(nc.vector.reciprocal(k["rsum"][:, t:t + 1], k["sums"][:, t:t + 1]))
                nc.vector.scalar_tensor_tensor(k["al"][:, t, :], k["al"][:, t, :], k["rsum"][:, t:t + 1], m.gauss[:],
                                               ALU.mult, ALU.mult).then_inc(k["weighed"], 1)
            for t in range(NT):
                dve.wait_ge(k["tanhed"], t + 1)
                nc.vector.tensor_tensor(m.x[:, t, :], m.x[:, t, :], k["th"][:, t, :], ALU.add)


ROUTE_BUFFERS = (("lg", [P, NT, E1], F32), ("pr", [P, NT, E1], F32), ("rmx", [P, NT], F32), ("rsm", [P, NT], F32),
                 ("top", [P, NT, 8], F32), ("idx", [P, NT, 8], U32), ("idf", [P, NT, 8], F32), ("wt", [P, NT, 2], F32),
                 ("oh", [P, NT, E1], F32))


def spread_over(ap, n):
    return ap.unsqueeze(2).to_broadcast([P, NT, n])


def softmax_steps(nc, dve, link, k, n):
    lg, pr = k["lg"][:, :, 0:n], k["pr"][:, :, 0:n]
    link(nc.vector.tensor_reduce(k["rmx"][:], lg, AX_X, ALU.max))
    nc.vector.tensor_tensor(lg, lg, spread_over(k["rmx"][:], n), ALU.subtract).then_inc(k["logits"], 1)
    dve.wait_ge(k["rexp"], 1)
    link(nc.vector.tensor_reduce(k["rsm"][:], pr, AX_X, ALU.add))
    link(nc.vector.reciprocal(k["rsm"][:], k["rsm"][:]))
    link(nc.vector.tensor_tensor(pr, pr, spread_over(k["rsm"][:], n), ALU.mult))


def top_steps(nc, link, k, values, n):
    for t in range(NT):
        ins = nc.vector.max(k["top"][:, t, :], values[:, t, 0:n])
    link(ins)
    for t in range(NT):
        ins = nc.vector.max_index(k["idx"][:, t, :], k["top"][:, t, :], values[:, t, 0:n])
    link(ins)
    link(nc.vector.tensor_copy(k["idf"][:], k["idx"][:]))


def one_hot(nc, m, link, k, out, choice, n):
    link(nc.vector.tensor_tensor(out, m.columns[:, :, 0:n], k["idf"][:, :, choice:choice + 1].to_broadcast([P, NT, n]),
                                 ALU.is_equal))


def combine_steps(nc, m, link, k, n):
    comb, oh = m.comb[:, :, 0:n], k["oh"][:, :, 0:n]
    one_hot(nc, m, link, k, comb, 0, n)
    one_hot(nc, m, link, k, oh, 1, n)
    link(nc.vector.tensor_tensor(comb, comb, k["wt"][:, :, 0:1].to_broadcast([P, NT, n]), ALU.mult))
    link(nc.vector.tensor_tensor(oh, oh, k["wt"][:, :, 1:2].to_broadcast([P, NT, n]), ALU.mult))
    link(nc.vector.tensor_tensor(comb, comb, oh, ALU.add))


def logits_on_pe(nc, m, k, src, off, weight, n):
    for t in range(NT):
        for i in range(DC):
            ins = nc.tensor.matmul(m.ps[:, 0, t * E1:t * E1 + n], src[:, i, off + t * P:off + (t + 1) * P],
                                   weight[:, i, :], start=(i == 0), stop=(i == DC - 1))
    ins.then_inc(k["routed"], 1)


def psum_logits(m, n):
    return m.ps[:, 0, 0:NT * E1].rearrange("p (t e) -> p t e", t=NT)[:, :, 0:n]


def conv_mixture_stage(nc, m, w, gate_w, up_w, down_w):
    RING = 3
    bufs = ROUTE_BUFFERS + STAT_BUFFERS + (("wg", [P, RING, DC, I1], F32), ("wu", [P, RING, DC, I1], F32), ("wd", [P, RING, D], F32),
                            ("th", [P, 2, S], F32), ("ga", [P, 2, S], F32), ("hid", [P, 2, S], F32),
                            ("ssum", [P, NT], F32))
    EXPERTS = E1 - 1
    units = EXPERTS + 1
    sems = NORM_SEMS + "routed logits rexp wload0 wload1 wload2 gated tanhed hidden down added"
    with Stage(nc, "cmix", sems, bufs) as (block, k):
        wload = (k["wload0"], k["wload1"], k["wload2"])
        @block.sync
        def _(sp):
            for e in range(EXPERTS):
                if e >= RING:
                    sp.wait_ge(k["down"], e - RING + 2)
                r = e % RING
                sp.dma_start(k["wg"][:, r], gate_w[e].rearrange("(c p) i -> p c i", p=P)).then_inc(wload[r], 16)
                sp.dma_start(k["wu"][:, r], up_w[e].rearrange("(c p) i -> p c i", p=P)).then_inc(wload[r], 16)
                sp.dma_start(k["wd"][:, r], down_w[e]).then_inc(wload[r], 16)

        @block.tensor
        def _(pe):
            norm_on_tensor(nc, m, pe, k)
            pe.wait_ge(k["nt_out"], DC)
            logits_on_pe(nc, m, k, m.nt, PAD, w.router, E1)

            def down(u):
                pe.wait_ge(k["hidden"], u + 1)
                if u >= 1:
                    pe.wait_ge(k["added"], u)
                for t in range(NT):
                    ins = nc.tensor.matmul(m.ps[:, 5 + t // 2, (t % 2) * D:(t % 2 + 1) * D],
                                           k["hid"][:, u % 2, t * P:(t + 1) * P],
                                           w.sdown[:] if u == 0 else k["wd"][:, (u - 1) % RING, :], start=True, stop=True)
                ins.then_inc(k["down"], 1)

            for u in range(units):
                gate, up = m.ps[:, 1 + 2 * (u % 2), :], m.ps[:, 2 + 2 * (u % 2), :]
                if u >= 2:
                    pe.wait_ge(k["hidden"], u - 1)
                if u == 0:
                    n = 0
                    for tap in range(KS1):
                        for i in range(DC):
                            nc.tensor.matmul(gate, w.conv[:, tap, i, :], m.nt[:, i, tap:tap + S], start=(n == 0),
                                             stop=(n == KS1 * DC - 1))
                            n += 1
                    for i in range(DC):
                        ins = nc.tensor.matmul(up, w.sup[:, i, :], m.nt[:, i, PAD:PAD + S], start=(i == 0),
                                               stop=(i == DC - 1))
                else:
                    r = (u - 1) % RING
                    pe.wait_ge(wload[r], 48 * ((u - 1) // RING + 1))
                    for bank, wt in ((gate, k["wg"]), (up, k["wu"])):
                        for i in range(DC):
                            ins = nc.tensor.matmul(bank, wt[:, r, i, :], m.nt[:, i, PAD:PAD + S], start=(i == 0),
                                                   stop=(i == DC - 1))
                ins.then_inc(k["gated"], 1)
                if u >= 1:
                    down(u - 1)
            down(units - 1)

        @block.scalar
        def _(act):
            norm_on_scalar(nc, m, act, k)
            act.wait_ge(k["logits"], 1)
            nc.scalar.activation(k["pr"][:], k["lg"][:], ACT.Exp).then_inc(k["rexp"], 1)
            for u in range(units):
                act.wait_ge(k["gated"], u + 1)
                if u >= 2:
                    act.wait_ge(k["hidden"], u - 1)
                nc.scalar.activation(k["th"][:, u % 2, :], m.ps[:, 1 + 2 * (u % 2), :], ACT.Tanh, scale=0.5)\
                    .then_inc(k["tanhed"], 1)

        @block.vector
        def _(dve):
            link = linker(dve, k["step"])
            norm_on_vector(nc, m, link, k)
            dve.wait_ge(k["routed"], 1)
            link(nc.vector.tensor_tensor(k["lg"][:], psum_logits(m, E1),
                                         w.rbias[:].unsqueeze(1).to_broadcast([P, NT, E1]), ALU.add))
            softmax_steps(nc, dve, link, k, E1)
            top_steps(nc, link, k, k["pr"], E1)
            link(nc.vector.tensor_tensor(k["ssum"][:], k["top"][:, :, 0], k["top"][:, :, 1], ALU.add))
            link(nc.vector.tensor_scalar(k["ssum"][:], k["ssum"][:], 1e-6, None, ALU.add))
            link(nc.vector.reciprocal(k["ssum"][:], k["ssum"][:]))
            link(nc.vector.tensor_tensor(k["wt"][:], k["top"][:, :, 0:2], spread_over(k["ssum"][:], 2), ALU.mult))
            combine_steps(nc, m, link, k, E1)
            for t in range(NT):
                ins = nc.vector.scalar_tensor_tensor(m.x[:, t, :], m.n[:, t, :], m.comb[:, t, EXPERTS:E1],
                                                     m.x[:, t, :], ALU.mult, ALU.add)
            link(ins)

            def add(u):
                dve.wait_ge(k["down"], u + 1)
                for t in range(NT):
                    y = m.ps[:, 5 + t // 2, (t % 2) * D:(t % 2 + 1) * D]
                    if u == 0:
                        ins = nc.vector.tensor_tensor(m.x[:, t, :], m.x[:, t, :], y, ALU.add)
                    else:
                        ins = nc.vector.scalar_tensor_tensor(m.x[:, t, :], y, m.comb[:, t, u - 1:u], m.x[:, t, :],
                                                             ALU.mult, ALU.add)
                ins.then_inc(k["added"], 1)

            for u in range(units):
                dve.wait_ge(k["tanhed"], u + 1)
                gate, up = m.ps[:, 1 + 2 * (u % 2), :], m.ps[:, 2 + 2 * (u % 2), :]
                link(nc.vector.scalar_tensor_tensor(k["ga"][:, u % 2, :], k["th"][:, u % 2, :], 1.0, gate, ALU.add, ALU.mult))
                if u >= 2:
                    dve.wait_ge(k["down"], u - 1)
                nc.vector.scalar_tensor_tensor(k["hid"][:, u % 2, :], k["ga"][:, u % 2, :], 0.5, up, ALU.mult, ALU.mult)\
                    .then_inc(k["hidden"], 1)
                if u >= 1:
                    add(u - 1)
                    if u >= 1:
                        dve.wait_ge(k["added"], u)
            add(units - 1)


RANK_BUFFERS = (("hot", [P, NT, E2], F32), ("taken", [P, NT, E2], F32), ("place", [P, NT, E2], F32),
                ("slots", [P, NT, 2], F32), ("slots_i", [P, NT, 2], I32))


def ranks_on_pe(nc, m, k, hot):
    for t in range(NT):
        for n in range(t + 1):
            nc.tensor.matmul(m.ps[:, 1, t * E2:(t + 1) * E2], m.earlier[:] if n == t else m.ones[:],
                             hot[:, n, :], start=(n == 0), stop=(n == t))
    for n in range(NT):
        ins = nc.tensor.matmul(m.ps[:, 1, NT * E2:(NT + 1) * E2], m.ones[:], hot[:, n, :],
                               start=(n == 0), stop=(n == NT - 1))
    ins.then_inc(k["ranked"], 1)


def rank_sums(nc, m, link, k, used):
    ranks = m.ps[:, 1, 0:NT * E2].rearrange("p (t e) -> p t e", t=NT)
    link(nc.vector.tensor_tensor(k["place"][:], ranks, used[:].unsqueeze(1).to_broadcast([P, NT, E2]), ALU.add))
    link(nc.vector.tensor_tensor(used[:], used[:], m.ps[:, 1, NT * E2:(NT + 1) * E2], ALU.add))


def pair_route_stage(nc, m, w, b, tokens, residual, table):
    bufs = ROUTE_BUFFERS + STAT_BUFFERS + RANK_BUFFERS + (
        ("an", [P, NT, D], F32), ("dl", [P, NT], F32), ("de", [P, NT], F32), ("ids", [P, NT], I32))
    sems = "step normed turned turned_out routed logits rexp picked ranked slotted stored kept_x copied"
    with Stage(nc, "proute", sems, bufs, True) as (block, k):
        @block.vector
        def _(dve):
            link = linker(dve, k["step"])
            affine_norm(nc, link, m.y, k["an"], m.ln1_g[:], m.ln1_b[:], k)
            for t in range(NT):
                ins = nc.vector.tensor_tensor(m.y[:, t, :], k["an"][:, t, :], m.n[:, t, :], ALU.add)
            ins.then_inc(k["normed"], 1)
            link(nc.vector.tensor_copy(k["ids"][:], m.token_ids[:, bass.ds(b * NT, NT)]))
            dve.wait_ge(k["routed"], 1)
            link(nc.vector.tensor_copy(k["lg"][:, :, 0:E2], psum_logits(m, E2)))
            top_steps(nc, link, k, k["lg"], E2)
            nc.vector.tensor_tensor(k["dl"][:], k["top"][:, :, 1], k["top"][:, :, 0], ALU.subtract)\
                .then_inc(k["logits"], 1)
            one_hot(nc, m, link, k, k["oh"][:, :, 0:E2], 0, E2)
            one_hot(nc, m, link, k, k["hot"][:], 1, E2)
            nc.vector.tensor_tensor(k["taken"][:], k["oh"][:, :, 0:E2], k["hot"][:], ALU.add)\
                .then_inc(k["picked"], 1)
            dve.wait_ge(k["rexp"], 1)
            link(nc.vector.tensor_scalar(k["dl"][:], k["de"][:], 1.0, None, ALU.add))
            link(nc.vector.reciprocal(k["wt"][:, :, 0], k["dl"][:]))
            link(nc.vector.tensor_tensor(k["wt"][:, :, 1], k["de"][:], k["wt"][:, :, 0], ALU.mult))
            nc.vector.tensor_copy(m.pair_weights[:, bass.ds(b * NT, NT), :], k["wt"][:])
            dve.wait_ge(k["ranked"], 1)
            rank_sums(nc, m, link, k, m.used2)
            link(nc.vector.tensor_tensor(k["place"][:], k["place"][:], m.first_slots[:], ALU.add))
            link(nc.vector.tensor_tensor(k["oh"][:, :, 0:E2], k["oh"][:, :, 0:E2], k["place"][:], ALU.mult))
            link(nc.vector.tensor_tensor(k["hot"][:], k["hot"][:], k["place"][:], ALU.mult))
            link(nc.vector.tensor_reduce(k["slots"][:, :, 0], k["oh"][:, :, 0:E2], AX_X, ALU.add))
            link(nc.vector.tensor_reduce(k["slots"][:, :, 1], k["hot"][:], AX_X, ALU.add))
            nc.vector.tensor_copy(k["slots_i"][:], k["slots"][:]).then_inc(k["slotted"], 1)
            nc.vector.tensor_copy(m.pair_slots[:, bass.ds(b * NT, NT), :], k["slots"][:])
            nc.vector.tensor_copy(m.pair_experts[:, bass.ds(b * NT, NT), :], k["idf"][:, :, 0:2])

        @block.tensor
        def _(pe):
            pe.wait_ge(k["normed"], 1)
            for t in range(NT):
                for c in range(DC):
                    ins = nc.tensor.transpose(m.ps[:, 2 + c, t * P:(t + 1) * P], m.y[:, t, c * P:(c + 1) * P],
                                              m.ident[:])
            ins.then_inc(k["turned"], 1)
            pe.wait_ge(k["turned_out"], 1)
            logits_on_pe(nc, m, k, m.nt, PAD, w.gate2, E2)
            pe.wait_ge(k["picked"], 1)
            ranks_on_pe(nc, m, k, k["taken"])

        @block.scalar
        def _(act):
            act.wait_ge(k["turned"], 1)
            nc.scalar.activation(m.nt[:, :, PAD:PAD + S], m.ps[:, 2:2 + DC, :], ACT.Copy).then_inc(k["turned_out"], 1)
            act.wait_ge(k["logits"], 1)
            nc.scalar.activation(k["de"][:], k["dl"][:], ACT.Exp).then_inc(k["rexp"], 1)

        @block.sync
        def _(sp):
            sp.dma_start(batch_rows(residual, b), m.x[:]).then_inc(k["kept_x"], 16)
            sp.wait_ge(k["normed"], 1)
            sp.dma_start(batch_rows(tokens, b), m.y[:]).then_inc(k["copied"], 16)
            sp.wait_ge(k["kept_x"], 16)
            sp.wait_ge(k["copied"], 16)

        @block.gpsimd
        def _(pool):
            pool.wait_ge(k["slotted"], 1)
            for t in range(NT):
                for c in range(2):
                    nc.gpsimd.indirect_dma_start(
                        out=table[:, :], out_offset=bass.IndirectOffsetOnAxis(ap=k["slots_i"][:, t, c:c + 1], axis=0),
                        in_=k["ids"][:, t:t + 1], in_offset=None).then_inc(k["stored"], 16)
            pool.wait_ge(k["stored"], 16 * 2 * NT)


def batch_rows(dram, b):
    return dram[bass.ds(b * S, S), :].rearrange("(t p) d -> p t d", p=P)


def single_route_stage(nc, m, w, b, tokens, residual, table):
    bufs = ROUTE_BUFFERS + STAT_BUFFERS + RANK_BUFFERS + (("kept", [P, NT, E2], F32), ("room", [P, NT], F32), ("ids", [P, NT], I32),
                                           ("idf3", [P, NT], F32), ("back", [P, NT], F32))
    with Stage(nc, "sroute", NORM_SEMS + "routed logits rexp picked ranked slotted stored kept_x copied", bufs,
               True) as (block, k):
        @block.tensor
        def _(pe):
            norm_on_tensor(nc, m, pe, k)
            pe.wait_ge(k["nt_out"], DC)
            logits_on_pe(nc, m, k, m.nt, PAD, w.gate3, E2)
            pe.wait_ge(k["picked"], 1)
            ranks_on_pe(nc, m, k, k["hot"])

        @block.scalar
        def _(act):
            norm_on_scalar(nc, m, act, k)
            act.wait_ge(k["logits"], 1)
            nc.scalar.activation(k["pr"][:, :, 0:E2], k["lg"][:, :, 0:E2], ACT.Exp).then_inc(k["rexp"], 1)

        @block.sync
        def _(sp):
            sp.dma_start(batch_rows(residual, b), m.x[:]).then_inc(k["kept_x"], 16)
            sp.wait_ge(k["normed"], NT)
            sp.dma_start(batch_rows(tokens, b), m.n[:]).then_inc(k["copied"], 16)
            sp.wait_ge(k["kept_x"], 16)
            sp.wait_ge(k["copied"], 16)

        @block.vector
        def _(dve):
            link = linker(dve, k["step"])
            link(nc.vector.tensor_copy(k["ids"][:], m.token_ids[:, bass.ds(b * NT, NT)]))
            link(nc.vector.tensor_copy(k["idf3"][:], k["ids"][:]))
            norm_on_vector(nc, m, link, k)
            dve.wait_ge(k["routed"], 1)
            link(nc.vector.tensor_copy(k["lg"][:, :, 0:E2], psum_logits(m, E2)))
            softmax_steps(nc, dve, link, k, E2)
            top_steps(nc, link, k, k["pr"], E2)
            one_hot(nc, m, link, k, k["oh"][:, :, 0:E2], 0, E2)
            nc.vector.tensor_copy(k["hot"][:], k["oh"][:, :, 0:E2]).then_inc(k["picked"], 1)
            dve.wait_ge(k["ranked"], 1)
            rank_sums(nc, m, link, k, m.used3)
            link(nc.vector.tensor_scalar(k["kept"][:], k["place"][:], float(CAPACITY), None, ALU.is_le))
            link(nc.vector.tensor_tensor(k["kept"][:], k["kept"][:], k["oh"][:, :, 0:E2], ALU.mult))
            link(nc.vector.tensor_reduce(k["room"][:], k["kept"][:], AX_X, ALU.add))
            link(nc.vector.tensor_tensor(m.one_weight[:, bass.ds(b * NT, NT)], k["top"][:, :, 0], k["room"][:],
                                         ALU.mult))
            link(nc.vector.tensor_tensor(k["place"][:], k["place"][:], m.first_slots3[:], ALU.add))
            link(nc.vector.tensor_tensor(k["place"][:], k["place"][:], k["kept"][:], ALU.mult))
            link(nc.vector.tensor_reduce(k["back"][:], k["place"][:], AX_X, ALU.add))
            link(nc.vector.tensor_scalar(m.one_slot[:, bass.ds(b * NT, NT)], k["back"][:], float(DROPPED), None,
                                         ALU.add))
            link(nc.vector.tensor_scalar(k["room"][:], k["room"][:], -1.0, 1.0, ALU.mult, ALU.add))
            link(nc.vector.tensor_tensor(k["idf3"][:], k["idf3"][:], k["room"][:], ALU.mult))
            link(nc.vector.tensor_tensor(k["back"][:], k["back"][:], k["idf3"][:], ALU.add))
            nc.vector.tensor_scalar(k["slots_i"][:, :, 0], k["back"][:], float(DROPPED), None, ALU.add)\
                .then_inc(k["slotted"], 1)

        @block.gpsimd
        def _(pool):
            pool.wait_ge(k["slotted"], 1)
            for t in range(NT):
                nc.gpsimd.indirect_dma_start(
                    out=table[:, :], out_offset=bass.IndirectOffsetOnAxis(ap=k["slots_i"][:, t, 0:1], axis=0),
                    in_=k["ids"][:, t:t + 1], in_offset=None).then_inc(k["stored"], 16)
            pool.wait_ge(k["stored"], 16 * NT)


def schedule_stage(nc, m):
    choices = B * NT * 2
    bufs = (("count_i", [P, E2], I32), ("blocks", [P, E2], F32), ("grid", [P, E2, E2], F32), ("ends", [P, E2], F32),
            ("move", [P, E2], F32), ("past", [P, BLOCKS, E2], F32), ("start", [P, BLOCKS, E2], F32),
            ("first", [P, BLOCKS], F32), ("expert", [P, BLOCKS], F32), ("slot", [P, BLOCKS], F32),
            ("number", [P, BLOCKS, E2], F32), ("upto", [P, E2, E2], F32), ("column", [P, choices, E2], F32),
            ("hot", [P, choices, E2], F32), ("moved", [P, choices], F32))
    shift = BLOCK.bit_length() - 1
    with Stage(nc, "sched", "step zeroed made", bufs) as (block, k):
        @block.gpsimd
        def _(pool):
            nc.gpsimd.memset(k["upto"][:], 1.0).then_inc(k["zeroed"], 1)
            nc.gpsimd.iota(k["number"][:], pattern=[[1, BLOCKS], [0, E2]], base=0, channel_multiplier=0,
                           allow_small_or_imprecise_dtypes=True).then_inc(k["made"], 1)
            nc.gpsimd.iota(k["column"][:], pattern=[[0, choices], [1, E2]], base=0, channel_multiplier=0,
                           allow_small_or_imprecise_dtypes=True).then_inc(k["made"], 1)
            pool.wait_ge(k["zeroed"], 1)
            nc.gpsimd.affine_select(out=k["upto"][:], in_=k["upto"][:], compare_op=ALU.is_ge, fill=0.0, base=0,
                                    pattern=[[1, E2], [-1, E2]], channel_multiplier=0).then_inc(k["made"], 1)

        @block.vector
        def _(dve):
            link = linker(dve, k["step"])

            def over(ap, n):
                return ap.unsqueeze(1).to_broadcast([P, n, E2])

            link(nc.vector.tensor_scalar(k["count_i"][:], m.used2[:], float(BLOCK - 1), None, ALU.add))
            link(nc.vector.tensor_scalar(k["count_i"][:], k["count_i"][:], shift, None, ALU.arith_shift_right))
            link(nc.vector.tensor_copy(k["blocks"][:], k["count_i"][:]))
            dve.wait_ge(k["made"], 3)
            link(nc.vector.tensor_tensor(k["grid"][:], k["upto"][:], over(k["blocks"][:], E2), ALU.mult))
            link(nc.vector.tensor_reduce(k["ends"][:], k["grid"][:], AX_X, ALU.add))
            link(nc.vector.tensor_tensor(k["past"][:], k["number"][:], over(k["ends"][:], BLOCKS), ALU.is_ge))
            link(nc.vector.tensor_reduce(k["expert"][:], k["past"][:], AX_X, ALU.add))
            link(nc.vector.tensor_tensor(k["start"][:], k["past"][:], over(k["blocks"][:], BLOCKS), ALU.mult))
            link(nc.vector.tensor_reduce(k["first"][:], k["start"][:], AX_X, ALU.add))
            link(nc.vector.tensor_tensor(k["first"][:], k["number"][:, :, 0], k["first"][:], ALU.subtract))
            link(nc.vector.tensor_scalar(k["first"][:], k["first"][:], float(BLOCK), None, ALU.mult))
            link(nc.vector.tensor_scalar(k["slot"][:], k["expert"][:], float(TOKENS), None, ALU.mult))
            nc.vector.tensor_tensor(m.block_slot[:], k["slot"][0:1], k["first"][0:1], ALU.add)
            nc.vector.tensor_scalar(m.block_expert[:], k["expert"][0:1], float(E2 - 1), None, ALU.min)
            link(nc.vector.tensor_tensor(k["move"][:], k["ends"][:], k["blocks"][:], ALU.subtract))
            link(nc.vector.tensor_scalar(k["move"][:], k["move"][:], float(BLOCK), None, ALU.mult))
            link(nc.vector.scalar_tensor_tensor(k["move"][:], k["column"][:, 0, :], -float(TOKENS), k["move"][:],
                                                ALU.mult, ALU.add))
            experts = m.pair_experts[:].rearrange("p t c -> p (t c)")
            link(nc.vector.tensor_tensor(k["hot"][:], k["column"][:],
                                         experts.unsqueeze(2).to_broadcast([P, choices, E2]), ALU.is_equal))
            link(nc.vector.tensor_tensor(k["hot"][:], k["hot"][:], over(k["move"][:], choices), ALU.mult))
            link(nc.vector.tensor_reduce(k["moved"][:], k["hot"][:], AX_X, ALU.add))
            nc.vector.tensor_tensor(m.pair_rows[:].rearrange("p t c -> p (t c)"), k["moved"][:],
                                    m.pair_slots[:].rearrange("p t c -> p (t c)"), ALU.add)


def sparse_mixture_stage(nc, m, tag, tiles, blocks, place, tokens, table, results, w1, b1, w2, b2):
    rows = sum(tiles)
    nt = len(tiles)
    starts = [sum(tiles[:t]) for t in range(nt)]
    RX, RO = 3, 4
    bufs = (("w1", [P, 2, DC, FF], F32), ("w2", [P, 2, FC, D], F32), ("b1", [P, 2, FC], F32), ("b2", [P, 2, D], F32),
            ("ids", [P, RX, nt], I32), ("xg", [P, RX, nt, D], F32), ("xt", [P, 2, DC, rows], F32),
            ("hidden", [P, 2, FC, rows], F32), ("res", [P, RO, D], F32))
    sems = ("ids0 ids1 ids2 xg0 xg1 xg2 wa0 wa1 wb0 wb1 st0 st1 st2 st3 turned xt_out chunk relu outs added")
    units = [(i, t) for i in range(blocks) for t in range(nt)]
    with Stage(nc, tag, sems, bufs, True) as (block, k):
        ids_in, x_in = [k[f"ids{r}"] for r in range(RX)], [k[f"xg{r}"] for r in range(RX)]
        first_in, second_in = (k["wa0"], k["wa1"]), (k["wb0"], k["wb1"])
        stored = [k[f"st{r}"] for r in range(RO)]

        @block.gpsimd
        def _(pool):
            def load_ids(i):
                slot = place(pool, i, "slot")
                for t in range(nt):
                    pool.dma_start(k["ids"][0:tiles[t], i % RX, t:t + 1],
                                   table[bass.ds(slot + starts[t], tiles[t]), :]).then_inc(ids_in[i % RX], 16)

            load_ids(0)
            for i in range(blocks):
                if i + 1 < blocks:
                    if i + 1 >= RX:
                        pool.wait_ge(x_in[(i + 1) % RX], 16 * nt * ((i + 1) // RX))
                    load_ids(i + 1)
                pool.wait_ge(ids_in[i % RX], 16 * nt * (i // RX + 1))
                if i >= RX:
                    pool.wait_ge(k["turned"], i - RX + 1)
                for t in range(nt):
                    nc.gpsimd.indirect_dma_start(
                        out=k["xg"][0:tiles[t], i % RX, t, :], out_offset=None, in_=tokens[:, :],
                        in_offset=bass.IndirectOffsetOnAxis(ap=k["ids"][0:tiles[t], i % RX, t:t + 1], axis=0))\
                        .then_inc(x_in[i % RX], 16)

        @block.sync
        def _(sp):
            def load_weights(i):
                e = place(sp, i, "expert")
                one = bass.ds(e, 1)
                if i >= 2:
                    sp.wait_ge(k["chunk"], FC * (i - 1))
                    sp.wait_ge(k["relu"], FC * (i - 1))
                sp.dma_start(k["w1"][:, i % 2], w1[one].rearrange("o (c p) f -> p (o c) f", p=P))\
                    .then_inc(first_in[i % 2], 16)
                sp.dma_start(k["b1"][:, i % 2], b1[one].rearrange("o p f -> p (o f)")).then_inc(first_in[i % 2], 16)
                if i >= 2:
                    sp.wait_ge(k["outs"], nt * (i - 1))
                    sp.wait_ge(k["added"], nt * (i - 1))
                sp.dma_start(k["w2"][:, i % 2], w2[one].rearrange("o (c p) d -> p (o c) d", p=P))\
                    .then_inc(second_in[i % 2], 16)
                sp.dma_start(k["b2"][:, i % 2], b2[one, :].partition_broadcast(P)).then_inc(second_in[i % 2], 16)

            def store(i):
                for t in range(nt):
                    u = i * nt + t
                    sp.wait_ge(k["added"], u + 1)
                    sp.dma_start(results[i * rows + starts[t]:i * rows + starts[t] + tiles[t], :], k["res"][0:tiles[t], u % RO, :])\
                        .then_inc(stored[u % RO], 16)

            load_weights(0)
            for i in range(blocks):
                if i + 1 < blocks:
                    load_weights(i + 1)
                store(i)
            for r in range(RO):
                sp.wait_ge(stored[r], 16 * len(range(r, len(units), RO)))

        @block.tensor
        def _(pe):
            def turn(i):
                pe.wait_ge(x_in[i % RX], 16 * nt * (i // RX + 1))
                if i >= 1:
                    pe.wait_ge(k["xt_out"], i)
                for t in range(nt):
                    for c in range(DC):
                        ins = nc.tensor.transpose(m.ps[:, c, starts[t]:starts[t] + tiles[t]],
                                                  k["xg"][0:tiles[t], i % RX, t, c * P:(c + 1) * P],
                                                  m.ident[0:tiles[t], 0:tiles[t]])
                ins.then_inc(k["turned"], 1)

            turn(0)
            for i in range(blocks):
                pe.wait_ge(k["xt_out"], i + 1)
                pe.wait_ge(first_in[i % 2], 32 * (i // 2 + 1))
                for f in range(FC):
                    n = i * FC + f
                    if n >= 4:
                        pe.wait_ge(k["relu"], n - 3)
                    for c in range(DC):
                        ins = nc.tensor.matmul(m.ps[:, 2 + n % 4, 0:rows], k["w1"][:, i % 2, c, f * P:(f + 1) * P],
                                               k["xt"][:, i % 2, c, :], start=(c == 0), stop=(c == DC - 1))
                    ins.then_inc(k["chunk"], 1)
                if i + 1 < blocks:
                    turn(i + 1)
                pe.wait_ge(k["relu"], FC * (i + 1))
                pe.wait_ge(second_in[i % 2], 32 * (i // 2 + 1))
                for t in range(nt):
                    u = i * nt + t
                    if u >= 2:
                        pe.wait_ge(k["added"], u - 1)
                    for f in range(FC):
                        ins = nc.tensor.matmul(m.ps[0:tiles[t], 6 + u % 2, 0:D],
                                               k["hidden"][:, i % 2, f, starts[t]:starts[t] + tiles[t]],
                                               k["w2"][:, i % 2, f, :], start=(f == 0), stop=(f == FC - 1))
                    ins.then_inc(k["outs"], 1)

        @block.scalar
        def _(act):
            for i in range(blocks):
                if i >= 2:
                    act.wait_ge(k["outs"], nt * (i - 1))
                for f in range(FC):
                    n = i * FC + f
                    act.wait_ge(k["chunk"], n + 1)
                    nc.scalar.activation(k["hidden"][:, i % 2, f, :], m.ps[:, 2 + n % 4, 0:rows], ACT.Relu,
                                         bias=k["b1"][:, i % 2, f:f + 1]).then_inc(k["relu"], 1)

        @block.vector
        def _(dve):
            def take_tokens(i):
                dve.wait_ge(k["turned"], i + 1)
                if i >= 2:
                    dve.wait_ge(k["chunk"], FC * (i - 1))
                nc.vector.tensor_copy(k["xt"][:, i % 2], m.ps[:, 0:DC, 0:rows]).then_inc(k["xt_out"], 1)

            take_tokens(0)
            for i in range(blocks):
                if i + 1 < blocks:
                    take_tokens(i + 1)
                for t in range(nt):
                    u = i * nt + t
                    dve.wait_ge(k["outs"], u + 1)
                    if u >= RO:
                        dve.wait_ge(stored[u % RO], 16 * (u // RO))
                    nc.vector.tensor_tensor(k["res"][0:tiles[t], u % RO, :], m.ps[0:tiles[t], 6 + u % 2, 0:D],
                                            k["b2"][0:tiles[t], i % 2, :], ALU.add).then_inc(k["added"], 1)


def gather_pair_stage(nc, m, b, results):
    bufs = (("slot", [P, NT, 2], I32), ("got", [P, NT, 2, D], F32), ("wt", [P, NT, 2], F32))
    with Stage(nc, "gather", "slots arrived step", bufs, True) as (block, k):
        @block.gpsimd
        def _(pool):
            pool.wait_ge(k["slots"], 1)
            for t in range(NT):
                for c in range(2):
                    nc.gpsimd.indirect_dma_start(
                        out=k["got"][:, t, c, :], out_offset=None, in_=results[:, :],
                        in_offset=bass.IndirectOffsetOnAxis(ap=k["slot"][:, t, c:c + 1], axis=0))\
                        .then_inc(k["arrived"], 16)

        @block.vector
        def _(dve):
            link = linker(dve, k["step"])
            nc.vector.tensor_copy(k["slot"][:], m.pair_rows[:, bass.ds(b * NT, NT), :]).then_inc(k["slots"], 1)
            link(nc.vector.tensor_copy(k["wt"][:], m.pair_weights[:, bass.ds(b * NT, NT), :]))
            dve.wait_ge(k["arrived"], 16 * 2 * NT)
            for t in range(NT):
                ins = nc.vector.tensor_scalar(m.y2[:, t, :], k["got"][:, t, 0, :], k["wt"][:, t, 0:1], None, ALU.mult)
            link(ins)
            for t in range(NT):
                nc.vector.scalar_tensor_tensor(m.y2[:, t, :], k["got"][:, t, 1, :], k["wt"][:, t, 1:2], m.y2[:, t, :],
                                               ALU.mult, ALU.add)


def finish_stage(nc, m, b, residual, results, out):
    bufs = (("slot", [P, NT], I32), ("got", [P, NT, D], F32), ("wt", [P, NT], F32))
    with Stage(nc, "finish", "xin slots arrived step summed stored", bufs, True) as (block, k):
        @block.sync
        def _(sp):
            sp.dma_start(m.x[:], batch_rows(residual, b)).then_inc(k["xin"], 16)
            sp.wait_ge(k["summed"], 1)
            sp.dma_start(batch_rows(out.rearrange("b s d -> (b s) d"), b), m.x[:]).then_inc(k["stored"], 16)
            sp.wait_ge(k["stored"], 16)

        @block.gpsimd
        def _(pool):
            pool.wait_ge(k["slots"], 1)
            for t in range(NT):
                nc.gpsimd.indirect_dma_start(
                    out=k["got"][:, t, :], out_offset=None, in_=results[:, :],
                    in_offset=bass.IndirectOffsetOnAxis(ap=k["slot"][:, t:t + 1], axis=0)).then_inc(k["arrived"], 16)

        @block.vector
        def _(dve):
            link = linker(dve, k["step"])
            nc.vector.tensor_copy(k["slot"][:], m.one_slot[:, bass.ds(b * NT, NT)]).then_inc(k["slots"], 1)
            link(nc.vector.tensor_copy(k["wt"][:], m.one_weight[:, bass.ds(b * NT, NT)]))
            dve.wait_ge(k["arrived"], 16 * NT)
            dve.wait_ge(k["xin"], 16)
            for t in range(NT):
                ins = nc.vector.scalar_tensor_tensor(m.x[:, t, :], k["got"][:, t, :], k["wt"][:, t:t + 1],
                                                     m.x[:, t, :], ALU.mult, ALU.add)
            ins.then_inc(k["summed"], 1)


def close_pair_stage(nc, m):
    with Stage(nc, "close2", "step", STAT_BUFFERS) as (block, k):
        @block.vector
        def _(dve):
            link = linker(dve, k["step"])
            affine_norm(nc, link, m.y2, m.y2, m.ln2_g[:], m.ln2_b[:], k)
            for t in range(NT):
                ins = nc.vector.tensor_tensor(m.y2[:, t, :], m.y2[:, t, :], m.y[:, t, :], ALU.add)
            link(ins)
            for t in range(NT):
                nc.vector.tensor_tensor(m.x[:, t, :], m.x[:, t, :], m.y2[:, t, :], ALU.add)


def reload_stage(nc, m, b, residual, tokens):
    with Stage(nc, "back", "arrived") as (block, k):
        @block.sync
        def _(sp):
            sp.dma_start(m.x[:], batch_rows(residual, b)).then_inc(k["arrived"], 16)
            sp.dma_start(m.y[:], batch_rows(tokens, b)).then_inc(k["arrived"], 16)
            sp.wait_ge(k["arrived"], 32)


def constant_stage(nc, m, loads, table2, table3, results3):
    wide = SLOTS2 // P
    with Stage(nc, "const", "loaded zeroed made blank filled", (("blank_i", [P, wide], I32),
                                                                ("blank_row", [1, D], F32))) as (block, k):
        @block.sync
        def _(sp):
            for dst, src in loads:
                sp.dma_start(dst, src).then_inc(k["loaded"], 16)
            sp.wait_ge(k["blank"], 1)
            sp.dma_start(table2.rearrange("(p n) o -> p (n o)", p=P), k["blank_i"][:]).then_inc(k["filled"], 16)
            sp.dma_start(table3[0:DROPPED, :].rearrange("(p n) o -> p (n o)", p=P), k["blank_i"][:, 0:DROPPED // P])\
                .then_inc(k["filled"], 16)
            sp.dma_start(results3[DROPPED:DROPPED + 1, :], k["blank_row"][:]).then_inc(k["filled"], 16)
            sp.wait_ge(k["filled"], 48)
            sp.wait_ge(k["loaded"], 16 * len(loads))

        @block.vector
        def _(dve):
            nc.vector.memset(m.ones[:], 1.0)
            nc.vector.memset(m.nt[:, :, 0:PAD], 0.0)
            nc.vector.memset(m.used2[:], 0.0)
            nc.vector.memset(m.used3[:], 0.0)
            nc.vector.memset(m.quarter_rows[:], 0.25)
            nc.vector.memset(m.one_rows[:], 1.0)
            nc.vector.memset(m.zero_rows[:], 0.0)
            nc.vector.memset(k["blank_row"][:], 0.0)
            nc.vector.memset(k["blank_i"][:], 0).then_inc(k["blank"], 1)

        @block.gpsimd
        def _(pool):
            g = nc.gpsimd
            for tile, value in ((m.ident, 0.0), (m.later, 0.0), (m.earlier, 1.0), (m.spread, 0.0)):
                ins = g.memset(tile[:], value)
            ins.then_inc(k["zeroed"], 1)
            pool.wait_ge(k["zeroed"], 1)
            g.affine_select(out=m.ident[:], in_=m.ident[:], compare_op=ALU.not_equal, fill=1.0, base=0,
                            pattern=[[-1, P]], channel_multiplier=1)
            g.affine_select(out=m.later[:], in_=m.later[:], compare_op=ALU.is_ge, fill=LOWEST, base=0,
                            pattern=[[-1, P]], channel_multiplier=1)
            g.affine_select(out=m.earlier[:], in_=m.earlier[:], compare_op=ALU.is_ge, fill=0.0, base=0,
                            pattern=[[1, P]], channel_multiplier=-1)
            view = m.spread[:].rearrange("p (j i) -> p j i", j=HG)
            g.affine_select(out=view, in_=view, compare_op=ALU.not_equal, fill=1.0, base=-DK,
                            pattern=[[-HP, HG], [0, HP]], channel_multiplier=1)
            g.iota(m.index[:], pattern=[[1, S]], base=0, channel_multiplier=0, allow_small_or_imprecise_dtypes=True)
            g.iota(m.token_ids[:], pattern=[[P, B * NT]], base=0, channel_multiplier=1)
            g.iota(m.first_slots[:], pattern=[[0, NT], [TOKENS, E2]], base=-1, channel_multiplier=0,
                   allow_small_or_imprecise_dtypes=True)
            g.iota(m.first_slots3[:], pattern=[[0, NT], [CAPACITY, E2]], base=-1 - DROPPED, channel_multiplier=0,
                   allow_small_or_imprecise_dtypes=True)
            g.iota(m.columns[:], pattern=[[0, NT], [1, E1]], base=0, channel_multiplier=0,
                   allow_small_or_imprecise_dtypes=True)


class Memory:

    def __init__(self, buffer):
        self.x = buffer("x", [P, NT, D], F32)
        self.n = buffer("n", [P, NT, D], F32)
        self.c = buffer("c", [P, NT, D], F32)
        self.y = buffer("y", [P, NT, D], F32)
        self.y2 = buffer("y2", [P, NT, D], F32)
        self.nt = buffer("nt", [P, DC, PAD + S], F32)
        self.ct = buffer("ct", [P, DC, S], F32)
        self.comb = buffer("comb", [P, NT, E1], F32)
        self.keep = buffer("keep", [P, S], F32)
        self.big = buffer("big", [P, S], F32)
        self.gauss = buffer("gauss", [P, S], F32)
        self.index = buffer("index", [P, S], F32)
        self.columns = buffer("columns", [P, NT, E1], F32)
        self.ident = buffer("ident", [P, P], F32)
        self.later = buffer("later", [P, P], F32)
        self.earlier = buffer("earlier", [P, P], F32)
        self.spread = buffer("spread", [P, P], F32)
        self.ones = buffer("ones", [P, P], F32)
        self.used2 = buffer("used2", [P, E2], F32)
        self.used3 = buffer("used3", [P, E2], F32)
        self.token_ids = buffer("token_ids", [P, B * NT], I32)
        self.first_slots = buffer("first_slots", [P, NT, E2], F32)
        self.first_slots3 = buffer("first_slots3", [P, NT, E2], F32)
        self.pair_weights = buffer("pair_weights", [P, B * NT, 2], F32)
        self.pair_slots = buffer("pair_slots", [P, B * NT, 2], F32)
        self.pair_experts = buffer("pair_experts", [P, B * NT, 2], F32)
        self.pair_rows = buffer("pair_rows", [P, B * NT, 2], I32)
        self.one_weight = buffer("one_weight", [P, B * NT], F32)
        self.one_slot = buffer("one_slot", [P, B * NT], I32)
        self.block_expert = buffer("block_expert", [1, BLOCKS], I32)
        self.block_slot = buffer("block_slot", [1, BLOCKS], I32)
        self.quarter_rows = buffer("quarter_rows", [3, S], BF16)
        self.one_rows = buffer("one_rows", [2, S], BF16)
        self.zero_rows = buffer("zero_rows", [3, S], BF16)
        self.delta_rows = buffer("delta_rows", [3, S], BF16)
        self.tau = buffer("tau", [P, 1], F32)
        self.pt = buffer("pt", [P, 1], F32)
        self.len_f = buffer("len_f", [P, 1], F32)
        self.ln0_g = buffer("ln0_g", [P, D], F32)
        self.ln0_b = buffer("ln0_b", [P, D], F32)
        self.ln1_g = buffer("ln1_g", [P, D], F32)
        self.ln1_b = buffer("ln1_b", [P, D], F32)
        self.ln2_g = buffer("ln2_g", [P, D], F32)
        self.ln2_b = buffer("ln2_b", [P, D], F32)


class Weights:
    pass


class AttentionWeights:

    def __init__(self, buffer, tag):
        self.q, self.k, self.v = (buffer(f"{tag}_w{n}", [P, DC, D], F32) for n in "qkv")
        self.o = buffer(f"{tag}_wo", [P, NG, D], F32)
        self.bq, self.bk = (buffer(f"{tag}_b{n}", [P, DC], F32) for n in "qk")
        self.bv = buffer(f"{tag}_bv", [P, D], F32)

    def loads(self, a, tag):
        chunks = "(c p) n -> p c n"
        return [(self.q[:], a[f"{tag}_wq"].rearrange(chunks, p=P)), (self.k[:], a[f"{tag}_wk"].rearrange(chunks, p=P)),
                (self.v[:], a[f"{tag}_wv"].rearrange(chunks, p=P)), (self.o[:], a[f"{tag}_wo"].rearrange(chunks, p=P)),
                (self.bq[:], a[f"{tag}_bq"]), (self.bk[:], a[f"{tag}_bk"]), (self.bv[:], row(a[f"{tag}_bv"]))]


def row(vector):
    return vector.rearrange("(a n) -> a n", a=1).partition_broadcast(P)


def residual_stack(nc, a):
    with ExitStack() as ctx:
        def buffer(name, shape, dt):
            return ctx.enter_context(nc.sbuf_tensor(name, shape, dt))

        m = Memory(buffer)
        m.ps = ctx.enter_context(nc.psum_tensor("banks", [P, 8, S], F32))
        w = Weights()
        attn = {tag: AttentionWeights(buffer, tag) for tag in ("a0", "a1", "a2")}
        loc = {}
        for tag in ("l2", "l3"):
            loc[tag] = Weights()
            loc[tag].a = buffer(f"{tag}_wa", [P, DC, D], F32)
            loc[tag].c = buffer(f"{tag}_wc", [P, 2 * DC, D], F32)
        w.router, w.rbias = buffer("w_router", [P, DC, E1], F32), buffer("w_rbias", [P, E1], F32)
        w.conv = buffer("w_conv", [P, KS1, DC, I1], F32)
        w.sup, w.sdown = buffer("w_sup", [P, DC, I1], F32), buffer("w_sdown", [P, D], F32)
        w.gate2, w.gate3 = buffer("w_gate2", [P, DC, E2], F32), buffer("w_gate3", [P, DC, E2], F32)

        chunks = "(c p) n -> p c n"
        loads = []
        for tag in attn:
            loads += attn[tag].loads(a, tag)
        for tag in loc:
            loads += [(loc[tag].a[:], a[f"{tag}_wa"].rearrange(chunks, p=P)),
                      (loc[tag].c[:], a[f"{tag}_wc"].rearrange(chunks, p=P))]
        loads += [(w.router[:], a["router_w"].rearrange(chunks, p=P)), (w.rbias[:], row(a["router_bias"])),
                  (w.conv[:], a["conv_w"]),
                  (w.sup[:], a["shared_up"].rearrange(chunks, p=P)), (w.sdown[:], a["shared_down"]),
                  (w.gate2[:], a["gate2"].rearrange(chunks, p=P)), (w.gate3[:], a["gate3"].rearrange(chunks, p=P))]
        loads += [(m.ln0_g[:], row(a["ln0_g"])), (m.ln0_b[:], row(a["ln0_b"])), (m.ln1_g[:], row(a["ln1_g"])),
                  (m.ln1_b[:], row(a["ln1_b"])), (m.ln2_g[:], row(a["ln2_g"])), (m.ln2_b[:], row(a["ln2_b"]))]
        residual = nc.dram_tensor("residual", [TOKENS, D], F32)
        tokens2 = nc.dram_tensor("tokens2", [TOKENS, D], F32)
        tokens3 = nc.dram_tensor("tokens3", [TOKENS, D], F32)
        table2 = nc.dram_tensor("table2", [SLOTS2, 1], I32)
        table3 = nc.dram_tensor("table3", [DROPPED + TOKENS, 1], I32)
        results2 = nc.dram_tensor("results2", [BLOCKS * BLOCK, D], F32)
        results3 = nc.dram_tensor("results3", [DROPPED + 1, D], F32)
        residual, tokens2, tokens3, table2, table3, results2, results3 = (
            t.ap() for t in (residual, tokens2, tokens3, table2, table3, results2, results3))
        constant_stage(nc, m, loads, table2, table3, results3)

        def pair_place(engine, i, what):
            if what == "expert":
                return engine.value_load(m.block_expert[0:1, i:i + 1], min_val=0, max_val=E2 - 1)
            return engine.value_load(m.block_slot[0:1, i:i + 1], min_val=0, max_val=SLOTS2 - BLOCK)

        def single_place(engine, i, what):
            return i if what == "expert" else i * CAPACITY

        x_rows = a["x"].rearrange("b s d -> (b s) d")
        with nc.Fori(0, B) as b:
            batch_stage(nc, m, "a", b, x_rows, a["ctx"], a["tau"], a["delta"], a["lens"], a["pt"])
            attention_stage(nc, m, "at0", attn["a0"], m.ct, False)
            attention_stage(nc, m, "at1", attn["a1"], m.ct, False, (m.ln0_g[:], m.ln0_b[:]))
            conv_mixture_stage(nc, m, w, a["gate_w"], a["up_w"], a["down_w"])
            location_stage(nc, m, "loc2", loc["l2"])
            attention_stage(nc, m, "at2", attn["a2"], m.nt, True)
            pair_route_stage(nc, m, w, b, tokens2, residual, table2)
        schedule_stage(nc, m)
        sparse_mixture_stage(nc, m, "mx2", (P, P), BLOCKS, pair_place, tokens2, table2, results2,
                             a["m2_w1"], a["m2_b1"], a["m2_w2"], a["m2_b2"])
        with nc.Fori(0, B) as b:
            batch_stage(nc, m, "c", b, residual, a["ctx"], a["tau"], a["delta"], a["lens"], a["pt"])
            reload_stage(nc, m, b, residual, tokens2)
            gather_pair_stage(nc, m, b, results2)
            close_pair_stage(nc, m)
            location_stage(nc, m, "loc3", loc["l3"])
            single_route_stage(nc, m, w, b, tokens3, residual, table3)
        sparse_mixture_stage(nc, m, "mx3", (P, P, CAPACITY - 2 * P), E2, single_place, tokens3, table3, results3,
                             a["m3_w1"], a["m3_b1"], a["m3_w2"], a["m3_b2"])
        with nc.Fori(0, B) as b:
            finish_stage(nc, m, b, residual, results3, a["out"])


def lay_out(inputs):
    import numpy as np
    i = {n: np.asarray(v) for n, v in inputs.items()}
    c, dim, head = np.meshgrid(np.arange(DC), np.arange(DK), np.arange(H // DC), indexing="ij")
    cols = ((c * H // DC + head) * DK + dim).reshape(-1)
    f32 = np.float32

    def columns(b):
        return b[cols].reshape(DC, P).T

    def out_rows(wo_t, bo):
        o = np.zeros((NG, HG, HP, D), f32)
        o[:, :, :DK] = wo_t.reshape(NG, HG, DK, D)
        o[0, 0, DK] = bo
        return o.reshape(NG * P, D)

    a = {"x": i["x"], "ctx": i["ctx_1024"], "tau": i["condB_tau"], "delta": i["fside_BxS2_0"], "pt": i["condB_pt"],
         "lens": i["_lenS2"]}
    for tag, pre in (("a0", "L0_xcond_"), ("a1", "L1_xcond_")):
        a[f"{tag}_wq"], a[f"{tag}_wk"] = i[pre + "Wq"].T[:, cols], i[pre + "Wk"].T[:, cols]
        a[f"{tag}_wv"], a[f"{tag}_bv"] = i[pre + "Wv"].T, i[pre + "bv"]
        a[f"{tag}_bq"], a[f"{tag}_bk"] = columns(i[pre + "bq"]), columns(i[pre + "bk"])
        a[f"{tag}_wo"] = out_rows(i[pre + "Wo"].T, i[pre + "bo"])
    heads = {n: i[f"L2_ffn_W{n}"].transpose(1, 0, 2).reshape(D, D) for n in "qkv"}
    a["a2_wq"], a["a2_wk"], a["a2_wv"] = heads["q"][:, cols], heads["k"][:, cols], heads["v"]
    a["a2_bq"] = a["a2_bk"] = np.zeros((P, DC), f32)
    a["a2_bv"] = np.zeros(D, f32)
    a["a2_wo"] = out_rows(np.eye(D, dtype=f32), np.zeros(D, f32))
    for tag, pre in (("l2", "L2_xcond_"), ("l3", "L3_xcond_")):
        a[f"{tag}_wa"], a[f"{tag}_wc"] = i[pre + "W_a"], i[pre + "W_c"].T
    a["router_w"], a["router_bias"] = i["L1_ffn_router_w"], i["L1_ffn_router_bias"]
    a["conv_w"] = i["L1_ffn_conv_w"].transpose(2, 1, 0).reshape(KS1, DC, P, I1).transpose(2, 0, 1, 3)
    a["shared_up"], a["shared_down"] = i["L1_ffn_shared_up_w"], i["L1_ffn_shared_down_w"]
    a["gate_w"], a["up_w"], a["down_w"] = (i[f"L1_ffn_expert_{n}_w"] for n in ("gate", "up", "down"))
    a["gate2"], a["gate3"] = i["L2_ffn_gate_W"], i["L3_ffn_gate_w"].T
    for tag, pre, names in (("m2", "L2_ffn_", ("W1", "b1", "W2", "b2")), ("m3", "L3_ffn_", ("w1", "b1", "w2", "b2"))):
        w1, b1, w2, b2 = (i[pre + n] for n in names)
        a[f"{tag}_w1"], a[f"{tag}_w2"], a[f"{tag}_b2"] = w1, w2, b2
        a[f"{tag}_b1"] = b1.reshape(E2, FC, P).transpose(0, 2, 1)
    a["ln0_g"], a["ln0_b"] = i["L0_ffn_ln_g"], i["L0_ffn_ln_b"]
    for n in ("ln1_g", "ln1_b", "ln2_g", "ln2_b"):
        a[n] = i["L2_ffn_" + n]
    return {n: np.ascontiguousarray(v) for n, v in a.items()}


def kernel(**inputs):
    import numpy as np
    import concourse.bacc as bacc
    from concourse.bass_utils import run_bass_kernel_spmd

    nc = bacc.Bacc("TRN2", target_bir_lowering=False, num_devices=1)
    arrays = {f"in_{n}": v for n, v in lay_out(inputs).items()}
    aps = {n[3:]: nc.dram_tensor(n, v.shape, mybir.dt.from_np(v.dtype), kind="ExternalInput").ap()
           for n, v in arrays.items()}
    aps["out"] = nc.dram_tensor("out_0", (B, S, D), F32, kind="ExternalOutput").ap()
    residual_stack(nc, aps)
    r = run_bass_kernel_spmd(nc, [arrays], core_ids=[0])
    return np.asarray(r.results[0]["out_0"])
```

```python
from contextlib import ExitStack, contextmanager

import concourse.bass as bass
from concourse import mybir

F32 = mybir.dt.float32
BF16 = mybir.dt.bfloat16
I32 = mybir.dt.int32
U32 = mybir.dt.uint32
ALU = mybir.AluOpType
ACT = mybir.ActivationFunctionType
AX_X = mybir.AxisListType.X

P = 128
B, S, D = 4, 512, 256
NT = S // P
DC = D // P
H, DK = 16, 16
HG = 4
NG = H // HG
HP = 32
PAIRS = ((0, 0), (0, 1), (0, 2), (1, 0), (1, 1), (2, 0))
ROW_DELTA = DK * len(PAIRS)
ROW_MAX = ROW_DELTA + 3
ROWS = ROW_MAX + 2
PAD = 2
EPS = 1e-5
LOWEST = -3.0e38
E1, I1, KS1 = 16, 128, 3
E2, FF = 8, 1024
FC = FF // P
CAPACITY = -(-5 * B * S // (4 * E2))
TOKENS = B * S
BLOCK = 2 * P
BLOCKS = (2 * TOKENS + E2 * (BLOCK - 1)) // BLOCK
SPARE = E2 * TOKENS
SLOTS2 = SPARE + BLOCKS * BLOCK
DROPPED = E2 * CAPACITY
WINDOW, DEV_POW, MASKED = 16.0, 128.0, -1000000000.0


@contextmanager
def Stage(nc, tag, sems, buffers=(), pool_dma=False):
    with ExitStack() as ctx:
        signals = {s: ctx.enter_context(nc.semaphore(f"{tag}_{s}")) for s in sems.split()}
        tiles = {name: ctx.enter_context(nc.sbuf_tensor(f"{tag}_{name}", shape, dt)) for name, shape, dt in buffers}
        with nc.Block() as block:
            yield block, {**signals, **tiles}
        numbers = [s.num for s in signals.values()]
        if pool_dma:
            nc.gpsimd.dma_reset(range(min(numbers), max(numbers) + 1))
        nc.all_engine_barrier(sems_to_clear=range(min(numbers), max(numbers) + 1))


def linker(engine, sem):
    count = [0]

    def link(ins):
        count[0] += 1
        ins.then_inc(sem, 1)
        engine.wait_ge(sem, count[0])
    return link


def inverse_root(nc, link, out, var, half, scratch, guess):
    v = nc.vector
    link(v.tensor_scalar(half, var, EPS, None, ALU.add))
    link(v.tensor_scalar(guess, half.bitcast(I32), 1, None, ALU.arith_shift_right))
    link(v.tensor_scalar(out.bitcast(I32), guess, -1.0, float(0x5F3759DF), ALU.mult, ALU.add))
    link(v.tensor_scalar(half, half, -0.5, None, ALU.mult))
    for _ in range(3):
        link(v.tensor_tensor(scratch, out, out, ALU.mult))
        link(v.tensor_tensor(scratch, scratch, half, ALU.mult))
        link(v.scalar_tensor_tensor(out, scratch, 1.5, out, ALU.add, ALU.mult))


def moments(nc, link, src, st, mv):
    for t in range(NT):
        ins = nc.vector.bn_stats(st[:, t, :], src[:, t, :])
    link(ins)
    for t in range(NT):
        ins = nc.vector.bn_aggr(mv[:, t, :], st[:, t, :])
    link(ins)


STAT_BUFFERS = (("st", [P, NT, 6], F32), ("mv", [P, NT, 2], F32), ("rs", [P, NT], F32), ("half", [P, NT], F32),
                ("scr", [P, NT], F32), ("guess", [P, NT], I32))


NORM_SEMS = "step normed nturned nt_out "


def norm_on_vector(nc, m, link, k):
    moments(nc, link, m.x, k["st"], k["mv"])
    inverse_root(nc, link, k["rs"][:], k["mv"][:, :, 1], k["half"][:], k["scr"][:], k["guess"][:])
    for t in range(NT):
        nc.vector.tensor_scalar(m.n[:, t, :], m.x[:, t, :], k["mv"][:, t, 0:1], k["rs"][:, t:t + 1],
                                ALU.subtract, ALU.mult).then_inc(k["normed"], 1)


def norm_on_tensor(nc, m, pe, k):
    for t in range(NT):
        pe.wait_ge(k["normed"], t + 1)
        for c in range(DC):
            ins = nc.tensor.transpose(m.ps[:, c, t * P:(t + 1) * P], m.n[:, t, c * P:(c + 1) * P], m.ident[:])
    ins.then_inc(k["nturned"], 1)


def norm_on_scalar(nc, m, act, k):
    act.wait_ge(k["nturned"], 1)
    for c in range(DC):
        nc.scalar.activation(m.nt[:, c, PAD:PAD + S], m.ps[:, c, :], ACT.Copy).then_inc(k["nt_out"], 1)


def affine_norm(nc, link, src, gain, add, added, dst, k, last, again=False):
    moments(nc, link, src, k["st"], k["mv"])
    for t in range(NT):
        nc.vector.scalar_tensor_tensor(k["cg"][:, t, :], src[:, t, :], k["mv"][:, t, 0:1], gain[:], ALU.subtract,
                                       ALU.mult)
    inverse_root(nc, link, k["rs"][:], k["mv"][:, :, 1], k["half"][:], k["scr"][:], k["guess"][:])
    if again:
        link(nc.vector.tensor_tensor(k["var2"][:], k["rs"][:], k["rs"][:], ALU.mult))
        link(nc.vector.tensor_tensor(k["var2"][:], k["var2"][:], k["mv"][:, :, 1], ALU.mult))
        inverse_root(nc, link, k["rs2"][:], k["var2"][:], k["half"][:], k["scr"][:], k["guess"][:])
        link(nc.vector.tensor_tensor(k["rs"][:], k["rs2"][:], k["rs"][:], ALU.mult))
    added()
    for t in range(NT):
        last(t, nc.vector.scalar_tensor_tensor(dst[:, t, :], k["cg"][:, t, :], k["rs"][:, t:t + 1], add[:, t, :],
                                               ALU.mult, ALU.add))


ATTENTION_BUFFERS = (
    ("qs", [P, H, S], BF16), ("ks", [P, H, S], BF16), ("v", [P, NT, H, HP], F32),
    ("ot", [P, NG, S], F32), ("on", [P, NG, S], F32),
    ("qp", [P, 3, DC, S], BF16), ("kp", [P, 3, DC, S], BF16),
    ("probs", [P, 4, 2, S], F32), ("recip", [P, NT, HG], F32),
    ("mx", [P, NG, NT, HG], F32), ("mxd", [P, NG, NT, HG], F32), ("m1", [P, NT, HG], BF16),
    ("mp", [P, NT, 2, HG], F32), ("mt", [2 * HG, 2, S], BF16), ("diag", [P, 2, P], F32),
    ("tq", [P, 1], F32), ("bqs", [P, DC], F32), ("rs2", [P, NT], F32), ("var2", [P, NT], F32), ("cg", [P, NT, D], F32),
) + STAT_BUFFERS


def attention_stage(nc, m, tag, w, source, causal, doubled=None, before=None):
    first = [(g, t, j) for g in range(NG) for t in range(NT) for j in range(HG)]
    second = [(g, t, j) for g in range(NG) for t in range(NT) for j in (0, 2)]
    per_group = NT * HG // 2
    LAG = HG * NT + 8
    TURN_LATER, SELECT_LATER, BACK_LATER = 2, 4, 8
    BANK_M, BANK_O, BANK_P = 2, 3, 4

    def order():
        out = []
        for u in range(2 * len(second) + LAG + 4):
            if u < len(first):
                out.append(("max", u))
                if u % (HG * NT) == HG * NT - 1:
                    out.append(("turn", u // (HG * NT)))
            s = (u - LAG) // 2
            if (u - LAG) % 2 == 0 and 0 <= s < len(second):
                out.append(("score", s))
            elif (u - LAG) % 2 == 1 and s % 2 == 1 and s >= 3:
                v = (s - 3) // 2
                out.append(("value", v))
                if v % NT == NT - 1:
                    out.append(("select", v // NT))
                    if v // NT % 2 == 1 and not causal:
                        out.append(("back", v // NT // 2))
        for kind, by in (("turn", TURN_LATER), ("select", SELECT_LATER), ("back", BACK_LATER)):
            for step in [o for o in out if o[0] == kind]:
                at = out.index(step)
                out.remove(step)
                out.insert(min(at + by, len(out)), step)
        return out

    ORDER = order()
    shared = [o for o in ORDER if o[0] in ("turn", "select", "back")]
    sems = NORM_SEMS + (
        "projq projk projv qfull kfull qrest krest v_out scaled qsplit ksplit fixed repk0 repk1 repq0 repq1 maxed "
        "maxdone turned turn_out mrow scored exped masked valued o_out selected backed back_out divided proj gstep "
        "ready shifted biased scattered")
    with Stage(nc, tag, sems, ATTENTION_BUFFERS, before is not None) as (block, k):
        qf, kf = k["ot"][:, 0:DC, :], k["ot"][:, DC:2 * DC, :]
        qrest, krest = k["on"][:, 0:DC, :], k["on"][:, DC:2 * DC, :]
        kc = source
        koff = PAD if causal else 0

        @block.sync
        def _(sp):
            for dst, src in ((k["qs"][ROW_DELTA:ROW_MAX], m.quarter_rows), (k["ks"][ROW_MAX:ROWS], m.one_rows),
                             (k["ks"][ROW_DELTA:ROW_MAX], m.zero_rows if causal else m.delta_rows)):
                sp.dma_start(dst, src[:].unsqueeze(1).to_broadcast([dst.shape[0], H, S])).then_inc(k["fixed"], 16)
            kside = (k["kp"], k["kfull"], k["ksplit"], k["ks"], (k["repk0"], k["repk1"]), 1)
            qside = (k["qp"], k["qfull"], k["qsplit"], k["qs"], (k["repq0"], k["repq1"]), 0)
            for (part, full, split, dst, rep, side), c in ((kside, 0), (qside, 0), (kside, 1), (qside, 1)):
                for p in range(3):
                    if p == 0:
                        sp.wait_ge(full, 2 * c + 2)
                    else:
                        sp.wait_ge(split, 2 * c + p)
                    for n, pair in enumerate(PAIRS):
                        if pair[side] == p:
                            heads = slice(c * H // DC, (c + 1) * H // DC)
                            sp.dma_start(dst[n * DK:(n + 1) * DK, heads].rearrange("i h s -> i (h s)"),
                                         part[:, p, c]).then_inc(rep[c], 16)
            for g in range(NG):
                sp.wait_ge(k["turn_out"], g + 1)
                sp.dma_start(k["qs"][ROW_MAX:ROWS, g * HG:(g + 1) * HG, :], k["mt"][:, g % 2, :])\
                    .then_inc(k["mrow"], 16)
            sp.wait_ge(k["mrow"], 16 * NG)

        @block.tensor
        def _(pe):
            def project(signal, bank, weight, src, off, c):
                for i in range(DC):
                    if src is m.nt:
                        pe.wait_ge(k["nt_out"], i + 1)
                    ins = nc.tensor.matmul(m.ps[:, bank + c, :], weight[:, i, c * P:(c + 1) * P],
                                           src[:, i, off:off + S], start=(i == 0), stop=(i == DC - 1))
                ins.then_inc(signal, 1)

            def project_v():
                for t in range(NT):
                    for i in range(DC):
                        ins = nc.tensor.matmul(m.ps[:, 4 + t, 0:D], kc[:, i, koff + t * P:koff + (t + 1) * P],
                                               w.v[:, i, :], start=(i == 0), stop=(i == DC - 1))
                    ins.then_inc(k["projv"], 1)

            if causal:
                norm_on_tensor(nc, m, pe, k)
                for c in range(DC):
                    project(k["projk"], 2, w.k, kc, koff, c)
                    project(k["projq"], 0, w.q, m.nt, PAD, c)
            else:
                for c in range(DC):
                    project(k["projk"], 2, w.k, kc, koff, c)
                norm_on_tensor(nc, m, pe, k)
                for c in range(DC):
                    project(k["projq"], 0, w.q, m.nt, PAD, c)
            project_v()
            pe.wait_ge(k["kfull"], 2 * DC)
            pe.wait_ge(k["qfull"], 2 * DC)
            pe.wait_ge(k["fixed"], 48)
            used = [0]

            def shared_bank():
                if used[0]:
                    last, n = shared[used[0] - 1]
                    pe.wait_ge(k[{"turn": "turn_out", "select": "divided", "back": "back_out"}[last]], n + 1)
                used[0] += 1

            def project_out(c, tiles):
                pe.wait_ge(k["back_out"], c + 1)
                for t in tiles:
                    ins = nc.tensor.matmul(m.ps[:, 4 + t, 0:D], k["on"][:, c, t * P:(t + 1) * P], w.o[:, c, :],
                                           start=(c == 0), stop=(c == DC - 1))
                    if c == DC - 1:
                        ins.then_inc(k["proj"], 1)

            for what, u in ORDER:
                if what == "max":
                    g, t, j = first[u]
                    h = g * HG + j
                    if (t, j) == (0, 0) and g % 2 == 0:
                        pe.wait_ge((k["repk0"], k["repk1"])[g // 2], 16 * len(PAIRS))
                        pe.wait_ge((k["repq0"], k["repq1"])[g // 2], 16 * len(PAIRS))
                    if u >= 2:
                        pe.wait_ge(k["maxed"], u - 1)
                    n = (t + 1) * P if causal else S
                    nc.tensor.matmul(m.ps[:, u % 2, 0:n], k["qs"][0:ROW_MAX, h, t * P:(t + 1) * P],
                                     k["ks"][0:ROW_MAX, h, 0:n], start=True, stop=True).then_inc(k["scored"], 1)
                elif what == "turn":
                    pe.wait_ge(k["maxdone"], u + 1)
                    shared_bank()
                    for t in range(NT):
                        ins = nc.tensor.transpose(m.ps[0:2 * HG, BANK_M, t * P:(t + 1) * P],
                                                  k["mp"][:, t].rearrange("p a j -> p (a j)"), m.ident[:])
                    ins.then_inc(k["turned"], 1)
                elif what == "score":
                    g, t, j = second[u]
                    if u == 0:
                        pe.wait_ge(k["v_out"], NT)
                        pe.wait_ge(k["ready"], 1)
                    if u % per_group == 0:
                        pe.wait_ge(k["mrow"], 16 * (g + 1))
                    if u >= 2:
                        pe.wait_ge(k["exped"], u - 1)
                    q0 = t * P if causal else 0
                    for i in range(2):
                        h = g * HG + j + i
                        ins = nc.tensor.matmul(m.ps[:, BANK_P + 2 * (u % 2) + i, q0:S],
                                               k["ks"][0:ROWS, h, t * P:(t + 1) * P], k["qs"][0:ROWS, h, q0:S],
                                               start=True, stop=True)
                    ins.then_inc(k["proj"], 1)
                elif what == "value":
                    g, t = u // NT, u % NT
                    if u == NG * NT - 1 and not causal:
                        pe.wait_ge(k["exped"], len(second) - 1)
                        project_out(0, (0, 1))
                    if causal:
                        pe.wait_ge(k["masked"], 2 * u + 2)
                    else:
                        pe.wait_ge(k["exped"], 2 * u + 2)
                    if t == 0 and g >= 1:
                        pe.wait_ge(k["o_out"], g)
                    q0 = t * P if causal else 0
                    for j in range(HG):
                        ins = nc.tensor.matmul(m.ps[HP * j:HP * (j + 1), BANK_O, q0:S],
                                               k["v"][:, t, g * HG + j, :],
                                               k["probs"][:, (2 * u + j // 2) % 4, j % 2, q0:S],
                                               start=(t == 0), stop=(t == NT - 1))
                    ins.then_inc(k["valued"], 1)
                elif what == "select":
                    pe.wait_ge(k["o_out"], u + 1)
                    shared_bank()
                    for t in range(NT):
                        ins = nc.tensor.transpose(m.ps[:, BANK_M, t * P:(t + 1) * P],
                                                  k["ot"][:, u, t * P:(t + 1) * P], m.ident[:])
                    ins.then_inc(k["selected"], 1)
                else:
                    if u == DC - 1:
                        pe.wait_ge(k["exped"], len(second))
                        project_out(0, (2, 3))
                    pe.wait_ge(k["divided"], 2 * u + 2)
                    shared_bank()
                    for t in range(NT):
                        ins = nc.tensor.transpose(m.ps[:, BANK_M, t * P:(t + 1) * P],
                                                  m.y[:, t, u * P:(u + 1) * P], m.ident[:])
                    ins.then_inc(k["backed"], 1)
            if not causal:
                project_out(1, range(NT))

        @block.scalar
        def _(act):
            def take_k(c):
                act.wait_ge(k["projk"], c + 1)
                nc.scalar.activation(kf[:, c, :], m.ps[:, 2 + c, :], ACT.Identity,
                                     bias=w.bk[:, c:c + 1]).then_inc(k["kfull"], 1)
                nc.scalar.activation(k["kp"][:, 0, c], m.ps[:, 2 + c, :], ACT.Identity,
                                     bias=w.bk[:, c:c + 1]).then_inc(k["kfull"], 1)

            def take_q(c):
                act.wait_ge(k["projq"], c + 1)
                for dst in (qf[:, c, :], k["qp"][:, 0, c]):
                    nc.scalar.activation(dst, m.ps[:, c, :], ACT.Identity, bias=k["bqs"][:, c:c + 1],
                                         scale=k["tq"][:, 0:1]).then_inc(k["qfull"], 1)

            act.wait_ge(k["scaled"], 1)
            if causal:
                norm_on_scalar(nc, m, act, k)
                for c in range(DC):
                    take_k(c)
                    take_q(c)
            else:
                for c in range(DC):
                    take_k(c)
                norm_on_scalar(nc, m, act, k)
                for c in range(DC):
                    take_q(c)
            for what, u in ORDER:
                if what == "turn":
                    act.wait_ge(k["turned"], u + 1)
                    if u >= 2:
                        act.wait_ge(k["mrow"], 16 * (u - 1))
                    nc.scalar.activation(k["mt"][:, u % 2, :], m.ps[0:2 * HG, BANK_M, :], ACT.Copy)\
                        .then_inc(k["turn_out"], 1)
                elif what == "back":
                    act.wait_ge(k["backed"], u + 1)
                    nc.scalar.activation(k["on"][:, u, :], m.ps[:, BANK_M, :], ACT.Copy).then_inc(k["back_out"], 1)
                elif what == "score":
                    g, t, j = second[u]
                    act.wait_ge(k["proj"], u + 1)
                    if u >= 4:
                        act.wait_ge(k["valued"], u // 2 - 1)
                    q0 = t * P if causal else 0
                    b = BANK_P + 2 * (u % 2)
                    nc.scalar.activation(k["probs"][:, u % 4, :, q0:S], m.ps[:, b:b + 2, q0:S], ACT.Exp)\
                        .then_inc(k["exped"], 1)
                elif what == "value" and u % NT == NT - 1:
                    g = u // NT
                    act.wait_ge(k["valued"], u + 1)
                    nc.scalar.activation(k["ot"][:, g, :], m.ps[:, BANK_O, :], ACT.Copy).then_inc(k["o_out"], 1)

        @block.vector
        def _(dve):
            link = linker(dve, k["step"])
            if causal:
                nc.vector.memset(k["tq"][:], 1.0 / 16.0)
                link(nc.vector.memset(k["mx"][:], LOWEST))
            else:
                link(nc.vector.tensor_scalar(k["tq"][:], m.tau[:], 0.25, None, ALU.mult))
            nc.vector.tensor_scalar(k["bqs"][:], w.bq[:], k["tq"][:, 0:1], None, ALU.mult).then_inc(k["scaled"], 1)
            if doubled is not None:
                affine_norm(nc, link, m.x, doubled[0], m.y, lambda: dve.wait_ge(k["shifted"], 1), m.x, k,
                            lambda t, ins: link(ins), again=True)
            norm_on_vector(nc, m, link, k)

            def take_v():
                dve.wait_ge(k["ready"], 1)
                for t in range(NT):
                    dve.wait_ge(k["projv"], t + 1)
                    nc.vector.tensor_tensor(
                        k["v"][:, t, :, 0:DK], m.ps[:, 4 + t, 0:D].rearrange("p (h i) -> p h i", h=H),
                        w.bv[:].rearrange("p (h i) -> p h i", h=H), ALU.add).then_inc(k["v_out"], 1)

            for c in range(DC):
                dve.wait_ge(k["qfull"], 2 * c + 2)
                nc.vector.tensor_tensor(qrest[:, c], qf[:, c], k["qp"][:, 0, c], ALU.subtract).then_inc(k["qrest"], 1)
                dve.wait_ge(k["qrest"], c + 1)
                nc.vector.tensor_copy(k["qp"][:, 1, c], qrest[:, c]).then_inc(k["qsplit"], 1)
                dve.wait_ge(k["qsplit"], 2 * c + 1)
                nc.vector.tensor_tensor(k["qp"][:, 2, c], qrest[:, c], k["qp"][:, 1, c], ALU.subtract)\
                    .then_inc(k["qsplit"], 1)
            take_v()

            def split_maxima(g):
                if causal:
                    link(nc.vector.tensor_tensor(k["mx"][:, g], k["mx"][:, g], k["mxd"][:, g], ALU.max))
                link(nc.vector.tensor_scalar(k["m1"][:], k["mx"][:, g], -1.0, None, ALU.mult))
                if g >= 1:
                    dve.wait_ge(k["turned"], g)
                nc.vector.tensor_copy(k["mp"][:, :, 0, :], k["m1"][:])
                nc.vector.scalar_tensor_tensor(k["mp"][:, :, 1, :], k["mx"][:, g], -1.0, k["m1"][:], ALU.mult,
                                               ALU.subtract).then_inc(k["maxdone"], 1)

            for what, u in ORDER:
                if what == "max":
                    g, t, j = first[u]
                    dve.wait_ge(k["scored"], u + 1)
                    if causal:
                        if t:
                            nc.vector.tensor_reduce(k["mx"][:, g, t, j:j + 1], m.ps[:, u % 2, 0:t * P], AX_X, ALU.max)
                        if u >= 2:
                            dve.wait_ge(k["maxed"], u - 1)
                        ins = nc.vector.tensor_tensor_reduce(
                            out=k["diag"][:, u % 2, :], in0=m.ps[:, u % 2, t * P:(t + 1) * P], in1=m.later[:],
                            scale=1.0, scalar=LOWEST, op0=ALU.add, op1=ALU.max, accum_out=k["mxd"][:, g, t, j:j + 1])
                    else:
                        ins = nc.vector.tensor_reduce(k["mx"][:, g, t, j:j + 1], m.ps[:, u % 2, :], AX_X, ALU.max)
                    ins.then_inc(k["maxed"], 1)
                    if u % (HG * NT) == HG * NT - 1:
                        dve.wait_ge(k["maxed"], u + 1)
                        split_maxima(g)
                elif what == "select":
                    dve.wait_ge(k["selected"], u + 1)
                    rows = m.ps[:, BANK_M, :].rearrange("p (t j i) -> p t j i", t=NT, j=HG)
                    link(nc.vector.reciprocal(k["recip"][:], rows[:, :, :, DK]))
                    out = m.y[:, :, u * HG * DK:(u + 1) * HG * DK].rearrange("p t (j i) -> p t j i", j=HG)
                    nc.vector.tensor_tensor(out, rows[:, :, :, 0:DK],
                                            k["recip"][:].unsqueeze(3).to_broadcast([P, NT, HG, DK]),
                                            ALU.mult).then_inc(k["divided"], 1)
            if not causal:
                dve.wait_ge(k["biased"], 1)
            for t in range(0 if causal else NT):
                dve.wait_ge(k["proj"], len(second) + t + 1)
                nc.vector.tensor_tensor(m.x[:, t, :], m.x[:, t, :], m.ps[:, 4 + t, 0:D], ALU.add)

        @block.gpsimd
        def _(pool):
            link = linker(pool, k["gstep"])
            if doubled is not None:
                for t in range(NT):
                    ins = nc.gpsimd.tensor_tensor(m.y[:, t, :], m.x[:, t, :], doubled[1], ALU.add)
                ins.then_inc(k["shifted"], 1)
            link(nc.gpsimd.memset(k["v"][:, :, :, DK:HP], 0.0))
            nc.gpsimd.memset(k["v"][:, :, :, DK:DK + 1], 1.0).then_inc(k["ready"], 1)
            for c in range(DC):
                pool.wait_ge(k["kfull"], 2 * c + 2)
                nc.gpsimd.tensor_tensor(krest[:, c], kf[:, c], k["kp"][:, 0, c], ALU.subtract).then_inc(k["krest"], 1)
                pool.wait_ge(k["krest"], c + 1)
                nc.gpsimd.tensor_copy(k["kp"][:, 1, c], krest[:, c]).then_inc(k["ksplit"], 1)
                pool.wait_ge(k["ksplit"], 2 * c + 1)
                nc.gpsimd.tensor_tensor(k["kp"][:, 2, c], krest[:, c], k["kp"][:, 1, c], ALU.subtract)\
                    .then_inc(k["ksplit"], 1)
            if not causal:
                pool.wait_ge(k["normed"], NT)
                for t in range(NT):
                    ins = nc.gpsimd.tensor_tensor(m.x[:, t, :], m.x[:, t, :], w.bo[:], ALU.add)
                ins.then_inc(k["biased"], 1)
            if before is not None:
                scatter_ids(nc, pool, k, *before)
            for what, u in ORDER:
                if what == "score" and causal:
                    g, t, j = second[u]
                    pool.wait_ge(k["exped"], u + 1)
                    blk = k["probs"][:, u % 4, :, t * P:(t + 1) * P]
                    nc.gpsimd.affine_select(out=blk, in_=blk, compare_op=ALU.is_ge, fill=0.0, base=0,
                                            pattern=[[0, 2], [1, P]], channel_multiplier=-1).then_inc(k["masked"], 1)


def load_scalars(sp, k, m, b, pairs):
    for dst, src in pairs:
        sp.dma_start(dst[:], src.rearrange("(n a) -> n a", a=1)[bass.ds(b, 1), :].partition_broadcast(P))\
            .then_inc(k["small"], 16)


def context_rows(ctx_in, b):
    return ctx_in[bass.ds(b, 1)].rearrange("o (t p) d -> p (o t) d", p=P)


def context_on_tensor(nc, m, pe, k):
    pe.wait_ge(k["cin"], 16)
    for t in range(NT):
        for c in range(DC):
            ins = nc.tensor.transpose(m.ps[:, 4 + c, t * P:(t + 1) * P], m.c[:, t, c * P:(c + 1) * P], m.ident[:])
    ins.then_inc(k["cturned"], 1)


def context_on_scalar(nc, m, act, k):
    act.wait_ge(k["cturned"], 1)
    nc.scalar.activation(m.ct[:], m.ps[:, 4:4 + DC, :], ACT.Copy)


LOAD_BUFFERS = (("drow", [1, S], F32), ("drest", [1, S], F32), ("dparts", [1, 3, S], BF16), ("len_i", [P, 1], I32))
LOAD_SEMS = " xin cin small cturned dsplit sent"


def load_on_sync(nc, m, sp, k, b, src, after):
    x_in, ctx_in, tau, delta, lens, pt = src
    sp.dma_start(m.c[:], context_rows(ctx_in, b)).then_inc(k["cin"], 16)
    if after is not None:
        sp.wait_ge(*after)
    sp.dma_start(m.x[:], batch_rows(x_in, b)).then_inc(k["xin"], 16)
    sp.dma_start(k["drow"][:], delta[bass.ds(b, 1), :]).then_inc(k["small"], 16)
    load_scalars(sp, k, m, b, ((m.tau, tau), (m.pt, pt), (k["len_i"], lens)))
    sp.wait_ge(k["dsplit"], 1)
    sp.dma_start(m.delta_rows[:, :], k["dparts"][:].rearrange("a r s -> a (r s)")).then_inc(k["sent"], 16)
    sp.wait_ge(k["sent"], 16)
    sp.wait_ge(k["xin"], 16)


def load_on_vector(nc, m, dve, link, k):
    dve.wait_ge(k["small"], 64)
    nc.vector.tensor_copy(m.len_f[:], k["len_i"][:])
    link(nc.vector.tensor_copy(k["dparts"][:, 0], k["drow"][:]))
    link(nc.vector.tensor_tensor(k["drest"][:], k["drow"][:], k["dparts"][:, 0], ALU.subtract))
    link(nc.vector.tensor_copy(k["dparts"][:, 1], k["drest"][:]))
    nc.vector.tensor_tensor(k["dparts"][:, 2], k["drest"][:], k["dparts"][:, 1], ALU.subtract)\
        .then_inc(k["dsplit"], 1)


def scatter_ids(nc, pool, k, table, slots, ids, choices):
    for t in range(NT):
        for c in range(choices):
            nc.gpsimd.indirect_dma_start(
                out=table[:, :], out_offset=bass.IndirectOffsetOnAxis(ap=slots[:, t, c:c + 1], axis=0),
                in_=ids[:, t:t + 1], in_offset=None).then_inc(k["scattered"], 16)
    pool.wait_ge(k["scattered"], 16 * NT * choices)


def window_steps(nc, m, link, k):
    v = nc.vector
    link(v.tensor_scalar(k["start"][:], m.pt[:], WINDOW, 0.0, ALU.subtract, ALU.max))
    link(v.tensor_scalar(k["end"][:, 0:1], m.pt[:], WINDOW, None, ALU.add))
    link(v.tensor_tensor(k["end"][:, 1:2], k["end"][:, 0:1], m.len_f[:], ALU.min))
    v.tensor_scalar(k["off"][:], m.index[:], k["start"][:, 0:1], None, ALU.is_lt)
    link(v.tensor_scalar(k["dist"][:], m.index[:], k["end"][:, 1:2], None, ALU.is_gt))
    link(v.tensor_tensor(k["off"][:], k["off"][:], k["dist"][:], ALU.max))
    v.tensor_scalar(k["keep"][:], k["off"][:], -1.0, 1.0, ALU.mult, ALU.add)
    v.tensor_scalar(k["big"][:], k["off"][:], MASKED, None, ALU.mult)
    link(v.tensor_scalar(k["dist"][:], m.index[:], m.pt[:, 0:1], None, ALU.subtract))
    v.tensor_tensor(k["off"][:], k["dist"][:], k["dist"][:], ALU.mult).then_inc(k["squared"], 1)


def location_stage(nc, m, tag, w):
    bufs = STAT_BUFFERS + (
        ("wac", [P, DC, S], F32), ("cw", [P, NT, D], F32), ("sc", [P, NT, S], F32), ("nmx", [P, NT], F32),
        ("sums", [P, NT], F32), ("rsum", [P, NT], F32), ("al", [P, NT, S], F32), ("alt", [P, NT, S], F32),
        ("th", [P, NT, D], F32), ("end", [P, 2], F32), ("start", [P, 1], F32), ("dist", [P, S], F32),
        ("off", [P, S], F32), ("keep", [P, S], F32), ("big", [P, S], F32), ("gauss", [P, S], F32))
    sems = NORM_SEMS + "ready ready_out scored maxed exped weighed turned turned_out outp tanhed squared"
    BANK_READY, BANK_TURN, BANK_OUT, BANK_CW = 2, 2, 0, 6
    steps = [("turn", 0)] + [step for t in range(NT - 1) for step in (("turn", t + 1), ("out", t))] + [("out", NT - 1)]
    with Stage(nc, tag, sems, bufs) as (block, k):
        @block.tensor
        def _(pe):
            for c in range(DC):
                for i in range(DC):
                    ins = nc.tensor.matmul(m.ps[:, BANK_READY + c, :], w.a[:, i, c * P:(c + 1) * P], m.ct[:, i, :],
                                           start=(i == 0), stop=(i == DC - 1))
                ins.then_inc(k["ready"], 1)
            for t in range(NT):
                for i in range(DC):
                    ins = nc.tensor.matmul(m.ps[:, BANK_CW + t // 2, (t % 2) * D:(t % 2 + 1) * D],
                                           m.ct[:, i, t * P:(t + 1) * P], w.c[:, i, :],
                                           start=(i == 0), stop=(i == DC - 1))
                if t % 2 == 1:
                    ins.then_inc(k["ready"], 1)
            norm_on_tensor(nc, m, pe, k)
            pe.wait_ge(k["ready_out"], 4)
            for t in range(NT):
                for c in range(DC):
                    pe.wait_ge(k["nt_out"], c + 1)
                    ins = nc.tensor.matmul(m.ps[:, 4 + t, :], m.nt[:, c, PAD + t * P:PAD + (t + 1) * P],
                                           k["wac"][:, c, :], start=(c == 0), stop=(c == DC - 1))
                ins.then_inc(k["scored"], 1)
            for what, t in steps:
                if what == "turn":
                    pe.wait_ge(k["weighed"], t + 1)
                    if t >= 2:
                        pe.wait_ge(k["turned_out"], t - 1)
                    for n in range(NT):
                        ins = nc.tensor.transpose(m.ps[:, BANK_TURN + t % 2, n * P:(n + 1) * P],
                                                  k["al"][:, t, n * P:(n + 1) * P], m.ident[:])
                    ins.then_inc(k["turned"], 1)
                else:
                    if t >= 2:
                        pe.wait_ge(k["tanhed"], t - 1)
                    for n in range(DC):
                        nc.tensor.matmul(m.ps[:, BANK_OUT + t % 2, 0:D], m.nt[:, n, PAD + t * P:PAD + (t + 1) * P],
                                         w.c[:, DC + n, :], start=(n == 0), stop=False)
                    pe.wait_ge(k["turned_out"], t + 1)
                    for n in range(NT):
                        ins = nc.tensor.matmul(m.ps[:, BANK_OUT + t % 2, 0:D], k["alt"][:, n, t * P:(t + 1) * P],
                                               k["cw"][:, n, :], start=False, stop=(n == NT - 1))
                    ins.then_inc(k["outp"], 1)

        @block.scalar
        def _(act):
            def exponential(t):
                act.wait_ge(k["maxed"], t + 1)
                nc.scalar.activation(k["al"][:, t, :], k["sc"][:, t, :], ACT.Exp, bias=k["nmx"][:, t:t + 1],
                                     accum_out=k["sums"][:, t:t + 1]).then_inc(k["exped"], 1)

            for c in range(DC):
                act.wait_ge(k["ready"], c + 1)
                nc.scalar.activation(k["wac"][:, c, :], m.ps[:, BANK_READY + c, :], ACT.Copy)\
                    .then_inc(k["ready_out"], 1)
            for h in range(NT // 2):
                act.wait_ge(k["ready"], DC + h + 1)
                nc.scalar.activation(k["cw"][:, 2 * h:2 * h + 2, :].rearrange("p t d -> p (t d)"),
                                     m.ps[:, BANK_CW + h, :], ACT.Copy).then_inc(k["ready_out"], 1)
            norm_on_scalar(nc, m, act, k)
            act.wait_ge(k["squared"], 1)
            nc.scalar.activation(k["gauss"][:], k["off"][:], ACT.Exp, scale=-1.0 / DEV_POW)
            exponential(0)
            for what, t in steps:
                if what == "turn":
                    if t + 1 < NT:
                        exponential(t + 1)
                    act.wait_ge(k["turned"], t + 1)
                    nc.scalar.activation(k["alt"][:, :, t * P:(t + 1) * P],
                                         m.ps[:, BANK_TURN + t % 2, :].rearrange("p (n q) -> p n q", n=NT), ACT.Copy)\
                        .then_inc(k["turned_out"], 1)
                else:
                    act.wait_ge(k["outp"], t + 1)
                    nc.scalar.activation(k["th"][:, t, :], m.ps[:, BANK_OUT + t % 2, 0:D], ACT.Tanh)\
                        .then_inc(k["tanhed"], 1)

        @block.vector
        def _(dve):
            link = linker(dve, k["step"])
            norm_on_vector(nc, m, link, k)
            window_steps(nc, m, link, k)
            dve.wait_ge(k["squared"], 1)

            def weigh(t):
                dve.wait_ge(k["exped"], t + 1)
                link(nc.vector.reciprocal(k["rsum"][:, t:t + 1], k["sums"][:, t:t + 1]))
                nc.vector.scalar_tensor_tensor(k["al"][:, t, :], k["al"][:, t, :], k["rsum"][:, t:t + 1],
                                               k["gauss"][:], ALU.mult, ALU.mult).then_inc(k["weighed"], 1)

            for t in range(NT):
                dve.wait_ge(k["scored"], t + 1)
                link(nc.vector.tensor_tensor(k["sc"][:, t, :], m.ps[:, 4 + t, :], k["keep"][:], ALU.mult))
                link(nc.vector.tensor_tensor(k["sc"][:, t, :], k["sc"][:, t, :], k["big"][:], ALU.add))
                nc.vector.tensor_reduce(k["nmx"][:, t:t + 1], k["sc"][:, t, :], AX_X, ALU.max, negate=True)\
                    .then_inc(k["maxed"], 1)
                if t >= 1:
                    weigh(t - 1)
            weigh(NT - 1)
            for t in range(NT):
                dve.wait_ge(k["tanhed"], t + 1)
                nc.vector.tensor_tensor(m.x[:, t, :], m.x[:, t, :], k["th"][:, t, :], ALU.add)


ROUTE_BUFFERS = (("lg", [P, NT, E1], F32), ("pr", [P, NT, E1], F32), ("rmx", [P, NT], F32), ("rsm", [P, NT], F32),
                 ("top", [P, NT, 8], F32), ("idx", [P, NT, 8], U32), ("idf", [P, NT, 8], F32), ("wt", [P, NT, 2], F32),
                 ("oh", [P, NT, E1], F32))


def spread_over(ap, n):
    return ap.unsqueeze(2).to_broadcast([P, NT, n])


def softmax_steps(nc, dve, link, k, n):
    lg, pr = k["lg"][:, :, 0:n], k["pr"][:, :, 0:n]
    link(nc.vector.tensor_reduce(k["rmx"][:], lg, AX_X, ALU.max))
    nc.vector.tensor_tensor(lg, lg, spread_over(k["rmx"][:], n), ALU.subtract).then_inc(k["logits"], 1)
    dve.wait_ge(k["rexp"], 1)
    link(nc.vector.tensor_reduce(k["rsm"][:], pr, AX_X, ALU.add))
    link(nc.vector.reciprocal(k["rsm"][:], k["rsm"][:]))
    link(nc.vector.tensor_tensor(pr, pr, spread_over(k["rsm"][:], n), ALU.mult))


def top_steps(nc, link, k, values, n):
    for t in range(NT):
        ins = nc.vector.max(k["top"][:, t, :], values[:, t, 0:n])
    link(ins)
    for t in range(NT):
        ins = nc.vector.max_index(k["idx"][:, t, :], k["top"][:, t, :], values[:, t, 0:n])
    link(ins)
    link(nc.vector.tensor_copy(k["idf"][:], k["idx"][:]))


def one_hot(nc, m, link, k, out, choice, n):
    link(nc.vector.tensor_tensor(out, m.columns[:, :, 0:n], k["idf"][:, :, choice:choice + 1].to_broadcast([P, NT, n]),
                                 ALU.is_equal))


def combine_steps(nc, m, link, k, n):
    comb, oh = m.comb[:, :, 0:n], k["oh"][:, :, 0:n]
    one_hot(nc, m, link, k, comb, 0, n)
    one_hot(nc, m, link, k, oh, 1, n)
    link(nc.vector.tensor_tensor(comb, comb, k["wt"][:, :, 0:1].to_broadcast([P, NT, n]), ALU.mult))
    link(nc.vector.tensor_tensor(oh, oh, k["wt"][:, :, 1:2].to_broadcast([P, NT, n]), ALU.mult))
    link(nc.vector.tensor_tensor(comb, comb, oh, ALU.add))


def logits_on_pe(nc, m, k, src, off, weight, n):
    for t in range(NT):
        for i in range(DC):
            ins = nc.tensor.matmul(m.ps[:, 0, t * E1:t * E1 + n], src[:, i, off + t * P:off + (t + 1) * P],
                                   weight[:, i, :], start=(i == 0), stop=(i == DC - 1))
    ins.then_inc(k["routed"], 1)


def psum_logits(m, n):
    return m.ps[:, 0, 0:NT * E1].rearrange("p (t e) -> p t e", t=NT)[:, :, 0:n]


def conv_mixture_stage(nc, m, w, gate_w, up_w, down_w):
    RING = 3
    bufs = ROUTE_BUFFERS + STAT_BUFFERS + (
        ("wg", [P, RING, DC, I1], F32), ("wu", [P, RING, DC, I1], F32), ("wd", [P, RING, D], F32),
        ("th", [P, 2, S], F32), ("ga", [P, 2, S], F32), ("hid", [P, 2, S], F32), ("ssum", [P, NT], F32))
    EXPERTS = E1 - 1
    units = EXPERTS + 1
    sems = NORM_SEMS + "routed logits rexp wload0 wload1 wload2 gated tanhed hidden down added"
    with Stage(nc, "cmix", sems, bufs) as (block, k):
        wload = (k["wload0"], k["wload1"], k["wload2"])
        @block.sync
        def _(sp):
            for e in range(EXPERTS):
                if e >= RING:
                    sp.wait_ge(k["down"], e - RING + 2)
                r = e % RING
                sp.dma_start(k["wg"][:, r], gate_w[e].rearrange("(c p) i -> p c i", p=P)).then_inc(wload[r], 16)
                sp.dma_start(k["wu"][:, r], up_w[e].rearrange("(c p) i -> p c i", p=P)).then_inc(wload[r], 16)
                sp.dma_start(k["wd"][:, r], down_w[e]).then_inc(wload[r], 16)

        @block.tensor
        def _(pe):
            norm_on_tensor(nc, m, pe, k)
            pe.wait_ge(k["nt_out"], DC)
            logits_on_pe(nc, m, k, m.nt, PAD, w.router, E1)

            def down(u):
                pe.wait_ge(k["hidden"], u + 1)
                if u >= 1:
                    pe.wait_ge(k["added"], u)
                for t in range(NT):
                    ins = nc.tensor.matmul(m.ps[:, 5 + t // 2, (t % 2) * D:(t % 2 + 1) * D],
                                           k["hid"][:, u % 2, t * P:(t + 1) * P],
                                           w.sdown[:] if u == 0 else k["wd"][:, (u - 1) % RING, :],
                                           start=True, stop=True)
                ins.then_inc(k["down"], 1)

            for u in range(units):
                gate, up = m.ps[:, 1 + 2 * (u % 2), :], m.ps[:, 2 + 2 * (u % 2), :]
                if u >= 2:
                    pe.wait_ge(k["hidden"], u - 1)
                if u == 0:
                    n = 0
                    for tap in range(KS1):
                        for i in range(DC):
                            nc.tensor.matmul(gate, w.conv[:, tap, i, :], m.nt[:, i, tap:tap + S], start=(n == 0),
                                             stop=(n == KS1 * DC - 1))
                            n += 1
                    for i in range(DC):
                        ins = nc.tensor.matmul(up, w.sup[:, i, :], m.nt[:, i, PAD:PAD + S], start=(i == 0),
                                               stop=(i == DC - 1))
                else:
                    r = (u - 1) % RING
                    pe.wait_ge(wload[r], 48 * ((u - 1) // RING + 1))
                    for bank, wt in ((gate, k["wg"]), (up, k["wu"])):
                        for i in range(DC):
                            ins = nc.tensor.matmul(bank, wt[:, r, i, :], m.nt[:, i, PAD:PAD + S], start=(i == 0),
                                                   stop=(i == DC - 1))
                ins.then_inc(k["gated"], 1)
                if u >= 1:
                    down(u - 1)
            down(units - 1)

        @block.scalar
        def _(act):
            norm_on_scalar(nc, m, act, k)
            act.wait_ge(k["logits"], 1)
            nc.scalar.activation(k["pr"][:], k["lg"][:], ACT.Exp).then_inc(k["rexp"], 1)
            for u in range(units):
                act.wait_ge(k["gated"], u + 1)
                if u >= 2:
                    act.wait_ge(k["hidden"], u - 1)
                nc.scalar.activation(k["th"][:, u % 2, :], m.ps[:, 1 + 2 * (u % 2), :], ACT.Tanh, scale=0.5)\
                    .then_inc(k["tanhed"], 1)

        @block.vector
        def _(dve):
            link = linker(dve, k["step"])
            norm_on_vector(nc, m, link, k)
            dve.wait_ge(k["routed"], 1)
            link(nc.vector.tensor_tensor(k["lg"][:], psum_logits(m, E1),
                                         w.rbias[:].unsqueeze(1).to_broadcast([P, NT, E1]), ALU.add))
            softmax_steps(nc, dve, link, k, E1)
            top_steps(nc, link, k, k["pr"], E1)
            link(nc.vector.tensor_tensor(k["ssum"][:], k["top"][:, :, 0], k["top"][:, :, 1], ALU.add))
            link(nc.vector.tensor_scalar(k["ssum"][:], k["ssum"][:], 1e-6, None, ALU.add))
            link(nc.vector.reciprocal(k["ssum"][:], k["ssum"][:]))
            link(nc.vector.tensor_tensor(k["wt"][:], k["top"][:, :, 0:2], spread_over(k["ssum"][:], 2), ALU.mult))
            combine_steps(nc, m, link, k, E1)
            for t in range(NT):
                ins = nc.vector.scalar_tensor_tensor(m.x[:, t, :], m.n[:, t, :], m.comb[:, t, EXPERTS:E1],
                                                     m.x[:, t, :], ALU.mult, ALU.add)
            link(ins)

            def add(u):
                dve.wait_ge(k["down"], u + 1)
                for t in range(NT):
                    y = m.ps[:, 5 + t // 2, (t % 2) * D:(t % 2 + 1) * D]
                    if u == 0:
                        ins = nc.vector.tensor_tensor(m.x[:, t, :], m.x[:, t, :], y, ALU.add)
                    else:
                        ins = nc.vector.scalar_tensor_tensor(m.x[:, t, :], y, m.comb[:, t, u - 1:u], m.x[:, t, :],
                                                             ALU.mult, ALU.add)
                ins.then_inc(k["added"], 1)

            for u in range(units):
                dve.wait_ge(k["tanhed"], u + 1)
                gate, up = m.ps[:, 1 + 2 * (u % 2), :], m.ps[:, 2 + 2 * (u % 2), :]
                link(nc.vector.scalar_tensor_tensor(k["ga"][:, u % 2, :], k["th"][:, u % 2, :], 1.0, gate, ALU.add,
                                                    ALU.mult))
                if u >= 2:
                    dve.wait_ge(k["down"], u - 1)
                nc.vector.scalar_tensor_tensor(k["hid"][:, u % 2, :], k["ga"][:, u % 2, :], 0.5, up, ALU.mult,
                                               ALU.mult).then_inc(k["hidden"], 1)
                if u >= 1:
                    add(u - 1)
                    if u >= 1:
                        dve.wait_ge(k["added"], u)
            add(units - 1)


RANK_BUFFERS = (("hot", [P, NT, E2], F32), ("taken", [P, NT + 1, E2], BF16), ("place", [P, NT, E2], F32),
                ("slots", [P, NT, 2], F32))


def ranks_on_pe(nc, m, k):
    blocks = NT + 1
    nc.tensor.matmul(m.ps[:, 1, 0:blocks * E2], m.earlier[:], k["taken"][:].rearrange("p t e -> p (t e)"),
                     start=True, stop=False)
    for back in range(1, blocks):
        ins = nc.tensor.matmul(m.ps[:, 1, back * E2:blocks * E2], m.ones[:],
                               k["taken"][:, 0:blocks - back].rearrange("p t e -> p (t e)"),
                               start=False, stop=(back == blocks - 1))
    ins.then_inc(k["ranked"], 1)


def rank_sums(nc, m, link, k, used):
    ranks = m.ps[:, 1, 0:NT * E2].rearrange("p (t e) -> p t e", t=NT)
    link(nc.vector.tensor_tensor(k["place"][:], ranks, used[:].unsqueeze(1).to_broadcast([P, NT, E2]), ALU.add))
    link(nc.vector.tensor_tensor(used[:], used[:], m.ps[:, 1, NT * E2:(NT + 1) * E2], ALU.add))


def pair_route_stage(nc, m, w, b, following, src, tokens, residual):
    bufs = ROUTE_BUFFERS + STAT_BUFFERS + RANK_BUFFERS + (
        ("cg", [P, NT, D], F32), ("nb", [P, NT, D], F32), ("dl", [P, NT], F32), ("de", [P, NT], F32)) + LOAD_BUFFERS
    sems = "step normed turned turned_out routed logits rexp picked ranked kept_x copied shifted" + LOAD_SEMS
    with Stage(nc, "proute", sems, bufs) as (block, k):
        @block.gpsimd
        def _(pool):
            for t in range(NT):
                ins = nc.gpsimd.tensor_tensor(k["nb"][:, t, :], m.n[:, t, :], m.ln1_b[:], ALU.add)
            ins.then_inc(k["shifted"], 1)

        @block.vector
        def _(dve):
            link = linker(dve, k["step"])
            nc.vector.memset(k["taken"][:, NT], 0.0)
            affine_norm(nc, link, m.y, m.ln1_g, k["nb"], lambda: dve.wait_ge(k["shifted"], 1), m.y, k,
                        lambda t, ins: ins.then_inc(k["normed"], 1))
            load_on_vector(nc, m, dve, link, k)
            nc.vector.tensor_copy(m.pair_ids[:], m.token_ids[:, bass.ds(b * NT, NT)])
            dve.wait_ge(k["routed"], 1)
            link(nc.vector.tensor_copy(k["lg"][:, :, 0:E2], psum_logits(m, E2)))
            top_steps(nc, link, k, k["lg"], E2)
            nc.vector.tensor_tensor(k["dl"][:], k["top"][:, :, 1], k["top"][:, :, 0], ALU.subtract)\
                .then_inc(k["logits"], 1)
            one_hot(nc, m, link, k, k["oh"][:, :, 0:E2], 0, E2)
            one_hot(nc, m, link, k, k["hot"][:], 1, E2)
            nc.vector.tensor_tensor(k["taken"][:, 0:NT], k["oh"][:, :, 0:E2], k["hot"][:], ALU.add)\
                .then_inc(k["picked"], 1)
            dve.wait_ge(k["rexp"], 1)
            link(nc.vector.tensor_scalar(k["dl"][:], k["de"][:], 1.0, None, ALU.add))
            link(nc.vector.reciprocal(k["wt"][:, :, 0], k["dl"][:]))
            link(nc.vector.tensor_tensor(k["wt"][:, :, 1], k["de"][:], k["wt"][:, :, 0], ALU.mult))
            nc.vector.tensor_copy(m.pair_weights[:, bass.ds(b * NT, NT), :], k["wt"][:])
            dve.wait_ge(k["ranked"], 1)
            rank_sums(nc, m, link, k, m.used2)
            link(nc.vector.tensor_tensor(k["place"][:], k["place"][:], m.first_slots[:], ALU.add))
            link(nc.vector.tensor_tensor(k["oh"][:, :, 0:E2], k["oh"][:, :, 0:E2], k["place"][:], ALU.mult))
            link(nc.vector.tensor_tensor(k["hot"][:], k["hot"][:], k["place"][:], ALU.mult))
            link(nc.vector.tensor_reduce(k["slots"][:, :, 0], k["oh"][:, :, 0:E2], AX_X, ALU.add))
            link(nc.vector.tensor_reduce(k["slots"][:, :, 1], k["hot"][:], AX_X, ALU.add))
            nc.vector.tensor_copy(m.pair_targets[:], k["slots"][:])
            nc.vector.tensor_copy(m.pair_slots[:, bass.ds(b * NT, NT), :], k["slots"][:])
            nc.vector.tensor_copy(m.pair_experts[:, bass.ds(b * NT, NT), :], k["idf"][:, :, 0:2])

        @block.tensor
        def _(pe):
            context_on_tensor(nc, m, pe, k)
            for t in range(NT):
                pe.wait_ge(k["normed"], t + 1)
                for c in range(DC):
                    ins = nc.tensor.transpose(m.ps[:, 2 + c, t * P:(t + 1) * P], m.y[:, t, c * P:(c + 1) * P],
                                              m.ident[:])
            ins.then_inc(k["turned"], 1)
            pe.wait_ge(k["turned_out"], 1)
            logits_on_pe(nc, m, k, m.nt, PAD, w.gate2, E2)
            pe.wait_ge(k["picked"], 1)
            ranks_on_pe(nc, m, k)

        @block.scalar
        def _(act):
            context_on_scalar(nc, m, act, k)
            act.wait_ge(k["turned"], 1)
            nc.scalar.activation(m.nt[:, :, PAD:PAD + S], m.ps[:, 2:2 + DC, :], ACT.Copy).then_inc(k["turned_out"], 1)
            act.wait_ge(k["logits"], 1)
            nc.scalar.activation(k["de"][:], k["dl"][:], ACT.Exp).then_inc(k["rexp"], 1)

        @block.sync
        def _(sp):
            sp.dma_start(batch_rows(residual, b), m.x[:]).then_inc(k["kept_x"], 16)
            load_on_sync(nc, m, sp, k, following, src, (k["kept_x"], 16))
            sp.wait_ge(k["normed"], NT)
            sp.dma_start(batch_rows(tokens, b), m.y[:]).then_inc(k["copied"], 16)
            sp.wait_ge(k["copied"], 16)

def batch_rows(dram, b):
    return dram[bass.ds(b * S, S), :].rearrange("(t p) d -> p t d", p=P)


def single_route_stage(nc, m, w, b, following, src, tokens, residual, table):
    bufs = ROUTE_BUFFERS + STAT_BUFFERS + RANK_BUFFERS + RESTORE_BUFFERS + (
        ("kept", [P, NT, E2], F32), ("room", [P, NT], F32), ("idf3", [P, NT], F32), ("back", [P, NT], F32),
        ("ids", [P, NT], I32), ("targets", [P, NT, 1], I32))
    sems = NORM_SEMS + "routed logits rexp picked ranked slotted scattered kept_x copied" + RESTORE_SEMS
    with Stage(nc, "sroute", sems, bufs, True) as (block, k):
        @block.gpsimd
        def _(pool):
            restore_on_gpsimd(nc, pool, k, src[2])
            pool.wait_ge(k["slotted"], 1)
            scatter_ids(nc, pool, k, table, k["targets"], k["ids"], 1)

        @block.tensor
        def _(pe):
            norm_on_tensor(nc, m, pe, k)
            pe.wait_ge(k["nt_out"], DC)
            logits_on_pe(nc, m, k, m.nt, PAD, w.gate3, E2)
            context_on_tensor(nc, m, pe, k)
            pe.wait_ge(k["picked"], 1)
            ranks_on_pe(nc, m, k)

        @block.scalar
        def _(act):
            norm_on_scalar(nc, m, act, k)
            act.wait_ge(k["logits"], 1)
            nc.scalar.activation(k["pr"][:, :, 0:E2], k["lg"][:, :, 0:E2], ACT.Exp).then_inc(k["rexp"], 1)
            context_on_scalar(nc, m, act, k)

        @block.sync
        def _(sp):
            sp.dma_start(batch_rows(residual, b), m.x[:]).then_inc(k["kept_x"], 16)
            sp.wait_ge(k["normed"], NT)
            sp.dma_start(batch_rows(tokens, b), m.n[:]).then_inc(k["copied"], 16)
            restore_on_sync(nc, m, sp, k, following, src, (k["kept_x"], 16))
            sp.wait_ge(k["copied"], 16)

        @block.vector
        def _(dve):
            link = linker(dve, k["step"])
            nc.vector.memset(k["taken"][:, NT], 0.0)
            resume_on_vector(nc, m, link, k, following)
            link(nc.vector.tensor_copy(k["ids"][:], m.token_ids[:, bass.ds(b * NT, NT)]))
            link(nc.vector.tensor_copy(k["idf3"][:], k["ids"][:]))
            norm_on_vector(nc, m, link, k)
            dve.wait_ge(k["routed"], 1)
            link(nc.vector.tensor_copy(k["lg"][:, :, 0:E2], psum_logits(m, E2)))
            softmax_steps(nc, dve, link, k, E2)
            top_steps(nc, link, k, k["pr"], E2)
            one_hot(nc, m, link, k, k["oh"][:, :, 0:E2], 0, E2)
            nc.vector.tensor_copy(k["taken"][:, 0:NT], k["oh"][:, :, 0:E2]).then_inc(k["picked"], 1)
            mix_on_vector(nc, m, dve, link, k)
            dve.wait_ge(k["ranked"], 1)
            rank_sums(nc, m, link, k, m.used3)
            link(nc.vector.tensor_scalar(k["kept"][:], k["place"][:], float(CAPACITY), None, ALU.is_le))
            link(nc.vector.tensor_tensor(k["kept"][:], k["kept"][:], k["oh"][:, :, 0:E2], ALU.mult))
            link(nc.vector.tensor_reduce(k["room"][:], k["kept"][:], AX_X, ALU.add))
            link(nc.vector.tensor_tensor(m.one_weight[:, bass.ds(b * NT, NT)], k["top"][:, :, 0], k["room"][:],
                                         ALU.mult))
            link(nc.vector.tensor_tensor(k["place"][:], k["place"][:], m.first_slots3[:], ALU.add))
            link(nc.vector.tensor_tensor(k["place"][:], k["place"][:], k["kept"][:], ALU.mult))
            link(nc.vector.tensor_reduce(k["back"][:], k["place"][:], AX_X, ALU.add))
            link(nc.vector.tensor_scalar(m.one_slot[:, bass.ds(b * NT, NT)], k["back"][:], float(DROPPED), None,
                                         ALU.add))
            link(nc.vector.tensor_scalar(k["room"][:], k["room"][:], -1.0, 1.0, ALU.mult, ALU.add))
            link(nc.vector.tensor_tensor(k["idf3"][:], k["idf3"][:], k["room"][:], ALU.mult))
            link(nc.vector.tensor_tensor(k["back"][:], k["back"][:], k["idf3"][:], ALU.add))
            nc.vector.tensor_scalar(k["targets"][:, :, 0], k["back"][:], float(DROPPED), None, ALU.add)\
                .then_inc(k["slotted"], 1)
            close_on_vector(nc, m, link, k)


def schedule_stage(nc, m, before):
    choices = B * NT * 2
    bufs = (("count_i", [P, E2], I32), ("blocks", [P, E2], F32), ("grid", [P, E2, E2], F32), ("ends", [P, E2], F32),
            ("move", [P, E2], F32), ("past", [P, BLOCKS, E2], F32), ("start", [P, BLOCKS, E2], F32),
            ("first", [P, BLOCKS], F32), ("expert", [P, BLOCKS], F32), ("slot", [P, BLOCKS], F32),
            ("number", [P, BLOCKS, E2], F32), ("upto", [P, E2, E2], F32), ("column", [P, choices, E2], F32),
            ("hot", [P, choices, E2], F32), ("moved", [P, choices], F32))
    shift = BLOCK.bit_length() - 1
    with Stage(nc, "sched", "step zeroed made scattered", bufs, True) as (block, k):
        @block.gpsimd
        def _(pool):
            nc.gpsimd.memset(k["upto"][:], 1.0).then_inc(k["zeroed"], 1)
            nc.gpsimd.iota(k["number"][:], pattern=[[1, BLOCKS], [0, E2]], base=0, channel_multiplier=0,
                           allow_small_or_imprecise_dtypes=True).then_inc(k["made"], 1)
            nc.gpsimd.iota(k["column"][:], pattern=[[0, choices], [1, E2]], base=0, channel_multiplier=0,
                           allow_small_or_imprecise_dtypes=True).then_inc(k["made"], 1)
            pool.wait_ge(k["zeroed"], 1)
            nc.gpsimd.affine_select(out=k["upto"][:], in_=k["upto"][:], compare_op=ALU.is_ge, fill=0.0, base=0,
                                    pattern=[[1, E2], [-1, E2]], channel_multiplier=0).then_inc(k["made"], 1)
            scatter_ids(nc, pool, k, *before)

        @block.vector
        def _(dve):
            link = linker(dve, k["step"])

            def over(ap, n):
                return ap.unsqueeze(1).to_broadcast([P, n, E2])

            link(nc.vector.tensor_scalar(k["count_i"][:], m.used2[:], float(BLOCK - 1), None, ALU.add))
            link(nc.vector.tensor_scalar(k["count_i"][:], k["count_i"][:], shift, None, ALU.arith_shift_right))
            link(nc.vector.tensor_copy(k["blocks"][:], k["count_i"][:]))
            dve.wait_ge(k["made"], 3)
            link(nc.vector.tensor_tensor(k["grid"][:], k["upto"][:], over(k["blocks"][:], E2), ALU.mult))
            link(nc.vector.tensor_reduce(k["ends"][:], k["grid"][:], AX_X, ALU.add))
            link(nc.vector.tensor_tensor(k["past"][:], k["number"][:], over(k["ends"][:], BLOCKS), ALU.is_ge))
            link(nc.vector.tensor_reduce(k["expert"][:], k["past"][:], AX_X, ALU.add))
            link(nc.vector.tensor_tensor(k["start"][:], k["past"][:], over(k["blocks"][:], BLOCKS), ALU.mult))
            link(nc.vector.tensor_reduce(k["first"][:], k["start"][:], AX_X, ALU.add))
            link(nc.vector.tensor_tensor(k["first"][:], k["number"][:, :, 0], k["first"][:], ALU.subtract))
            link(nc.vector.tensor_scalar(k["first"][:], k["first"][:], float(BLOCK), None, ALU.mult))
            link(nc.vector.tensor_scalar(k["slot"][:], k["expert"][:], float(TOKENS), None, ALU.mult))
            nc.vector.tensor_tensor(m.block_slot[:], k["slot"][0:1], k["first"][0:1], ALU.add)
            nc.vector.tensor_scalar(m.block_expert[:], k["expert"][0:1], float(E2 - 1), None, ALU.min)
            link(nc.vector.tensor_tensor(k["move"][:], k["ends"][:], k["blocks"][:], ALU.subtract))
            link(nc.vector.tensor_scalar(k["move"][:], k["move"][:], float(BLOCK), None, ALU.mult))
            link(nc.vector.scalar_tensor_tensor(k["move"][:], k["column"][:, 0, :], -float(TOKENS), k["move"][:],
                                                ALU.mult, ALU.add))
            experts = m.pair_experts[:].rearrange("p t c -> p (t c)")
            link(nc.vector.tensor_tensor(k["hot"][:], k["column"][:],
                                         experts.unsqueeze(2).to_broadcast([P, choices, E2]), ALU.is_equal))
            link(nc.vector.tensor_tensor(k["hot"][:], k["hot"][:], over(k["move"][:], choices), ALU.mult))
            link(nc.vector.tensor_reduce(k["moved"][:], k["hot"][:], AX_X, ALU.add))
            nc.vector.tensor_tensor(m.pair_rows[:].rearrange("p t c -> p (t c)"), k["moved"][:],
                                    m.pair_slots[:].rearrange("p t c -> p (t c)"), ALU.add)


def sparse_mixture_stage(nc, m, tag, tiles, blocks, place, tokens, table, results, w1, b1, w2, b2):
    rows = sum(tiles)
    nt = len(tiles)
    starts = [sum(tiles[:t]) for t in range(nt)]
    RX, RO = 3, 4
    bufs = (("w1", [P, 2, DC, FF], F32), ("w2", [P, 2, FC, D], F32), ("b1", [P, 2, FC], F32), ("b2", [P, 2, D], F32),
            ("ids", [P, RX, nt], I32), ("xg", [P, RX, nt, D], F32), ("xt", [P, 2, DC, rows], F32),
            ("hidden", [P, 2, FC, rows], F32), ("res", [P, RO, D], F32))
    sems = ("ids0 ids1 ids2 xg0 xg1 xg2 wa0 wa1 wb0 wb1 st0 st1 st2 st3 turned xt_out chunk relu outs added")
    units = [(i, t) for i in range(blocks) for t in range(nt)]
    with Stage(nc, tag, sems, bufs, True) as (block, k):
        ids_in, x_in = [k[f"ids{r}"] for r in range(RX)], [k[f"xg{r}"] for r in range(RX)]
        first_in, second_in = (k["wa0"], k["wa1"]), (k["wb0"], k["wb1"])
        stored = [k[f"st{r}"] for r in range(RO)]

        @block.gpsimd
        def _(pool):
            def load_ids(i):
                slot = place(pool, i, "slot")
                for t in range(nt):
                    pool.dma_start(k["ids"][0:tiles[t], i % RX, t:t + 1],
                                   table[bass.ds(slot + starts[t], tiles[t]), :]).then_inc(ids_in[i % RX], 16)

            load_ids(0)
            for i in range(blocks):
                pool.wait_ge(ids_in[i % RX], 16 * nt * (i // RX + 1))
                if i >= RX:
                    pool.wait_ge(k["turned"], i - RX + 1)
                for t in range(nt):
                    nc.gpsimd.indirect_dma_start(
                        out=k["xg"][0:tiles[t], i % RX, t, :], out_offset=None, in_=tokens[:, :],
                        in_offset=bass.IndirectOffsetOnAxis(ap=k["ids"][0:tiles[t], i % RX, t:t + 1], axis=0))\
                        .then_inc(x_in[i % RX], 16)
                if i + 1 < blocks:
                    if i + 1 >= RX:
                        pool.wait_ge(x_in[(i + 1) % RX], 16 * nt * ((i + 1) // RX))
                    load_ids(i + 1)

        @block.sync
        def _(sp):
            def load_weights(i):
                e = place(sp, i, "expert")
                one = bass.ds(e, 1)
                if i >= 2:
                    sp.wait_ge(k["chunk"], FC * (i - 1))
                    sp.wait_ge(k["relu"], FC * (i - 1))
                sp.dma_start(k["w1"][:, i % 2], w1[one].rearrange("o (c p) f -> p (o c) f", p=P))\
                    .then_inc(first_in[i % 2], 16)
                sp.dma_start(k["b1"][:, i % 2], b1[one].rearrange("o p f -> p (o f)")).then_inc(first_in[i % 2], 16)
                if i >= 2:
                    sp.wait_ge(k["outs"], nt * (i - 1))
                    sp.wait_ge(k["added"], nt * (i - 1))
                sp.dma_start(k["w2"][:, i % 2], w2[one].rearrange("o (c p) d -> p (o c) d", p=P))\
                    .then_inc(second_in[i % 2], 16)
                sp.dma_start(k["b2"][:, i % 2], b2[one, :].partition_broadcast(P)).then_inc(second_in[i % 2], 16)

            def store(i):
                for t in range(nt):
                    u = i * nt + t
                    sp.wait_ge(k["added"], u + 1)
                    row = i * rows + starts[t]
                    sp.dma_start(results[row:row + tiles[t], :], k["res"][0:tiles[t], u % RO, :])\
                        .then_inc(stored[u % RO], 16)

            sp.wait_ge(x_in[0], 16 * nt)
            load_weights(0)
            for i in range(blocks):
                if i + 1 < blocks:
                    load_weights(i + 1)
                store(i)
            for r in range(RO):
                sp.wait_ge(stored[r], 16 * len(range(r, len(units), RO)))

        @block.tensor
        def _(pe):
            def turn(i):
                pe.wait_ge(x_in[i % RX], 16 * nt * (i // RX + 1))
                if i >= 1:
                    pe.wait_ge(k["xt_out"], i)
                for t in range(nt):
                    for c in range(DC):
                        ins = nc.tensor.transpose(m.ps[:, c, starts[t]:starts[t] + tiles[t]],
                                                  k["xg"][0:tiles[t], i % RX, t, c * P:(c + 1) * P],
                                                  m.ident[0:tiles[t], 0:tiles[t]])
                ins.then_inc(k["turned"], 1)

            turn(0)
            for i in range(blocks):
                pe.wait_ge(k["xt_out"], i + 1)
                pe.wait_ge(first_in[i % 2], 32 * (i // 2 + 1))
                for f in range(FC):
                    n = i * FC + f
                    if n >= 4:
                        pe.wait_ge(k["relu"], n - 3)
                    for c in range(DC):
                        ins = nc.tensor.matmul(m.ps[:, 2 + n % 4, 0:rows], k["w1"][:, i % 2, c, f * P:(f + 1) * P],
                                               k["xt"][:, i % 2, c, :], start=(c == 0), stop=(c == DC - 1))
                    ins.then_inc(k["chunk"], 1)
                if i + 1 < blocks:
                    turn(i + 1)
                pe.wait_ge(k["relu"], FC * (i + 1))
                pe.wait_ge(second_in[i % 2], 32 * (i // 2 + 1))
                for t in range(nt):
                    u = i * nt + t
                    if u >= 2:
                        pe.wait_ge(k["added"], u - 1)
                    for f in range(FC):
                        ins = nc.tensor.matmul(m.ps[0:tiles[t], 6 + u % 2, 0:D],
                                               k["hidden"][:, i % 2, f, starts[t]:starts[t] + tiles[t]],
                                               k["w2"][:, i % 2, f, :], start=(f == 0), stop=(f == FC - 1))
                    ins.then_inc(k["outs"], 1)

        @block.scalar
        def _(act):
            for i in range(blocks):
                if i >= 2:
                    act.wait_ge(k["outs"], nt * (i - 1))
                for f in range(FC):
                    n = i * FC + f
                    act.wait_ge(k["chunk"], n + 1)
                    nc.scalar.activation(k["hidden"][:, i % 2, f, :], m.ps[:, 2 + n % 4, 0:rows], ACT.Relu,
                                         bias=k["b1"][:, i % 2, f:f + 1]).then_inc(k["relu"], 1)

        @block.vector
        def _(dve):
            def take_tokens(i):
                dve.wait_ge(k["turned"], i + 1)
                if i >= 2:
                    dve.wait_ge(k["chunk"], FC * (i - 1))
                nc.vector.tensor_copy(k["xt"][:, i % 2], m.ps[:, 0:DC, 0:rows]).then_inc(k["xt_out"], 1)

            take_tokens(0)
            for i in range(blocks):
                if i + 1 < blocks:
                    take_tokens(i + 1)
                for t in range(nt):
                    u = i * nt + t
                    dve.wait_ge(k["outs"], u + 1)
                    if u >= RO:
                        dve.wait_ge(stored[u % RO], 16 * (u // RO))
                    nc.vector.tensor_tensor(k["res"][0:tiles[t], u % RO, :], m.ps[0:tiles[t], 6 + u % 2, 0:D],
                                            k["b2"][0:tiles[t], i % 2, :], ALU.add).then_inc(k["added"], 1)


RESTORE_BUFFERS = (("slot", [P, NT, 2], I32), ("got", [P, NT, 2, D], F32), ("mixw", [P, NT, 2], F32),
                   ("len_i", [P, 1], I32), ("mix", [P, NT, D], F32), ("cg", [P, NT, D], F32))
RESTORE_SEMS = " xin cin small cturned resume got0 got1 got2 got3"


def restore_on_sync(nc, m, sp, k, b, src, after):
    residual, tokens, results, ctx_in, lens, pt = src
    sp.dma_start(m.c[:], context_rows(ctx_in, b)).then_inc(k["cin"], 16)
    sp.dma_start(m.y[:], batch_rows(tokens, b)).then_inc(k["xin"], 16)
    load_scalars(sp, k, m, b, ((m.pt, pt), (k["len_i"], lens)))
    if after is not None:
        sp.wait_ge(*after)
    sp.dma_start(m.x[:], batch_rows(residual, b)).then_inc(k["xin"], 16)


def restore_on_gpsimd(nc, pool, k, results):
    pool.wait_ge(k["resume"], 1)
    for t in range(NT):
        for c in range(2):
            nc.gpsimd.indirect_dma_start(
                out=k["got"][:, t, c, :], out_offset=None, in_=results[:, :],
                in_offset=bass.IndirectOffsetOnAxis(ap=k["slot"][:, t, c:c + 1], axis=0))\
                .then_inc(k[f"got{t}"], 16)


def resume_on_vector(nc, m, link, k, b):
    nc.vector.tensor_copy(k["slot"][:], m.pair_rows[:, bass.ds(b * NT, NT), :]).then_inc(k["resume"], 1)
    link(nc.vector.tensor_copy(k["mixw"][:], m.pair_weights[:, bass.ds(b * NT, NT), :]))


def mix_on_vector(nc, m, dve, link, k):
    dve.wait_ge(k["small"], 32)
    nc.vector.tensor_copy(m.len_f[:], k["len_i"][:])
    dve.wait_ge(k["xin"], 32)
    link(nc.vector.tensor_tensor(m.y[:], m.y[:], m.ln2_b[:].unsqueeze(1).to_broadcast([P, NT, D]), ALU.add))
    link(nc.vector.tensor_tensor(m.y[:], m.x[:], m.y[:], ALU.add))
    for t in range(NT):
        dve.wait_ge(k[f"got{t}"], 32)
        link(nc.vector.tensor_scalar(k["mix"][:, t, :], k["got"][:, t, 0, :], k["mixw"][:, t, 0:1], None, ALU.mult))
        link(nc.vector.scalar_tensor_tensor(k["mix"][:, t, :], k["got"][:, t, 1, :], k["mixw"][:, t, 1:2],
                                            k["mix"][:, t, :], ALU.mult, ALU.add))


def close_on_vector(nc, m, link, k):
    affine_norm(nc, link, k["mix"], m.ln2_g, m.y, lambda: None, m.x, k, lambda t, ins: None)


def restore_stage(nc, m, b, src):
    with Stage(nc, "back", "step" + RESTORE_SEMS, STAT_BUFFERS + RESTORE_BUFFERS, True) as (block, k):
        @block.sync
        def _(sp):
            restore_on_sync(nc, m, sp, k, b, src, None)

        @block.scalar
        def _(act):
            context_on_scalar(nc, m, act, k)

        @block.tensor
        def _(pe):
            context_on_tensor(nc, m, pe, k)

        @block.gpsimd
        def _(pool):
            restore_on_gpsimd(nc, pool, k, src[2])

        @block.vector
        def _(dve):
            link = linker(dve, k["step"])
            resume_on_vector(nc, m, link, k, b)
            mix_on_vector(nc, m, dve, link, k)
            close_on_vector(nc, m, link, k)


def finish_stage(nc, m, residual, results, out):
    bufs = (("x", [P, B, NT, D], F32), ("got", [P, B, NT, D], F32))
    sems = "x0 x1 x2 x3 got0 got1 got2 got3 summed stored"
    with Stage(nc, "finish", sems, bufs, True) as (block, k):
        rows = out.rearrange("b s d -> (b s) d")

        @block.sync
        def _(sp):
            for b in range(B):
                sp.dma_start(k["x"][:, b], batch_rows(residual, b)).then_inc(k[f"x{b}"], 16)
            for b in range(B):
                sp.wait_ge(k["summed"], b + 1)
                sp.dma_start(batch_rows(rows, b), k["x"][:, b]).then_inc(k["stored"], 16)
            sp.wait_ge(k["stored"], 16 * B)

        @block.gpsimd
        def _(pool):
            for b in range(B):
                for t in range(NT):
                    n = b * NT + t
                    nc.gpsimd.indirect_dma_start(
                        out=k["got"][:, b, t, :], out_offset=None, in_=results[:, :],
                        in_offset=bass.IndirectOffsetOnAxis(ap=m.one_slot[:, n:n + 1], axis=0))\
                        .then_inc(k[f"got{b}"], 16)

        @block.vector
        def _(dve):
            for b in range(B):
                dve.wait_ge(k[f"got{b}"], 16 * NT)
                dve.wait_ge(k[f"x{b}"], 16)
                for t in range(NT):
                    n = b * NT + t
                    ins = nc.vector.scalar_tensor_tensor(k["x"][:, b, t, :], k["got"][:, b, t, :],
                                                         m.one_weight[:, n:n + 1], k["x"][:, b, t, :],
                                                         ALU.mult, ALU.add)
                ins.then_inc(k["summed"], 1)


def constant_stage(nc, m, loads, batch, table2, table3, results3):
    wide = SLOTS2 // P
    bufs = (("blank_i", [P, wide], I32), ("blank_row", [1, D], F32)) + LOAD_BUFFERS
    with Stage(nc, "const", "loaded zeroed unit blank filled step" + LOAD_SEMS, bufs) as (block, k):
        @block.scalar
        def _(act):
            load_on_sync(nc, m, act, k, 0, batch, None)
            context_on_scalar(nc, m, act, k)

        @block.tensor
        def _(pe):
            pe.wait_ge(k["unit"], 1)
            context_on_tensor(nc, m, pe, k)

        @block.sync
        def _(sp):
            for dst, src in loads:
                sp.dma_start(dst, src).then_inc(k["loaded"], 16)
            sp.wait_ge(k["blank"], 1)
            sp.dma_start(table2[0:SLOTS2, :].rearrange("(p n) o -> p (n o)", p=P), k["blank_i"][:])\
                .then_inc(k["filled"], 16)
            sp.dma_start(table3[0:DROPPED, :].rearrange("(p n) o -> p (n o)", p=P), k["blank_i"][:, 0:DROPPED // P])\
                .then_inc(k["filled"], 16)
            sp.dma_start(results3[DROPPED:DROPPED + 1, :], k["blank_row"][:]).then_inc(k["filled"], 16)
            sp.wait_ge(k["filled"], 48)
            sp.wait_ge(k["loaded"], 16 * len(loads))

        @block.vector
        def _(dve):
            nc.vector.memset(m.ones[:], 1.0)
            nc.vector.memset(m.nt[:, :, 0:PAD], 0.0)
            nc.vector.memset(m.used2[:], 0.0)
            nc.vector.memset(m.used3[:], 0.0)
            nc.vector.memset(m.quarter_rows[:], 0.25)
            nc.vector.memset(m.one_rows[:], 1.0)
            nc.vector.memset(m.zero_rows[:], 0.0)
            nc.vector.memset(k["blank_row"][:], 0.0)
            nc.vector.memset(k["blank_i"][:], 0).then_inc(k["blank"], 1)
            load_on_vector(nc, m, dve, linker(dve, k["step"]), k)

        @block.gpsimd
        def _(pool):
            g = nc.gpsimd
            for tile, value in ((m.ident, 0.0), (m.later, 0.0), (m.earlier, 1.0)):
                ins = g.memset(tile[:], value)
            ins.then_inc(k["zeroed"], 1)
            pool.wait_ge(k["zeroed"], 1)
            g.affine_select(out=m.ident[:], in_=m.ident[:], compare_op=ALU.not_equal, fill=1.0, base=0,
                            pattern=[[-1, P]], channel_multiplier=1).then_inc(k["unit"], 1)
            g.affine_select(out=m.later[:], in_=m.later[:], compare_op=ALU.is_ge, fill=LOWEST, base=0,
                            pattern=[[-1, P]], channel_multiplier=1)
            g.affine_select(out=m.earlier[:], in_=m.earlier[:], compare_op=ALU.is_ge, fill=0.0, base=0,
                            pattern=[[1, P]], channel_multiplier=-1)
            g.iota(m.index[:], pattern=[[1, S]], base=0, channel_multiplier=0, allow_small_or_imprecise_dtypes=True)
            g.iota(m.token_ids[:], pattern=[[P, B * NT]], base=0, channel_multiplier=1)
            g.iota(m.first_slots[:], pattern=[[0, NT], [TOKENS, E2]], base=-1, channel_multiplier=0,
                   allow_small_or_imprecise_dtypes=True)
            g.iota(m.first_slots3[:], pattern=[[0, NT], [CAPACITY, E2]], base=-1 - DROPPED, channel_multiplier=0,
                   allow_small_or_imprecise_dtypes=True)
            g.iota(m.pair_targets[:], pattern=[[P, 2 * NT]], base=SLOTS2, channel_multiplier=1)
            g.memset(m.pair_ids[:], 0)
            g.iota(m.columns[:], pattern=[[0, NT], [1, E1]], base=0, channel_multiplier=0,
                   allow_small_or_imprecise_dtypes=True)


class Memory:

    def __init__(self, buffer):
        self.x = buffer("x", [P, NT, D], F32)
        self.n = buffer("n", [P, NT, D], F32)
        self.c = buffer("c", [P, NT, D], F32)
        self.y = buffer("y", [P, NT, D], F32)
        self.nt = buffer("nt", [P, DC, PAD + S], F32)
        self.ct = buffer("ct", [P, DC, S], F32)
        self.comb = buffer("comb", [P, NT, E1], F32)
        self.index = buffer("index", [P, S], F32)
        self.columns = buffer("columns", [P, NT, E1], F32)
        self.ident = buffer("ident", [P, P], F32)
        self.later = buffer("later", [P, P], F32)
        self.earlier = buffer("earlier", [P, P], BF16)
        self.ones = buffer("ones", [P, P], BF16)
        self.used2 = buffer("used2", [P, E2], F32)
        self.used3 = buffer("used3", [P, E2], F32)
        self.token_ids = buffer("token_ids", [P, B * NT], I32)
        self.first_slots = buffer("first_slots", [P, NT, E2], F32)
        self.first_slots3 = buffer("first_slots3", [P, NT, E2], F32)
        self.pair_weights = buffer("pair_weights", [P, B * NT, 2], F32)
        self.pair_slots = buffer("pair_slots", [P, B * NT, 2], F32)
        self.pair_experts = buffer("pair_experts", [P, B * NT, 2], F32)
        self.pair_rows = buffer("pair_rows", [P, B * NT, 2], I32)
        self.pair_ids = buffer("pair_ids", [P, NT], I32)
        self.pair_targets = buffer("pair_targets", [P, NT, 2], I32)
        self.one_weight = buffer("one_weight", [P, B * NT], F32)
        self.one_slot = buffer("one_slot", [P, B * NT], I32)
        self.block_expert = buffer("block_expert", [1, BLOCKS], I32)
        self.block_slot = buffer("block_slot", [1, BLOCKS], I32)
        self.quarter_rows = buffer("quarter_rows", [3, S], BF16)
        self.one_rows = buffer("one_rows", [2, S], BF16)
        self.zero_rows = buffer("zero_rows", [3, S], BF16)
        self.delta_rows = buffer("delta_rows", [3, S], BF16)
        self.tau = buffer("tau", [P, 1], F32)
        self.pt = buffer("pt", [P, 1], F32)
        self.len_f = buffer("len_f", [P, 1], F32)
        self.ln0_g = buffer("ln0_g", [P, D], F32)
        self.ln0_b = buffer("ln0_b", [P, D], F32)
        self.ln1_g = buffer("ln1_g", [P, D], F32)
        self.ln1_b = buffer("ln1_b", [P, D], F32)
        self.ln2_g = buffer("ln2_g", [P, D], F32)
        self.ln2_b = buffer("ln2_b", [P, D], F32)


class Weights:
    pass


class AttentionWeights:

    def __init__(self, buffer, tag, out=True):
        self.q, self.k, self.v = (buffer(f"{tag}_w{n}", [P, DC, D], F32) for n in "qkv")
        self.out = out
        if out:
            self.o, self.bo = buffer(f"{tag}_wo", [P, DC, D], F32), buffer(f"{tag}_bo", [P, D], F32)
        self.bq, self.bk = (buffer(f"{tag}_b{n}", [P, DC], F32) for n in "qk")
        self.bv = buffer(f"{tag}_bv", [P, D], F32)

    def loads(self, a, tag):
        chunks = "(c p) n -> p c n"
        out = []
        if self.out:
            out = [(self.o[:], a[f"{tag}_wo"].rearrange(chunks, p=P)), (self.bo[:], row(a[f"{tag}_bo"]))]
        return out + [
            (self.q[:], a[f"{tag}_wq"].rearrange(chunks, p=P)), (self.k[:], a[f"{tag}_wk"].rearrange(chunks, p=P)),
            (self.v[:], a[f"{tag}_wv"].rearrange(chunks, p=P)), (self.bq[:], a[f"{tag}_bq"]),
            (self.bk[:], a[f"{tag}_bk"]), (self.bv[:], row(a[f"{tag}_bv"]))]


def row(vector):
    return vector.rearrange("(a n) -> a n", a=1).partition_broadcast(P)


def residual_stack(nc, a):
    with ExitStack() as ctx:
        def buffer(name, shape, dt):
            return ctx.enter_context(nc.sbuf_tensor(name, shape, dt))

        m = Memory(buffer)
        m.ps = ctx.enter_context(nc.psum_tensor("banks", [P, 8, S], F32))
        w = Weights()
        attn = {tag: AttentionWeights(buffer, tag, tag != "a2") for tag in ("a0", "a1", "a2")}
        loc = {}
        for tag in ("l2", "l3"):
            loc[tag] = Weights()
            loc[tag].a = buffer(f"{tag}_wa", [P, DC, D], F32)
            loc[tag].c = buffer(f"{tag}_wc", [P, 2 * DC, D], F32)
        w.router, w.rbias = buffer("w_router", [P, DC, E1], F32), buffer("w_rbias", [P, E1], F32)
        w.conv = buffer("w_conv", [P, KS1, DC, I1], F32)
        w.sup, w.sdown = buffer("w_sup", [P, DC, I1], F32), buffer("w_sdown", [P, D], F32)
        w.gate2, w.gate3 = buffer("w_gate2", [P, DC, E2], F32), buffer("w_gate3", [P, DC, E2], F32)

        chunks = "(c p) n -> p c n"
        loads = []
        for tag in attn:
            loads += attn[tag].loads(a, tag)
        for tag in loc:
            loads += [(loc[tag].a[:], a[f"{tag}_wa"].rearrange(chunks, p=P)),
                      (loc[tag].c[:], a[f"{tag}_wc"].rearrange(chunks, p=P))]
        loads += [(w.router[:], a["router_w"].rearrange(chunks, p=P)), (w.rbias[:], row(a["router_bias"])),
                  (w.conv[:], a["conv_w"]),
                  (w.sup[:], a["shared_up"].rearrange(chunks, p=P)), (w.sdown[:], a["shared_down"]),
                  (w.gate2[:], a["gate2"].rearrange(chunks, p=P)), (w.gate3[:], a["gate3"].rearrange(chunks, p=P))]
        loads += [(m.ln0_g[:], row(a["ln0_g"])), (m.ln0_b[:], row(a["ln0_b"])), (m.ln1_g[:], row(a["ln1_g"])),
                  (m.ln1_b[:], row(a["ln1_b"])), (m.ln2_g[:], row(a["ln2_g"])), (m.ln2_b[:], row(a["ln2_b"]))]
        residual = nc.dram_tensor("residual", [TOKENS, D], F32)
        tokens2 = nc.dram_tensor("tokens2", [TOKENS, D], F32)
        tokens3 = nc.dram_tensor("tokens3", [TOKENS, D], F32)
        table2 = nc.dram_tensor("table2", [SLOTS2 + 2 * S, 1], I32)
        table3 = nc.dram_tensor("table3", [DROPPED + TOKENS, 1], I32)
        results2 = nc.dram_tensor("results2", [BLOCKS * BLOCK, D], F32)
        results3 = nc.dram_tensor("results3", [DROPPED + 1, D], F32)
        residual, tokens2, tokens3, table2, table3, results2, results3 = (
            t.ap() for t in (residual, tokens2, tokens3, table2, table3, results2, results3))
        x_rows = a["x"].rearrange("b s d -> (b s) d")
        batch = (x_rows, a["ctx"], a["tau"], a["delta"], a["lens"], a["pt"])
        constant_stage(nc, m, loads, batch, table2, table3, results3)

        def pair_place(engine, i, what):
            if what == "expert":
                return engine.value_load(m.block_expert[0:1, i:i + 1], min_val=0, max_val=E2 - 1)
            return engine.value_load(m.block_slot[0:1, i:i + 1], min_val=0, max_val=SLOTS2 - BLOCK)

        def single_place(engine, i, what):
            return i if what == "expert" else i * CAPACITY

        pairs_before = (table2, m.pair_targets, m.pair_ids, 2)
        with nc.Fori(0, B) as b:
            attention_stage(nc, m, "at0", attn["a0"], m.ct, False, before=pairs_before)
            attention_stage(nc, m, "at1", attn["a1"], m.ct, False, doubled=(m.ln0_g, m.ln0_b[:]))
            conv_mixture_stage(nc, m, w, a["gate_w"], a["up_w"], a["down_w"])
            location_stage(nc, m, "loc2", loc["l2"])
            attention_stage(nc, m, "at2", attn["a2"], m.nt, True)
            pair_route_stage(nc, m, w, b, (b + 1) % B, batch, tokens2, residual)
        schedule_stage(nc, m, pairs_before)
        sparse_mixture_stage(nc, m, "mx2", (P, P), BLOCKS, pair_place, tokens2, table2, results2,
                             a["m2_w1"], a["m2_b1"], a["m2_w2"], a["m2_b2"])
        back = (residual, tokens2, results2, a["ctx"], a["lens"], a["pt"])
        restore_stage(nc, m, 0, back)
        with nc.Fori(0, B) as b:
            location_stage(nc, m, "loc3", loc["l3"])
            single_route_stage(nc, m, w, b, (b + 1) % B, back, tokens3, residual, table3)
        sparse_mixture_stage(nc, m, "mx3", (P, P, CAPACITY - 2 * P), E2, single_place, tokens3, table3, results3,
                             a["m3_w1"], a["m3_b1"], a["m3_w2"], a["m3_b2"])
        finish_stage(nc, m, residual, results3, a["out"])


def lay_out(inputs):
    import numpy as np
    i = {n: np.asarray(v) for n, v in inputs.items()}
    c, dim, head = np.meshgrid(np.arange(DC), np.arange(DK), np.arange(H // DC), indexing="ij")
    cols = ((c * H // DC + head) * DK + dim).reshape(-1)
    f32 = np.float32

    def columns(b):
        return b[cols].reshape(DC, P).T

    a = {"x": i["x"], "ctx": i["ctx_1024"], "tau": i["condB_tau"], "delta": i["fside_BxS2_0"], "pt": i["condB_pt"],
         "lens": i["_lenS2"]}
    for tag, pre in (("a0", "L0_xcond_"), ("a1", "L1_xcond_")):
        a[f"{tag}_wq"], a[f"{tag}_wk"] = i[pre + "Wq"].T[:, cols], i[pre + "Wk"].T[:, cols]
        a[f"{tag}_wv"], a[f"{tag}_bv"] = i[pre + "Wv"].T, i[pre + "bv"]
        a[f"{tag}_bq"], a[f"{tag}_bk"] = columns(i[pre + "bq"]), columns(i[pre + "bk"])
        a[f"{tag}_wo"], a[f"{tag}_bo"] = i[pre + "Wo"].T, i[pre + "bo"]
    heads = {n: i[f"L2_ffn_W{n}"].transpose(1, 0, 2).reshape(D, D) for n in "qkv"}
    a["a2_wq"], a["a2_wk"], a["a2_wv"] = heads["q"][:, cols], heads["k"][:, cols], heads["v"]
    a["a2_bq"] = a["a2_bk"] = np.zeros((P, DC), f32)
    a["a2_bv"] = np.zeros(D, f32)
    for tag, pre in (("l2", "L2_xcond_"), ("l3", "L3_xcond_")):
        a[f"{tag}_wa"], a[f"{tag}_wc"] = i[pre + "W_a"].T, i[pre + "W_c"].T
    a["router_w"], a["router_bias"] = i["L1_ffn_router_w"], i["L1_ffn_router_bias"]
    a["conv_w"] = i["L1_ffn_conv_w"].transpose(2, 1, 0).reshape(KS1, DC, P, I1).transpose(2, 0, 1, 3)
    a["shared_up"], a["shared_down"] = i["L1_ffn_shared_up_w"], i["L1_ffn_shared_down_w"]
    a["gate_w"], a["up_w"], a["down_w"] = (i[f"L1_ffn_expert_{n}_w"] for n in ("gate", "up", "down"))
    a["gate2"], a["gate3"] = i["L2_ffn_gate_W"], i["L3_ffn_gate_w"].T
    for tag, pre, names in (("m2", "L2_ffn_", ("W1", "b1", "W2", "b2")), ("m3", "L3_ffn_", ("w1", "b1", "w2", "b2"))):
        w1, b1, w2, b2 = (i[pre + n] for n in names)
        a[f"{tag}_w1"], a[f"{tag}_w2"], a[f"{tag}_b2"] = w1, w2, b2
        a[f"{tag}_b1"] = b1.reshape(E2, FC, P).transpose(0, 2, 1)
    a["ln0_g"], a["ln0_b"] = i["L0_ffn_ln_g"], i["L0_ffn_ln_b"]
    for n in ("ln1_g", "ln1_b", "ln2_g", "ln2_b"):
        a[n] = i["L2_ffn_" + n]
    return {n: np.ascontiguousarray(v) for n, v in a.items()}


def kernel(**inputs):
    import numpy as np
    import concourse.bacc as bacc
    from concourse.bass_utils import run_bass_kernel_spmd

    nc = bacc.Bacc("TRN2", target_bir_lowering=False, num_devices=1)
    arrays = {f"in_{n}": v for n, v in lay_out(inputs).items()}
    aps = {n[3:]: nc.dram_tensor(n, v.shape, mybir.dt.from_np(v.dtype), kind="ExternalInput").ap()
           for n, v in arrays.items()}
    aps["out"] = nc.dram_tensor("out_0", (B, S, D), F32, kind="ExternalOutput").ap()
    residual_stack(nc, aps)
    r = run_bass_kernel_spmd(nc, [arrays], core_ids=[0])
    return np.asarray(r.results[0]["out_0"])
```
